# Optimizing a Trainium2 kernel written in Bass

```python
import numpy as np
import jax
import jax.numpy as jnp

def _softmax(x, axis=-1):
    return jax.nn.softmax(x, axis=axis)

def _gelu(x):
    return jax.nn.gelu(x, approximate=True)

def _silu(x):
    return jax.nn.silu(x)

def _sigmoid(x):
    return jax.nn.sigmoid(x)

def _layernorm(x, axis=-1, eps=1e-05):
    m = jnp.mean(x, axis=axis, keepdims=True)
    v = jnp.var(x, axis=axis, keepdims=True)
    return (x - m) / jnp.sqrt(v + eps)

def _scatter_add(tgt, idx, src, axis=0):
    return tgt.at[idx].add(src)

def _segment_sum(src, seg, n):
    return jax.ops.segment_sum(src, seg, n)
kernel_name = 'mk_decoder_postln_d4_seqx_r4_a69724'

def setup_inputs(seed: int=0):
    np.random.seed(seed)
    _w = jnp.asarray

    def _rec_inputs():
        import jax
        import jax.numpy as jnp
        _rk = jax.random.key(seed)
        x = 7.22e-05 + 1 * jax.random.normal(jax.random.fold_in(_rk, 1), (8, 112, 256), jnp.float32)
        _lenS = 112 - jax.random.randint(jax.random.fold_in(_rk, 7), (8,), 0, max(1, 112 // 4) + 1, jnp.int32)
        _lenS2 = 375 - jax.random.randint(jax.random.fold_in(_rk, 8), (8,), 0, max(1, 375 // 4) + 1, jnp.int32)
        _ctx_768P = jax.random.normal(jax.random.fold_in(_rk, 11), (8, 16, 192), jnp.float32)
        _ctx_768c = jax.random.dirichlet(jax.random.fold_in(_rk, 511), 0.3 * jnp.ones((16,), jnp.float32), (8, 375))
        _ctx_768t = jnp.einsum('bsk,bkd->bsd', _ctx_768c, _ctx_768P)
        _ctx_768t = _ctx_768t * jax.lax.rsqrt(jnp.mean(jnp.square(_ctx_768t)) + 1e-12) * 0.953939
        ctx_768 = -0.000191848 + 0.999787 * (_ctx_768t + 0.3 * jax.random.normal(jax.random.fold_in(_rk, 611), (8, 375, 192), jnp.float32))
        _validS = jnp.arange(112)[None, :] < _lenS[:, None]
        _validS2 = jnp.arange(375)[None, :] < _lenS2[:, None]
        _causal = jnp.tril(jnp.ones((112, 112), dtype=bool))
        mask_BxS2_bf1 = jnp.ones((8, 375), dtype=bool)
        return (x, ctx_768, mask_BxS2_bf1)
    x, ctx_768, mask_BxS2_bf1 = _rec_inputs()

    def _L0_attn_setup():
        import jax, jax.numpy as jnp
        import numpy as np
        import math
        H = 8
        D = 32
        DEPTH = 1
        LAMBDA_INIT = 0.8 - 0.6 * math.exp(-0.3 * DEPTH)
        EPS = 1e-08
        key = jax.random.key(seed)
        ks = jax.random.split(key, 9)
        B, T, IN_DIM, OUT_DIM = (2, 512, 256, 256)
        E = 2 * H * D
        inp = {'x': jax.random.normal(ks[0], (B, T, IN_DIM), dtype=jnp.float32), 'Wq': jax.random.normal(ks[1], (IN_DIM, E), dtype=jnp.float32) * IN_DIM ** (-0.5), 'Wkv': jax.random.normal(ks[2], (IN_DIM, 2 * E), dtype=jnp.float32) * IN_DIM ** (-0.5), 'Wout': jax.random.normal(ks[3], (E, OUT_DIM), dtype=jnp.float32) * E ** (-0.5), 'lambda_q1': 0.1 * jax.random.normal(ks[4], (D,), dtype=jnp.float32), 'lambda_k1': 0.1 * jax.random.normal(ks[5], (D,), dtype=jnp.float32), 'lambda_q2': 0.1 * jax.random.normal(ks[6], (D,), dtype=jnp.float32), 'lambda_k2': 0.1 * jax.random.normal(ks[7], (D,), dtype=jnp.float32), 'gamma': jnp.ones((2 * D,), dtype=jnp.float32)}
        return inp
    _L0_attn_all = _L0_attn_setup()
    _L0_attn_in = {k: v for k, v in _L0_attn_all.items() if k in ('Wq', 'Wkv', 'Wout', 'lambda_q1', 'lambda_k1', 'lambda_q2', 'lambda_k2', 'gamma')}
    del _L0_attn_all

    def _L0_xattn_setup():
        import jax, jax.numpy as jnp
        import numpy as np
        NUM_HEADS = 16
        CLAMP = 10000.0
        key = jax.random.key(seed)
        ks = jax.random.split(key, 8)
        B, Nq, Nkv, Cq, Ckv = (4, 512, 512, 256, 192)
        s_q = 1.0 / np.sqrt(Cq)
        s_kv = 1.0 / np.sqrt(Ckv)
        return {'query': jax.random.normal(ks[0], (B, Nq, Cq), jnp.float32), 'key_value': jax.random.normal(ks[1], (B, Nkv, Ckv), jnp.float32), 'Wq': jax.random.normal(ks[2], (Cq, Cq), jnp.float32) * s_q, 'bq': jnp.zeros((Cq,), jnp.float32), 'Wk': jax.random.normal(ks[3], (Ckv, Cq), jnp.float32) * s_kv, 'bk': jnp.zeros((Cq,), jnp.float32), 'Wv': jax.random.normal(ks[4], (Ckv, Cq), jnp.float32) * s_kv, 'bv': jnp.zeros((Cq,), jnp.float32), 'Wo': jax.random.normal(ks[5], (Cq, Cq), jnp.float32) * s_q, 'bo': jnp.zeros((Cq,), jnp.float32)}
    _L0_xattn_all = _L0_xattn_setup()
    _L0_xattn_in = {k: v for k, v in _L0_xattn_all.items() if k in ('Wq', 'bq', 'Wk', 'bk', 'Wv', 'bv', 'Wo', 'bo')}
    del _L0_xattn_all

    def _L0_ffn_setup():
        import jax, jax.numpy as jnp
        import numpy as np
        TOP_K = 2
        key = jax.random.key(seed)
        ks = jax.random.split(key, 6)
        B, S, D, U, E = (4, 256, 256, 1024, 8)
        return {'x': jax.random.normal(ks[0], (B, S, D), dtype=jnp.float32), 'w_up': jax.random.normal(ks[1], (E, U, D), dtype=jnp.float32), 'w_down': jax.random.normal(ks[2], (E, D, U), dtype=jnp.float32), 'b_up': jax.random.normal(ks[3], (E, U), dtype=jnp.float32), 'b_down': jax.random.normal(ks[4], (E, D), dtype=jnp.float32), 'w_router': jax.random.normal(ks[5], (E, D), dtype=jnp.float32)}
    _L0_ffn_all = _L0_ffn_setup()
    _L0_ffn_in = {k: v for k, v in _L0_ffn_all.items() if k in ('w_up', 'w_down', 'b_up', 'b_down', 'w_router')}
    del _L0_ffn_all

    def _L1_attn_setup():
        import jax, jax.numpy as jnp
        import numpy as np
        H = 16
        GRID = 16
        TOK_PER_FRAME = GRID * GRID

        def _rope(x, pos, dim):
            half = dim // 2
            omega = jnp.arange(half, dtype=x.dtype) / (dim / 2.0)
            inv = 1.0 / 10000.0 ** omega
            freq = pos.astype(x.dtype)[:, None] * inv
            sin = jnp.concatenate([jnp.sin(freq), jnp.sin(freq)], axis=-1)
            cos = jnp.concatenate([jnp.cos(freq), jnp.cos(freq)], axis=-1)
            y = x.reshape(*x.shape[:-1], half, 2)
            y1, y2 = (y[..., 0], y[..., 1])
            rot = jnp.stack((-y2, y1), axis=-1).reshape(x.shape)
            return x * cos + rot * sin

        def _apply_3d_rope(qk, f_ids, h_ids, w_ids, d_dim):
            s = 0
            parts = []
            for pos in (f_ids, h_ids, w_ids):
                parts.append(_rope(qk[..., s:s + d_dim], pos, d_dim))
                s += d_dim
            if s < qk.shape[-1]:
                parts.append(qk[..., s:])
            return jnp.concatenate(parts, axis=-1)
        key = jax.random.key(seed)
        ks = jax.random.split(key, 5)
        D = 256
        B, N = (4, 512)
        sc = 0.02
        return {'hidden_states': jax.random.normal(ks[0], (B, N, D), jnp.float32), 'Wq': jax.random.normal(ks[1], (D, D), jnp.float32) * sc, 'bq': jnp.zeros((D,), jnp.float32), 'Wk': jax.random.normal(ks[2], (D, D), jnp.float32) * sc, 'bk': jnp.zeros((D,), jnp.float32), 'Wv': jax.random.normal(ks[3], (D, D), jnp.float32) * sc, 'bv': jnp.zeros((D,), jnp.float32), 'Wo': jax.random.normal(ks[4], (D, D), jnp.float32) * sc, 'bo': jnp.zeros((D,), jnp.float32)}
    _L1_attn_all = _L1_attn_setup()
    _L1_attn_in = {k: v for k, v in _L1_attn_all.items() if k in ('Wq', 'bq', 'Wk', 'bk', 'Wv', 'bv', 'Wo', 'bo')}
    del _L1_attn_all

    def _L1_xattn_setup():
        import jax, jax.numpy as jnp
        import numpy as np
        DIM = 256
        CTX_DIM = 192
        HEADS = 16
        key = jax.random.key(seed)
        ks = jax.random.split(key, 7)
        B, N, M = (4, 1024, 64)
        x = jax.random.normal(ks[0], (B, N, DIM), dtype=jnp.float32)
        context = jax.random.normal(ks[1], (B, M, CTX_DIM), dtype=jnp.float32)
        context_mask = jnp.ones((B, M), dtype=bool)
        s_d = 1.0 / np.sqrt(DIM)
        s_c = 1.0 / np.sqrt(CTX_DIM)
        Wq = jax.random.normal(ks[2], (DIM, DIM), dtype=jnp.float32) * s_d
        Wk = jax.random.normal(ks[3], (CTX_DIM, DIM), dtype=jnp.float32) * s_c
        Wv = jax.random.normal(ks[4], (CTX_DIM, DIM), dtype=jnp.float32) * s_c
        Wo = jax.random.normal(ks[5], (DIM, DIM), dtype=jnp.float32) * s_d
        return {'x': x, 'context': context, 'context_mask': context_mask, 'Wq': Wq, 'Wk': Wk, 'Wv': Wv, 'Wo': Wo}
    _L1_xattn_all = _L1_xattn_setup()
    _L1_xattn_in = {k: v for k, v in _L1_xattn_all.items() if k in ('Wq', 'Wk', 'Wv', 'Wo')}
    del _L1_xattn_all

    def _L1_ffn_setup():
        import jax, jax.numpy as jnp
        import numpy as np
        B, S, D, E, K = (4, 512, 256, 8, 2)
        H = 4 * D
        key = jax.random.key(seed)
        ks = jax.random.split(key, 4)
        sc = lambda n: 1.0 / np.sqrt(n)
        return {'x': jax.random.normal(ks[0], (B, S, D), jnp.float32), 'gate_w': jax.random.normal(ks[1], (D, E), jnp.float32) * sc(D), 'gate_b': jnp.zeros((E,), jnp.float32), 'w1': jax.random.normal(ks[2], (E, D, H), jnp.float32) * sc(D), 'b1': jnp.zeros((E, H), jnp.float32), 'w2': jax.random.normal(ks[3], (E, H, D), jnp.float32) * sc(H), 'b2': jnp.zeros((E, D), jnp.float32)}
    _L1_ffn_all = _L1_ffn_setup()
    _L1_ffn_in = {k: v for k, v in _L1_ffn_all.items() if k in ('gate_w', 'gate_b', 'w1', 'b1', 'w2', 'b2')}
    del _L1_ffn_all

    def _L2_attn_setup():
        import jax, jax.numpy as jnp
        import numpy as np
        B, S, DIM, H = (2, 512, 256, 16)
        D = DIM // H

        def _xavier(key, shape):
            a = float(np.sqrt(6.0 / (shape[0] + shape[1])))
            return jax.random.uniform(key, shape, minval=-a, maxval=a, dtype=jnp.float32)

        def _split_heads(t):
            b, s, _ = t.shape
            return t.reshape(b, s, H, D).transpose(0, 2, 1, 3).reshape(b * H, s, D)
        key = jax.random.key(seed)
        ks = jax.random.split(key, 8)
        x = jax.random.normal(ks[0], (B, S, DIM), dtype=jnp.float32)
        Wq = _xavier(ks[1], (DIM, DIM))
        Wk = _xavier(ks[2], (DIM, DIM))
        Wv = _xavier(ks[3], (DIM, DIM))
        Wo = _xavier(ks[4], (DIM, DIM))
        bq = jax.random.normal(ks[5], (DIM,), dtype=jnp.float32) * 0.02
        bk = jax.random.normal(ks[6], (DIM,), dtype=jnp.float32) * 0.02
        bv = jax.random.normal(ks[7], (DIM,), dtype=jnp.float32) * 0.02
        bo = jnp.zeros((DIM,), dtype=jnp.float32)
        return {'x': x, 'Wq': Wq, 'bq': bq, 'Wk': Wk, 'bk': bk, 'Wv': Wv, 'bv': bv, 'Wo': Wo, 'bo': bo}
    _L2_attn_all = _L2_attn_setup()
    _L2_attn_in = {k: v for k, v in _L2_attn_all.items() if k in ('Wq', 'bq', 'Wk', 'bk', 'Wv', 'bv', 'Wo', 'bo')}
    del _L2_attn_all

    def _L2_xattn_setup():
        import jax, jax.numpy as jnp
        import numpy as np
        QUERY_DIM, KV_DIM, EMBED_DIM, NUM_HEADS = (256, 192, 256, 16)
        HEAD_DIM = EMBED_DIM // NUM_HEADS
        SCALE = HEAD_DIM ** (-0.5)
        LN_EPS = 1e-05

        def _l2norm(x, eps=1e-12):
            n = jnp.sqrt(jnp.sum(x * x, axis=-1, keepdims=True))
            return x / jnp.maximum(n, eps)
        key = jax.random.key(seed)
        ks = jax.random.split(key, 12)
        B, Nq, Nk = (2, 512, 512)
        s = lambda d: 1.0 / np.sqrt(d)
        return {'query': jax.random.normal(ks[0], (B, Nq, QUERY_DIM), jnp.float32), 'key': jax.random.normal(ks[1], (B, Nk, KV_DIM), jnp.float32), 'value': jax.random.normal(ks[2], (B, Nk, KV_DIM), jnp.float32), 'Wq': jax.random.normal(ks[3], (QUERY_DIM, EMBED_DIM), jnp.float32) * s(QUERY_DIM), 'bq': jnp.zeros((EMBED_DIM,), jnp.float32), 'Wk': jax.random.normal(ks[4], (KV_DIM, EMBED_DIM), jnp.float32) * s(KV_DIM), 'bk': jnp.zeros((EMBED_DIM,), jnp.float32), 'Wv': jax.random.normal(ks[5], (KV_DIM, EMBED_DIM), jnp.float32) * s(KV_DIM), 'bv': jnp.zeros((EMBED_DIM,), jnp.float32), 'Wo': jax.random.normal(ks[6], (EMBED_DIM, EMBED_DIM), jnp.float32) * s(EMBED_DIM), 'bo': jnp.zeros((EMBED_DIM,), jnp.float32), 'ln_gamma': jnp.ones((EMBED_DIM,), jnp.float32), 'ln_beta': jnp.zeros((EMBED_DIM,), jnp.float32)}
    _L2_xattn_all = _L2_xattn_setup()
    _L2_xattn_in = {k: v for k, v in _L2_xattn_all.items() if k in ('Wq', 'bq', 'Wk', 'bk', 'Wv', 'bv', 'Wo', 'bo', 'ln_gamma', 'ln_beta')}
    del _L2_xattn_all

    def _L2_ffn_setup():
        import jax, jax.numpy as jnp
        import numpy as np
        INT8_MAX = 127.0

        def _absmax_scale(x, axes):
            amax = jnp.max(jnp.abs(x), axis=axes, keepdims=True)
            return jnp.maximum(amax, 1e-12) / INT8_MAX
        key = jax.random.key(seed)
        k1, k2 = jax.random.split(key)
        lhs = jax.random.normal(k1, (4, 2048, 256), dtype=jnp.float32)
        rhs = jax.random.normal(k2, (256, 256), dtype=jnp.float32)
        return {'lhs': lhs, 'rhs': rhs}
    _L2_ffn_all = _L2_ffn_setup()
    _L2_ffn_in = {k: v for k, v in _L2_ffn_all.items() if k in ('rhs',)}
    del _L2_ffn_all

    def _L3_attn_setup():
        import jax, jax.numpy as jnp
        import numpy as np
        import math
        HIDDEN = 256
        HEADS = 16
        HEAD_DIM = HIDDEN // HEADS
        NUM_FEATURES = 64
        B, N = (4, 1024)

        def _feature_map(x, rf):
            proj = jnp.einsum('bhnd,fd->bhnf', x, rf) / jnp.sqrt(jnp.float32(NUM_FEATURES))
            norm = jnp.linalg.norm(x, axis=-1, keepdims=True)
            return jnp.exp(proj - norm)
        key = jax.random.key(seed)
        ks = jax.random.split(key, 5)
        x = jax.random.normal(ks[0], (B, N, HIDDEN), dtype=jnp.float32)
        w_qkv = jax.random.normal(ks[1], (3 * HIDDEN, HIDDEN), dtype=jnp.float32) / math.sqrt(HIDDEN)
        w_out = jax.random.normal(ks[2], (HIDDEN, HIDDEN), dtype=jnp.float32) / math.sqrt(HIDDEN)
        b_out = jnp.zeros((HIDDEN,), dtype=jnp.float32)
        random_features = jax.random.normal(ks[3], (NUM_FEATURES, HEAD_DIM), dtype=jnp.float32)
        return {'x': x, 'w_qkv': w_qkv, 'w_out': w_out, 'b_out': b_out, 'random_features': random_features}
    _L3_attn_all = _L3_attn_setup()
    _L3_attn_in = {k: v for k, v in _L3_attn_all.items() if k in ('w_qkv', 'w_out', 'b_out', 'random_features')}
    del _L3_attn_all

    def _L3_xattn_setup():
        import jax, jax.numpy as jnp
        import numpy as np
        IMAGE_DIM = 256
        TEXT_DIM = 192
        NUM_HEADS = 16
        HEAD_DIM = IMAGE_DIM // NUM_HEADS
        key = jax.random.key(seed)
        ks = jax.random.split(key, 14)
        B, N, M = (4, 1024, 128)
        s_img = 1.0 / np.sqrt(IMAGE_DIM)
        s_txt = 1.0 / np.sqrt(TEXT_DIM)
        s_ff = 1.0 / np.sqrt(2 * IMAGE_DIM)
        return {'x': jax.random.normal(ks[0], (B, N, IMAGE_DIM), jnp.float32), 'y': jax.random.normal(ks[1], (B, M, TEXT_DIM), jnp.float32), 'Wq': jax.random.normal(ks[2], (IMAGE_DIM, IMAGE_DIM), jnp.float32) * s_img, 'bq': jax.random.normal(ks[3], (IMAGE_DIM,), jnp.float32) * s_img, 'Wk': jax.random.normal(ks[4], (TEXT_DIM, IMAGE_DIM), jnp.float32) * s_txt, 'bk': jax.random.normal(ks[5], (IMAGE_DIM,), jnp.float32) * s_txt, 'Wv': jax.random.normal(ks[6], (TEXT_DIM, IMAGE_DIM), jnp.float32) * s_txt, 'bv': jax.random.normal(ks[7], (IMAGE_DIM,), jnp.float32) * s_txt, 'W1': jax.random.normal(ks[8], (IMAGE_DIM, 2 * IMAGE_DIM), jnp.float32) * s_img, 'b1': jax.random.normal(ks[9], (2 * IMAGE_DIM,), jnp.float32) * s_img, 'W2': jax.random.normal(ks[10], (2 * IMAGE_DIM, IMAGE_DIM), jnp.float32) * s_ff, 'b2': jax.random.normal(ks[11], (IMAGE_DIM,), jnp.float32) * s_ff}
    _L3_xattn_all = _L3_xattn_setup()
    _L3_xattn_in = {k: v for k, v in _L3_xattn_all.items() if k in ('Wq', 'bq', 'Wk', 'bk', 'Wv', 'bv', 'W1', 'b1', 'W2', 'b2')}
    del _L3_xattn_all

    def _L3_ffn_setup():
        import jax, jax.numpy as jnp
        import numpy as np
        D_IN, D_HID = (256, 1024)

        def _ternary(key, shape):
            return jax.random.randint(key, shape, -1, 2).astype(jnp.float32)

        def _tlin(x, w, s):
            return jnp.einsum('bsi,oi->bso', x, w) * s
        key = jax.random.key(seed)
        ks = jax.random.split(key, 12)
        inv = lambda fan: 1.0 / np.sqrt(fan).astype(np.float32)
        return {'x': jax.random.normal(ks[0], (4, 512, D_IN), dtype=jnp.float32), 'w1_w': _ternary(ks[1], (D_HID, D_IN)), 'w1_s': jax.random.uniform(ks[2], (D_HID,), dtype=jnp.float32) * inv(D_IN), 'w2_w': _ternary(ks[3], (D_HID, D_IN)), 'w2_s': jax.random.uniform(ks[4], (D_HID,), dtype=jnp.float32) * inv(D_IN), 'h1_w': _ternary(ks[5], (D_HID, D_HID)), 'h1_s': jax.random.uniform(ks[6], (D_HID,), dtype=jnp.float32) * inv(D_HID), 'h2_w': _ternary(ks[7], (D_HID, D_HID)), 'h2_s': jax.random.uniform(ks[8], (D_HID,), dtype=jnp.float32) * inv(D_HID), 'w3_w': _ternary(ks[9], (D_IN, D_HID)), 'w3_s': jax.random.uniform(ks[10], (D_IN,), dtype=jnp.float32) * inv(D_HID)}
    _L3_ffn_all = _L3_ffn_setup()
    _L3_ffn_in = {k: v for k, v in _L3_ffn_all.items() if k in ('w1_w', 'w1_s', 'w2_w', 'w2_s', 'h1_w', 'h1_s', 'h2_w', 'h2_s', 'w3_w', 'w3_s')}
    del _L3_ffn_all
    return {'x': x, 'ctx_768': ctx_768, 'mask_BxS2_bf1': mask_BxS2_bf1, 'L0_attn_Wq': _L0_attn_in['Wq'], 'L0_attn_Wkv': _L0_attn_in['Wkv'], 'L0_attn_Wout': _L0_attn_in['Wout'], 'L0_attn_lambda_q1': _L0_attn_in['lambda_q1'], 'L0_attn_lambda_k1': _L0_attn_in['lambda_k1'], 'L0_attn_lambda_q2': _L0_attn_in['lambda_q2'], 'L0_attn_lambda_k2': _L0_attn_in['lambda_k2'], 'L0_attn_gamma': _L0_attn_in['gamma'], 'L0_xattn_Wq': _L0_xattn_in['Wq'], 'L0_xattn_bq': _L0_xattn_in['bq'], 'L0_xattn_Wk': _L0_xattn_in['Wk'], 'L0_xattn_bk': _L0_xattn_in['bk'], 'L0_xattn_Wv': _L0_xattn_in['Wv'], 'L0_xattn_bv': _L0_xattn_in['bv'], 'L0_xattn_Wo': _L0_xattn_in['Wo'], 'L0_xattn_bo': _L0_xattn_in['bo'], 'L0_ffn_w_up': _L0_ffn_in['w_up'], 'L0_ffn_w_down': _L0_ffn_in['w_down'], 'L0_ffn_b_up': _L0_ffn_in['b_up'], 'L0_ffn_b_down': _L0_ffn_in['b_down'], 'L0_ffn_w_router': _L0_ffn_in['w_router'], 'L1_attn_Wq': _L1_attn_in['Wq'], 'L1_attn_bq': _L1_attn_in['bq'], 'L1_attn_Wk': _L1_attn_in['Wk'], 'L1_attn_bk': _L1_attn_in['bk'], 'L1_attn_Wv': _L1_attn_in['Wv'], 'L1_attn_bv': _L1_attn_in['bv'], 'L1_attn_Wo': _L1_attn_in['Wo'], 'L1_attn_bo': _L1_attn_in['bo'], 'L1_xattn_Wq': _L1_xattn_in['Wq'], 'L1_xattn_Wk': _L1_xattn_in['Wk'], 'L1_xattn_Wv': _L1_xattn_in['Wv'], 'L1_xattn_Wo': _L1_xattn_in['Wo'], 'L1_ffn_gate_w': _L1_ffn_in['gate_w'], 'L1_ffn_gate_b': _L1_ffn_in['gate_b'], 'L1_ffn_w1': _L1_ffn_in['w1'], 'L1_ffn_b1': _L1_ffn_in['b1'], 'L1_ffn_w2': _L1_ffn_in['w2'], 'L1_ffn_b2': _L1_ffn_in['b2'], 'L2_attn_Wq': _L2_attn_in['Wq'], 'L2_attn_bq': _L2_attn_in['bq'], 'L2_attn_Wk': _L2_attn_in['Wk'], 'L2_attn_bk': _L2_attn_in['bk'], 'L2_attn_Wv': _L2_attn_in['Wv'], 'L2_attn_bv': _L2_attn_in['bv'], 'L2_attn_Wo': _L2_attn_in['Wo'], 'L2_attn_bo': _L2_attn_in['bo'], 'L2_xattn_Wq': _L2_xattn_in['Wq'], 'L2_xattn_bq': _L2_xattn_in['bq'], 'L2_xattn_Wk': _L2_xattn_in['Wk'], 'L2_xattn_bk': _L2_xattn_in['bk'], 'L2_xattn_Wv': _L2_xattn_in['Wv'], 'L2_xattn_bv': _L2_xattn_in['bv'], 'L2_xattn_Wo': _L2_xattn_in['Wo'], 'L2_xattn_bo': _L2_xattn_in['bo'], 'L2_xattn_ln_gamma': _L2_xattn_in['ln_gamma'], 'L2_xattn_ln_beta': _L2_xattn_in['ln_beta'], 'L2_ffn_rhs': _L2_ffn_in['rhs'], 'L3_attn_w_qkv': _L3_attn_in['w_qkv'], 'L3_attn_w_out': _L3_attn_in['w_out'], 'L3_attn_b_out': _L3_attn_in['b_out'], 'L3_attn_random_features': _L3_attn_in['random_features'], 'L3_xattn_Wq': _L3_xattn_in['Wq'], 'L3_xattn_bq': _L3_xattn_in['bq'], 'L3_xattn_Wk': _L3_xattn_in['Wk'], 'L3_xattn_bk': _L3_xattn_in['bk'], 'L3_xattn_Wv': _L3_xattn_in['Wv'], 'L3_xattn_bv': _L3_xattn_in['bv'], 'L3_xattn_W1': _L3_xattn_in['W1'], 'L3_xattn_b1': _L3_xattn_in['b1'], 'L3_xattn_W2': _L3_xattn_in['W2'], 'L3_xattn_b2': _L3_xattn_in['b2'], 'L3_ffn_w1_w': _L3_ffn_in['w1_w'], 'L3_ffn_w1_s': _L3_ffn_in['w1_s'], 'L3_ffn_w2_w': _L3_ffn_in['w2_w'], 'L3_ffn_w2_s': _L3_ffn_in['w2_s'], 'L3_ffn_h1_w': _L3_ffn_in['h1_w'], 'L3_ffn_h1_s': _L3_ffn_in['h1_s'], 'L3_ffn_h2_w': _L3_ffn_in['h2_w'], 'L3_ffn_h2_s': _L3_ffn_in['h2_s'], 'L3_ffn_w3_w': _L3_ffn_in['w3_w'], 'L3_ffn_w3_s': _L3_ffn_in['w3_s']}

def reference(x, ctx_768, mask_BxS2_bf1, L0_attn_Wq, L0_attn_Wkv, L0_attn_Wout, L0_attn_lambda_q1, L0_attn_lambda_k1, L0_attn_lambda_q2, L0_attn_lambda_k2, L0_attn_gamma, L0_xattn_Wq, L0_xattn_bq, L0_xattn_Wk, L0_xattn_bk, L0_xattn_Wv, L0_xattn_bv, L0_xattn_Wo, L0_xattn_bo, L0_ffn_w_up, L0_ffn_w_down, L0_ffn_b_up, L0_ffn_b_down, L0_ffn_w_router, L1_attn_Wq, L1_attn_bq, L1_attn_Wk, L1_attn_bk, L1_attn_Wv, L1_attn_bv, L1_attn_Wo, L1_attn_bo, L1_xattn_Wq, L1_xattn_Wk, L1_xattn_Wv, L1_xattn_Wo, L1_ffn_gate_w, L1_ffn_gate_b, L1_ffn_w1, L1_ffn_b1, L1_ffn_w2, L1_ffn_b2, L2_attn_Wq, L2_attn_bq, L2_attn_Wk, L2_attn_bk, L2_attn_Wv, L2_attn_bv, L2_attn_Wo, L2_attn_bo, L2_xattn_Wq, L2_xattn_bq, L2_xattn_Wk, L2_xattn_bk, L2_xattn_Wv, L2_xattn_bv, L2_xattn_Wo, L2_xattn_bo, L2_xattn_ln_gamma, L2_xattn_ln_beta, L2_ffn_rhs, L3_attn_w_qkv, L3_attn_w_out, L3_attn_b_out, L3_attn_random_features, L3_xattn_Wq, L3_xattn_bq, L3_xattn_Wk, L3_xattn_bk, L3_xattn_Wv, L3_xattn_bv, L3_xattn_W1, L3_xattn_b1, L3_xattn_W2, L3_xattn_b2, L3_ffn_w1_w, L3_ffn_w1_s, L3_ffn_w2_w, L3_ffn_w2_s, L3_ffn_h1_w, L3_ffn_h1_s, L3_ffn_h2_w, L3_ffn_h2_s, L3_ffn_w3_w, L3_ffn_w3_s):
    import jax
    import jax.numpy as jnp

    def _L0_attn_ref(x, Wq, Wkv, Wout, lambda_q1, lambda_k1, lambda_q2, lambda_k2, gamma):
        import jax, jax.numpy as jnp
        import numpy as np
        import math
        H = 8
        D = 32
        DEPTH = 1
        LAMBDA_INIT = 0.8 - 0.6 * math.exp(-0.3 * DEPTH)
        EPS = 1e-08
        B, T, _ = x.shape
        scaling = D ** (-0.5)
        q = (x @ Wq).reshape(B, T, 2 * H, D).transpose(0, 2, 1, 3) * scaling
        kv = x @ Wkv
        k, v = jnp.split(kv, 2, axis=-1)
        k = k.reshape(B, T, 2 * H, D).transpose(0, 2, 1, 3)
        v = v.reshape(B, T, H, 2 * D).transpose(0, 2, 1, 3)
        dots = jnp.einsum('bhqd,bhkd->bhqk', q, k)
        attn_w = jax.nn.softmax(dots.astype(jnp.float32), axis=-1).astype(dots.dtype)
        lam1 = jnp.exp(jnp.sum(lambda_q1 * lambda_k1))
        lam2 = jnp.exp(jnp.sum(lambda_q2 * lambda_k2))
        lam = lam1 - lam2 + LAMBDA_INIT
        attn_w = attn_w.reshape(B, H, 2, T, T)
        attn_w = attn_w[:, :, 0] - lam * attn_w[:, :, 1]
        attn = jnp.einsum('bhqk,bhkd->bhqd', attn_w, v)
        rms = jnp.sqrt(jnp.mean(attn * attn, axis=-1, keepdims=True))
        attn = gamma * (attn / (rms + EPS))
        attn = attn * (1.0 - LAMBDA_INIT)
        attn = attn.transpose(0, 2, 1, 3).reshape(B, T, 2 * H * D)
        return attn @ Wout

    def _L0_xattn_ref(query, key_value, Wq, bq, Wk, bk, Wv, bv, Wo, bo):
        import jax, jax.numpy as jnp
        import numpy as np
        NUM_HEADS = 16
        CLAMP = 10000.0
        B, Nq, Cq = query.shape
        Nkv = key_value.shape[1]
        H = NUM_HEADS
        D = Cq // H
        scale = D ** (-0.5)
        q = (query @ Wq + bq).reshape(B, Nq, H, D).transpose(0, 2, 1, 3)
        k = (key_value @ Wk + bk).reshape(B, Nkv, H, D).transpose(0, 2, 1, 3)
        v = (key_value @ Wv + bv).reshape(B, Nkv, H, D).transpose(0, 2, 1, 3)
        attn = jnp.einsum('bhqd,bhkd->bhqk', q, k) * scale
        attn = jnp.clip(attn, -CLAMP, CLAMP)
        attn = jax.nn.softmax(attn, axis=-1)
        attn = jnp.where(jnp.any(jnp.isnan(attn)), jnp.asarray(1.0 / Nkv, attn.dtype), attn)
        x = jnp.einsum('bhqk,bhkd->bqhd', attn, v).reshape(B, Nq, Cq)
        return x @ Wo + bo

    def _L0_ffn_ref(x, w_up, w_down, b_up, b_down, w_router):
        import jax, jax.numpy as jnp
        import numpy as np
        TOP_K = 2
        logits = jnp.einsum('bsd,ed->bse', x, w_router)
        top_vals, top_idx = jax.lax.top_k(logits, TOP_K)
        router_weights = jax.nn.softmax(top_vals, axis=-1)
        up = jnp.einsum('eud,bsd->bseu', w_up, x) + b_up
        h = jax.nn.gelu(up, approximate=False)
        down = jnp.einsum('edu,bseu->bsed', w_down, h) + b_down
        sel = jnp.take_along_axis(down, top_idx[..., None], axis=2)
        return jnp.einsum('bskd,bsk->bsd', sel, router_weights)

    def _L1_attn_ref(hidden_states, Wq, bq, Wk, bk, Wv, bv, Wo, bo):
        import jax, jax.numpy as jnp
        import numpy as np
        H = 16
        GRID = 16
        TOK_PER_FRAME = GRID * GRID

        def _rope(x, pos, dim):
            half = dim // 2
            omega = jnp.arange(half, dtype=x.dtype) / (dim / 2.0)
            inv = 1.0 / 10000.0 ** omega
            freq = pos.astype(x.dtype)[:, None] * inv
            sin = jnp.concatenate([jnp.sin(freq), jnp.sin(freq)], axis=-1)
            cos = jnp.concatenate([jnp.cos(freq), jnp.cos(freq)], axis=-1)
            y = x.reshape(*x.shape[:-1], half, 2)
            y1, y2 = (y[..., 0], y[..., 1])
            rot = jnp.stack((-y2, y1), axis=-1).reshape(x.shape)
            return x * cos + rot * sin

        def _apply_3d_rope(qk, f_ids, h_ids, w_ids, d_dim):
            s = 0
            parts = []
            for pos in (f_ids, h_ids, w_ids):
                parts.append(_rope(qk[..., s:s + d_dim], pos, d_dim))
                s += d_dim
            if s < qk.shape[-1]:
                parts.append(qk[..., s:])
            return jnp.concatenate(parts, axis=-1)
        B, N, D = hidden_states.shape
        hd = D // H
        d_dim = 2 * (hd // 3 // 2)

        def heads(x):
            return x.reshape(B, N, H, hd).transpose(0, 2, 1, 3)
        q = heads(hidden_states @ Wq + bq)
        k = heads(hidden_states @ Wk + bk)
        v = heads(hidden_states @ Wv + bv)
        ids = jnp.arange(N)
        f_ids = ids // TOK_PER_FRAME
        rem = ids - TOK_PER_FRAME * f_ids
        h_ids = rem // GRID
        w_ids = rem - GRID * h_ids
        q = _apply_3d_rope(q, f_ids, h_ids, w_ids, d_dim)
        k = _apply_3d_rope(k, f_ids, h_ids, w_ids, d_dim)
        scale = hd ** (-0.5)
        attn = jnp.einsum('bhqd,bhkd->bhqk', q, k) * scale
        attn = jax.nn.softmax(attn.astype(jnp.float32), axis=-1).astype(q.dtype)
        ctx = jnp.einsum('bhqk,bhkd->bhqd', attn, v)
        ctx = ctx.transpose(0, 2, 1, 3).reshape(B, N, D)
        return ctx @ Wo + bo

    def _L1_xattn_ref(x, context, context_mask, Wq, Wk, Wv, Wo):
        import jax, jax.numpy as jnp
        import numpy as np
        DIM = 256
        CTX_DIM = 192
        HEADS = 16
        B, N, _ = x.shape
        M = context.shape[1]
        hd = DIM // HEADS
        scale = hd ** (-0.5)
        q = (x @ Wq).reshape(B, N, HEADS, hd).transpose(0, 2, 1, 3)
        k = (context @ Wk).reshape(B, M, HEADS, hd).transpose(0, 2, 1, 3)
        v = (context @ Wv).reshape(B, M, HEADS, hd).transpose(0, 2, 1, 3)
        scores = jnp.einsum('bhid,bhjd->bhij', q, k) * scale
        max_neg = -jnp.finfo(scores.dtype).max
        scores = jnp.where(context_mask[:, None, None, :], scores, max_neg)
        attn = jax.nn.softmax(scores, axis=-1)
        out = jnp.einsum('bhij,bhjd->bhid', attn, v)
        out = out.transpose(0, 2, 1, 3).reshape(B, N, DIM)
        return out @ Wo

    def _L1_ffn_ref(x, gate_w, gate_b, w1, b1, w2, b2):
        import jax, jax.numpy as jnp
        import numpy as np
        B, S, D, E, K = (4, 512, 256, 8, 2)
        H = 4 * D
        Bx, Sx, Dx = x.shape
        n_exp = w1.shape[0]
        logits = jnp.einsum('bsd,de->bse', x, gate_w) + gate_b
        scores = jax.nn.softmax(logits, axis=-1)
        topk_s, topk_i = jax.lax.top_k(scores, K)
        onehot = jax.nn.one_hot(topk_i, n_exp, dtype=scores.dtype)
        dispatch = jnp.einsum('bske,bsk->bse', onehot, topk_s)
        xf = x.reshape(-1, Dx)
        wf = dispatch.reshape(-1, n_exp)
        out = jnp.zeros_like(xf)
        for i in range(n_exp):
            wi = wf[:, i:i + 1]
            h = jax.nn.relu(xf * wi @ w1[i] + b1[i])
            y = h @ w2[i] + b2[i]
            out = jnp.where(wi > 0, y, out)
        return out.reshape(Bx, Sx, Dx)

    def _L2_attn_ref(x, Wq, bq, Wk, bk, Wv, bv, Wo, bo):
        import jax, jax.numpy as jnp
        import numpy as np
        B, S, DIM, H = (2, 512, 256, 16)
        D = DIM // H

        def _xavier(key, shape):
            a = float(np.sqrt(6.0 / (shape[0] + shape[1])))
            return jax.random.uniform(key, shape, minval=-a, maxval=a, dtype=jnp.float32)

        def _split_heads(t):
            b, s, _ = t.shape
            return t.reshape(b, s, H, D).transpose(0, 2, 1, 3).reshape(b * H, s, D)
        b, s, _ = x.shape
        q = _split_heads(x @ Wq.T + bq)
        k = _split_heads(x @ Wk.T + bk)
        v = _split_heads(x @ Wv.T + bv)
        q = jnp.exp(q)
        k = jnp.exp(k)
        kv = jnp.cumsum(k[:, :, :, None] * v[:, :, None, :], axis=1)
        k1 = jnp.cumsum(k, axis=1)
        num = jnp.einsum('zsD,zsDd->zsd', q, kv)
        den = jnp.sum(q * k1, axis=-1, keepdims=True)
        out = num / den
        out = out.reshape(b, H, s, D).transpose(0, 2, 1, 3).reshape(b, s, DIM)
        return out @ Wo.T + bo

    def _L2_xattn_ref(query, key, value, Wq, bq, Wk, bk, Wv, bv, Wo, bo, ln_gamma, ln_beta):
        import jax, jax.numpy as jnp
        import numpy as np
        QUERY_DIM, KV_DIM, EMBED_DIM, NUM_HEADS = (256, 192, 256, 16)
        HEAD_DIM = EMBED_DIM // NUM_HEADS
        SCALE = HEAD_DIM ** (-0.5)
        LN_EPS = 1e-05

        def _l2norm(x, eps=1e-12):
            n = jnp.sqrt(jnp.sum(x * x, axis=-1, keepdims=True))
            return x / jnp.maximum(n, eps)
        B, Nq, _ = query.shape
        Nk = key.shape[1]
        Qp = query @ Wq + bq
        K = _l2norm(key @ Wk + bk)
        V = value @ Wv + bv
        Q = _l2norm(Qp)
        Q = Q.reshape(B, Nq, NUM_HEADS, HEAD_DIM).transpose(0, 2, 1, 3)
        K = K.reshape(B, Nk, NUM_HEADS, HEAD_DIM).transpose(0, 2, 1, 3)
        V = V.reshape(B, Nk, NUM_HEADS, HEAD_DIM).transpose(0, 2, 1, 3)
        scores = jnp.einsum('bhqd,bhkd->bhqk', Q, K) * SCALE
        attn = jax.nn.softmax(scores, axis=-1)
        out = jnp.einsum('bhqk,bhkd->bhqd', attn, V)
        out = out.transpose(0, 2, 1, 3).reshape(B, Nq, EMBED_DIM)
        out = out @ Wo + bo
        x = out + Qp
        mu = jnp.mean(x, axis=-1, keepdims=True)
        var = jnp.mean((x - mu) ** 2, axis=-1, keepdims=True)
        return (x - mu) / jnp.sqrt(var + LN_EPS) * ln_gamma + ln_beta

    def _L2_ffn_ref(lhs, rhs):
        import jax, jax.numpy as jnp
        import numpy as np
        INT8_MAX = 127.0

        def _absmax_scale(x, axes):
            amax = jnp.max(jnp.abs(x), axis=axes, keepdims=True)
            return jnp.maximum(amax, 1e-12) / INT8_MAX
        lhs_scale = _absmax_scale(lhs, (2,))
        rhs_scale = _absmax_scale(rhs, (0,))
        q_lhs = jnp.clip(jnp.round(lhs / lhs_scale), -INT8_MAX, INT8_MAX).astype(jnp.int8)
        q_rhs = jnp.clip(jnp.round(rhs / rhs_scale), -INT8_MAX, INT8_MAX).astype(jnp.int8)
        acc = jax.lax.dot_general(q_lhs, q_rhs, (((2,), (0,)), ((), ())), preferred_element_type=jnp.int32)
        return acc.astype(jnp.float32) * lhs_scale * rhs_scale

    def _L3_attn_ref(x, w_qkv, w_out, b_out, random_features):
        import jax, jax.numpy as jnp
        import numpy as np
        import math
        HIDDEN = 256
        HEADS = 16
        HEAD_DIM = HIDDEN // HEADS
        NUM_FEATURES = 64
        B, N = (4, 1024)

        def _feature_map(x, rf):
            proj = jnp.einsum('bhnd,fd->bhnf', x, rf) / jnp.sqrt(jnp.float32(NUM_FEATURES))
            norm = jnp.linalg.norm(x, axis=-1, keepdims=True)
            return jnp.exp(proj - norm)
        b, n, _ = x.shape
        qkv = jnp.einsum('bnh,oh->bno', x, w_qkv)
        qkv = qkv.reshape(b, n, 3, HEADS, HEAD_DIM)
        qkv = jnp.transpose(qkv, (2, 0, 3, 1, 4))
        q, k, v = (qkv[0], qkv[1], qkv[2])
        q_prime = _feature_map(q, random_features)
        k_prime = _feature_map(k, random_features)
        kv = jnp.einsum('bhnf,bhnd->bhfd', k_prime, v)
        normalizer = jnp.einsum('bhnf,bhf->bhn', q_prime, k_prime.sum(axis=2))
        out = jnp.einsum('bhnf,bhfd->bhnd', q_prime, kv)
        out = out / (normalizer[..., None] + 1e-06)
        out = jnp.transpose(out, (0, 2, 1, 3)).reshape(b, n, HIDDEN)
        return jnp.einsum('bnh,oh->bno', out, w_out) + b_out

    def _L3_xattn_ref(x, y, Wq, bq, Wk, bk, Wv, bv, W1, b1, W2, b2):
        import jax, jax.numpy as jnp
        import numpy as np
        IMAGE_DIM = 256
        TEXT_DIM = 192
        NUM_HEADS = 16
        HEAD_DIM = IMAGE_DIM // NUM_HEADS
        B, N, _ = x.shape
        M = y.shape[1]
        q = (x @ Wq + bq).reshape(B, N, NUM_HEADS, HEAD_DIM)
        k = (y @ Wk + bk).reshape(B, M, NUM_HEADS, HEAD_DIM)
        v = (y @ Wv + bv).reshape(B, M, NUM_HEADS, HEAD_DIM)
        scale = 1.0 / np.sqrt(HEAD_DIM)
        scores = jnp.einsum('bnhd,bmhd->bhnm', q, k) * scale
        attn = jax.nn.softmax(scores, axis=-1)
        out = jnp.einsum('bhnm,bmhd->bnhd', attn, v).reshape(B, N, IMAGE_DIM)
        h = jax.nn.relu(out @ W1 + b1)
        return h @ W2 + b2

    def _L3_ffn_ref(x, w1_w, w1_s, w2_w, w2_s, h1_w, h1_s, h2_w, h2_s, w3_w, w3_s):
        import jax, jax.numpy as jnp
        import numpy as np
        D_IN, D_HID = (256, 1024)

        def _ternary(key, shape):
            return jax.random.randint(key, shape, -1, 2).astype(jnp.float32)

        def _tlin(x, w, s):
            return jnp.einsum('bsi,oi->bso', x, w) * s
        h = jax.nn.silu(_tlin(x, w1_w, w1_s)) * _tlin(x, w2_w, w2_s)
        h = jax.nn.gelu(_tlin(h, h1_w, h1_s), approximate=False)
        h = jax.nn.gelu(_tlin(h, h2_w, h2_s), approximate=False)
        return _tlin(h, w3_w, w3_s)
    x = _layernorm(x + _L0_attn_ref(x, L0_attn_Wq, L0_attn_Wkv, L0_attn_Wout, L0_attn_lambda_q1, L0_attn_lambda_k1, L0_attn_lambda_q2, L0_attn_lambda_k2, L0_attn_gamma), axis=-1)
    x = _layernorm(x + _L0_xattn_ref(x, ctx_768, L0_xattn_Wq, L0_xattn_bq, L0_xattn_Wk, L0_xattn_bk, L0_xattn_Wv, L0_xattn_bv, L0_xattn_Wo, L0_xattn_bo), axis=-1)
    x = _layernorm(x + _L0_ffn_ref(x, L0_ffn_w_up, L0_ffn_w_down, L0_ffn_b_up, L0_ffn_b_down, L0_ffn_w_router), axis=-1)
    x = _layernorm(x + _L1_attn_ref(x, L1_attn_Wq, L1_attn_bq, L1_attn_Wk, L1_attn_bk, L1_attn_Wv, L1_attn_bv, L1_attn_Wo, L1_attn_bo), axis=-1)
    x = _layernorm(x + _L1_xattn_ref(x, ctx_768, mask_BxS2_bf1, L1_xattn_Wq, L1_xattn_Wk, L1_xattn_Wv, L1_xattn_Wo), axis=-1)
    x = _layernorm(x + _L1_ffn_ref(x, L1_ffn_gate_w, L1_ffn_gate_b, L1_ffn_w1, L1_ffn_b1, L1_ffn_w2, L1_ffn_b2), axis=-1)
    x = _layernorm(x + _L2_attn_ref(x, L2_attn_Wq, L2_attn_bq, L2_attn_Wk, L2_attn_bk, L2_attn_Wv, L2_attn_bv, L2_attn_Wo, L2_attn_bo), axis=-1)
    x = _layernorm(x + _L2_xattn_ref(x, ctx_768, ctx_768, L2_xattn_Wq, L2_xattn_bq, L2_xattn_Wk, L2_xattn_bk, L2_xattn_Wv, L2_xattn_bv, L2_xattn_Wo, L2_xattn_bo, L2_xattn_ln_gamma, L2_xattn_ln_beta), axis=-1)
    x = _layernorm(x + _L2_ffn_ref(x, L2_ffn_rhs), axis=-1)
    x = _layernorm(x + _L3_attn_ref(x, L3_attn_w_qkv, L3_attn_w_out, L3_attn_b_out, L3_attn_random_features), axis=-1)
    x = _layernorm(x + _L3_xattn_ref(x, ctx_768, L3_xattn_Wq, L3_xattn_bq, L3_xattn_Wk, L3_xattn_bk, L3_xattn_Wv, L3_xattn_bv, L3_xattn_W1, L3_xattn_b1, L3_xattn_W2, L3_xattn_b2), axis=-1)
    x = _layernorm(x + _L3_ffn_ref(x, L3_ffn_w1_w, L3_ffn_w1_s, L3_ffn_w2_w, L3_ffn_w2_s, L3_ffn_h1_w, L3_ffn_h1_s, L3_ffn_h2_w, L3_ffn_h2_s, L3_ffn_w3_w, L3_ffn_w3_s), axis=-1)
    return x

_drawn_inputs = setup_inputs


def setup_inputs(seed=0):
    import zlib

    import numpy as np

    out = dict(_drawn_inputs(seed))
    spreads = {'L0_attn_gamma': (1.0, 0.2),
     'L0_xattn_bq': (0.0, 0.1),
     'L0_xattn_bk': (0.0, 2.0),
     'L0_xattn_bv': (0.0, 0.1),
     'L0_xattn_bo': (0.0, 0.1),
     'L1_attn_bq': (0.0, 0.8),
     'L1_attn_bk': (0.0, 0.8),
     'L1_attn_bv': (0.0, 0.1),
     'L1_attn_bo': (0.0, 0.1),
     'L1_ffn_gate_b': (0.0, 0.1),
     'L1_ffn_b1': (0.0, 0.1),
     'L1_ffn_b2': (0.0, 0.1),
     'L2_attn_bo': (0.0, 0.1),
     'L2_xattn_bq': (0.0, 0.1),
     'L2_xattn_bk': (0.0, 2.0),
     'L2_xattn_bv': (0.0, 0.1),
     'L2_xattn_bo': (0.0, 0.1),
     'L2_xattn_ln_gamma': (1.0, 0.2),
     'L2_xattn_ln_beta': (0.0, 0.1),
     'L3_attn_b_out': (0.0, 0.1)}
    factors = {'L0_ffn_b_down': 7.885,
     'L1_attn_Wq': 8.0,
     'L1_attn_Wk': 7.944,
     'L2_attn_bq': 26.081,
     'L2_attn_bk': 26.49,
     'L2_attn_bv': 3.216,
     'L2_xattn_Wk': 64.0,
     'L3_attn_random_features': 8.0,
     'L3_xattn_bq': 6.676,
     'L3_xattn_bk': 64.0,
     'L3_ffn_w1_w': 8.0,
     'L3_ffn_w1_s': 8.0,
     'L3_ffn_w2_w': 8.0,
     'L3_ffn_w2_s': 8.0,
     'L3_ffn_h1_w': 8.0,
     'L3_ffn_h1_s': 8.0,
     'L3_ffn_h2_w': 8.0,
     'L3_ffn_h2_s': 8.0,
     'L3_ffn_w3_w': 8.0,
     'L3_ffn_w3_s': 8.0}
    for name, (base, spread) in spreads.items():
        noise = np.random.default_rng([zlib.crc32(name.encode()), seed]).standard_normal(out[name].shape)
        drawn = base * np.exp(spread * noise) if base else spread * noise
        out[name] = jnp.asarray(drawn.astype(out[name].dtype))
    for name, factor in factors.items():
        out[name] = (out[name] * factor).astype(out[name].dtype)
    return out
```

```python
import math
from contextlib import ExitStack

import numpy as np
import concourse.bass as bass
from concourse import mybir

F32 = mybir.dt.float32
BF16 = mybir.dt.bfloat16
U32 = mybir.dt.uint32
U8 = mybir.dt.uint8
ALU = mybir.AluOpType
ACT = mybir.ActivationFunctionType
AX_X = mybir.AxisListType.X

B, T, DM = 8, 112, 256
S2, KC, KT = 375, 96, 125
HEADS, GROUPS = 16, 4
EXPERTS, HID, HALF = 8, 1024, 448
START = 64
LN_EPS = 1e-5
LAMBDA_INIT = 0.8 - 0.6 * math.exp(-0.3 * 1)
CLAMP = 10000.0
BIG = float(2.0 ** 126)
LOWEST = -3.0e38
MAGIC = float(1.5 * 2 ** 23)


class Attn:

    def __init__(self, name, ctx=False, chunks=2, heads_per_chunk=8, scale=0.25, kind="softmax",
                 clip=False, mask=False, qk_norm=False, diff=False, rope=False, feats=False, mlp=False):
        self.name, self.ctx, self.chunks, self.hpc = name, ctx, chunks, heads_per_chunk
        self.scale, self.kind, self.clip, self.mask, self.qk_norm = scale, kind, clip, mask, qk_norm
        self.diff, self.rope, self.feats, self.mlp = diff, rope, feats, mlp
        self.keys = S2 if ctx else T
        self.tiles = 3 if ctx else 1
        self.rows = KT if ctx else T
        self.kdim = KC if ctx else 128
        self.qc = 512 if diff else 256
        self.items = ["q"] + ([] if ctx else ["k"]) + (["qrow"] if qk_norm else [])
        self.items += [f"v{t}" for t in range(self.tiles)]
        if rope:
            self.items += ["rq", "rk"]
        if feats:
            self.items += [f"{what}{s}{m}" for s in "qk" for m in range(2) for what in ("n", "p")]
        dve_frees = kind != "softmax" or mask or qk_norm
        self.dve_frees = dve_frees
        self.per = {"proj": len(self.items), "head": HEADS if kind == "softmax" else 0,
                    "dhead": HEADS if dve_frees else 0, "group": GROUPS, "pt": GROUPS * self.tiles,
                    "batch": 1, "ln": 2 if qk_norm else 1, "row": 1, "kprep": 2 if ctx else 0,
                    "inv": GROUPS * (2 if diff or kind == "linear" else 1), "mstep": HEADS}
        cols = [("wq", 2 * self.qc), ("wk", 2 * self.qc), ("wv", 2 * self.qc), ("headmask", heads_per_chunk),
                ("bq", 4), ("bk", 4), ("bvT", 4), ("bo", DM)]
        cols += [("b1", 4)] if mlp else [("wo", 4 * DM)]
        if diff:
            cols += [("lam", 4 * 32), ("gamma", 64)]
        if qk_norm:
            cols += [("bqrow", DM), ("ln_g", DM), ("ln_b", DM)]
        if rope:
            cols += [("rot", 128), ("cos", T), ("sin", T)]
        if feats:
            cols += [("rf", 4 * 128), ("ones2", 4 * 128)]
        self.at, n = {}, 0
        for key, width in cols:
            self.at[key] = (n, width)
            n += width
        self.cols = n


class Ffn:

    def __init__(self, name, dn, up=0):
        self.name = name
        self.per = {"ln": 1, "row": 1, "dn": dn / B, "up": up / B}


SUBS = [
    Attn("L0_attn", chunks=4, heads_per_chunk=4, scale=32 ** -0.5, diff=True),
    Attn("L0_xattn", ctx=True, clip=True),
    Ffn("L0_ffn", dn=8 + 8 * EXPERTS, up=16 * EXPERTS),
    Attn("L1_attn", rope=True),
    Attn("L1_xattn", ctx=True, mask=True),
    Ffn("L1_ffn", dn=8 + 8 * EXPERTS, up=16 * EXPERTS),
    Attn("L2_attn", kind="causal"),
    Attn("L2_xattn", ctx=True, qk_norm=True),
    Ffn("L2_ffn", dn=8),
    Attn("L3_attn", kind="linear", chunks=8, heads_per_chunk=2, feats=True),
    Attn("L3_xattn", ctx=True, mlp=True),
    Ffn("L3_ffn", dn=8, up=2 * 16),
]
UNITS = ("proj", "head", "dhead", "group", "pt", "batch", "ln", "row", "kprep", "inv", "mstep", "dn", "up")
for _i, _s in enumerate(SUBS):
    _s.index = _i
    _s.base = {u: int(sum(a.per.get(u, 0) * B for a in SUBS[:_i])) for u in UNITS}
ATTNS = [s for s in SUBS if isinstance(s, Attn)]
for _i, _s in enumerate(ATTNS):
    _s.slot = _i % 2
    _s.order = _i
    _s.ctx_before = sum(a.ctx for a in ATTNS[:_i])
SLOT_COLS = [max(a.cols for a in ATTNS if a.slot == s) for s in range(2)]

RSLOTS, RCOLS = 4, 2048
RING_L0, RING_L1, RING_X, RING_GLU, RING_H1, RING_H2, RING_W3, RING_ALL = 0, 16, 32, 34, 36, 40, 44, 45


def columns(*parts):
    where, n = {}, 0
    for key, width in parts:
        where[key] = (n, width)
        n += width
    return where, n


CONST_AT, CONST_COLS = columns(("ident", 128), ("iota", 8), ("causal", T), ("ones", T), ("clampcol", 1),
                               ("eps", 1), ("minus_half", 8), ("plus_half", 8))
FFN_AT, FFN_COLS = columns(("L0_router", 16), ("L0_bup", 64), ("L0_bdown", DM), ("L1_router", 16), ("gate_b", 8),
                           ("L1_b1", 64), ("L1_b2", DM), ("rhsT", 2 * DM), ("s1", 8), ("s2", 8), ("sh1", 8),
                           ("sh2", 8), ("s3row", DM))


class Steps:

    def __init__(self, eng, sem, base, length):
        self.eng, self.sem, self.base, self.length, self.n = eng, sem, base, length, 0

    def __call__(self, instruction):
        self.n += 1
        assert self.n <= self.length
        instruction.then_inc(self.sem, 1)
        self.eng.wait_ge(self.sem, self.base + self.n)


def decoder(nc, ctxT, mask, x, consts, ffn_small, packs, ring_dram, out):
    ctx = ExitStack()
    with ctx:
        def sb(name, shape, dt=F32):
            return ctx.enter_context(nc.sbuf_tensor(name, shape, dt))

        def sem(name):
            return ctx.enter_context(nc.semaphore(name))

        cst = sb("cst", [128, CONST_COLS])
        ffs = sb("ffs", [128, FFN_COLS])
        wat = [sb(f"wat{s}", [128, SLOT_COLS[s]]) for s in range(2)]
        x_res = sb("x_res", [T, B, DM])
        xT = sb("xT", [128, 2, B * T])
        wring = sb("wring", [128, RSLOTS, RCOLS])
        vbuf = sb("vbuf", [KT, 2, 3, HEADS * 32])
        xb = sb("xb", [T, 2, DM])
        res = sb("res", [T, 2, DM])
        xln = sb("xln", [T, 2, DM])
        st = sb("st", [T, 2, 6])
        mv = sb("mv", [T, 2, 4])
        xTb = sb("xTb", [128, 2, 2, T])

        def carve(arena, name):
            at = [0]

            def take(rows, *dims):
                n = int(np.prod(dims))
                a = arena[0:rows, at[0]:at[0] + n]
                at[0] += n
                assert at[0] <= arena.shape[1], (name, at[0])
                if len(dims) == 1:
                    return a
                names = "abcd"[:len(dims)]
                sizes = {k: v for k, v in zip(names, dims)}
                return a.rearrange(f"p ({' '.join(names)}) -> p {' '.join(names)}", **sizes)
            return take

        big = sb("big", [128, 14336])
        take = carve(big, "big attention")
        kall = take(128, 2, B * S2)
        rowb = take(T, B, S2)
        pts = take(KT, 2, 3, 4 * T)
        rowf = take(T, 2, S2)
        qsq = take(128, 2, S2)
        qrow = take(T, 2, 2, DM)
        take = carve(big, "big features")
        fq = take(128, 2, 8, T)
        fk = take(128, 2, 8, T)
        nT = take(128, 4, 4 * T)
        pj = take(128, 4, 4 * T)
        rT = take(128, 2, 2, 2, T)
        kT = take(128, 2, 4, T)
        take = carve(big, "big hidden")
        take(128, 2 * B * S2)
        hT = take(128, 2, 4, T)
        hid = big[:, 0:14336].rearrange("p (u m n) -> p u m n", u=2, m=8)
        hidh = big[:, 0:7168].rearrange("p (u m n) -> p u m n", u=2, m=8)

        arena = sb("arena", [128, 9200])
        take = carve(arena, "arena attention")
        qT = take(128, 2, 4, T)
        qblk = take(128, 2, HEADS, T)
        pr = take(T, 2, 4, S2)
        sc = take(T, 2, S2)
        oT = take(128, 2, 4, T)
        take = carve(big, "big differential")
        take(128, 6000)
        take(T, 3000 + 2688)
        vd = take(T, 2, 512)
        wd = take(T, 2, 2, T)
        take2 = carve(big, "big differential 2")
        on = take2(T, 2, 512)
        osq = take2(T, 512)
        take = carve(arena, "arena feed-forward")
        acc = take(T, B, DM)
        tmp = take(128, 4, HALF)
        lg = take(T, B, 8)
        top = take(T, B, 8)
        topx = take(T, B, 8)
        topi = topx.bitcast(U32)
        ti = take(T, B, 2)
        oh0, oh1 = take(T, B, 8), take(T, B, 8)
        wts = take(T, B, 8)
        ex = take(T, B, 9)
        gw = take(T, 6, B)
        wtT = take(8, B * T)
        wcol = take(T, 2, B)
        bup = take(128, 2, 8)
        xs = take(T, 2, DM)
        qf = take(T, 2, DM)
        rqf = take(128, 2, DM)
        diag = take(128, 2, 128)
        rsb = take(T, DM)
        qs = take(128, 2, 8)
        qbT = take(128, 2 * T).bitcast(BF16).rearrange("p (a b c) -> p a b c", a=2, b=2)
        rqT = take(128, DM).bitcast(BF16).rearrange("p (a b) -> p a b", a=2)
        junk = sb("junk", [T, DM])

        ctxb = sb("ctxb", [KC, 2, 2, S2])
        maskb = sb("maskb", [T, 2, S2], U8)
        mx = sb("mx", [T, 2, HEADS])
        nm = sb("nm", [T, 2, HEADS])
        nm2 = sb("nm2", [T, 2, HEADS])
        ls = sb("ls", [T, 2, HEADS])
        rv = sb("rv", [T, 2, HEADS])
        fl = sb("fl", [T, 2, HEADS])
        lamt = sb("lamt", [T, 40])
        gam = sb("gam", [T, 64])
        rms = sb("rms", [T, 2, 5, 8])
        qn = sb("qn", [T, 2, 5])

        bank = [ctx.enter_context(nc.psum_tensor(f"bank{i}", [128, 512], F32)) for i in range(8)]
        PROJ, SCORE, PT, OT, TL = bank[0:2], bank[2:4], bank[4:6], bank[6], bank[7]

        def c(key, rows=128):
            a, n = CONST_AT[key]
            return cst[0:rows, a:a + n]

        def f(key, rows=128):
            a, n = FFN_AT[key]
            return ffs[0:rows, a:a + n]

        def w(sub, key, rows=128):
            a, n = sub.at[key]
            return wat[sub.slot][0:rows, a:a + n]

        consts_in, x_in = sem("consts_in"), sem("x_in")
        mask_in = [sem("mask_in0"), sem("mask_in1")]
        weights_in = [sem(f"weights_in_{a.name}") for a in ATTNS]
        ring_in = [sem(f"ring_in{i}") for i in range(RSLOTS)]
        ctx_in = [sem("ctx_in0"), sem("ctx_in1")]
        out_done = sem("out_done")
        passed = {e.engine: sem(f"passed_{n}") for n, e in (("sp", nc.sync), ("dve", nc.vector), ("pool", nc.gpsimd))}
        proj_ready, proj_done = sem("proj_ready"), sem("proj_done")
        kprep_ready, kprep_done = sem("kprep_ready"), sem("kprep_done")
        knorm_ready, knorm_done = sem("knorm_ready"), sem("knorm_done")
        row_step, row_ready = sem("row_step"), sem("row_ready")
        rowf_ready = sem("rowf_ready")
        xtb_ready = sem("xtb_ready")
        qblk_ready = sem("qblk_ready")
        rot_step = sem("rot_step")
        sq_ready = sem("sq_ready")
        fsub_ready, feat_ready = sem("fsub_ready"), sem("feat_ready")
        qrow_ready = sem("qrow_ready")
        qn_step, qn_root = sem("qn_step"), sem("qn_root")
        head_ready = sem("head_ready")
        dhead_done = sem("dhead_done")
        mstep = sem("mstep")
        mclip = sem("mclip")
        max_ready = sem("max_ready")
        exp_done = sem("exp_done")
        floor_ready, clip_done, sum_done = sem("floor_ready"), sem("clip_done"), sem("sum_done")
        inv_step, wd_step = sem("inv_step"), sem("wd_step")
        norm_done = sem("norm_done")
        t_ready, t_done = sem("t_ready"), sem("t_done")
        pv_done = sem("pv_done")
        o_step, o_pool = sem("o_step"), sem("o_pool")
        onT_ready = sem("onT_ready")
        ot_done = sem("ot_done")
        hid_ready, hid_done = sem("hid_ready"), sem("hid_done")
        y_ready = sem("y_ready")
        xb_ready = sem("xb_ready")
        ln_dve, ln_pool = sem("ln_dve"), sem("ln_pool")
        ln_in = sem("ln_in")
        xln_ready, xres_done = sem("xln_ready"), sem("xres_done")
        xt_ready, xt_done = sem("xt_ready"), sem("xt_done")
        lam_step, lam_exp = sem("lam_step"), sem("lam_exp")
        v_zero = sem("v_zero")
        rt_ready, rt_step, rt_exp = sem("rt_ready"), [sem("rt_step0"), sem("rt_step1")], sem("rt_exp")
        wt_ready, wt_T, wt_done = sem("wt_ready"), sem("wt_T"), sem("wt_done")
        xs_ready, xs_T, xs_done = sem("xs_ready"), sem("xs_T"), sem("xs_done")
        up_ready, up_done = sem("up_ready"), sem("up_done")
        dn_ready, dn_done = sem("dn_ready"), sem("dn_done")
        col_ready, bup_ready = sem("col_ready"), sem("bup_ready")
        glu_done = sem("glu_done")
        rq_step, rq_T, rq_done = sem("rq_step"), sem("rq_T"), sem("rq_done")
        q_step, q_T, q_done = sem("q_step"), sem("q_T"), sem("q_done")

        block = ctx.enter_context(nc.Block())

        def at(sub, unit, b, k):
            return START + sub.base[unit] + int(sub.per[unit]) * b + k

        def xt_at(sub, b):
            return START + B + sub.base["row"] + b + 1

        def ln_unit(sub, b):
            if isinstance(b, int) and b < 0 and sub.index:
                sub, b = SUBS[sub.index - 1], B + b
            return sub.base["ln"] + int(sub.per["ln"]) * b

        def wait_rows(eng, sub, b):
            eng.wait_ge(xt_done, START + sub.base["row"] + b + 1)

        def wait_xres(eng, sub, b):
            if sub.index == 0:
                eng.wait_ge(x_in, 16)
            else:
                eng.wait_ge(xres_done, START + sub.base["row"] + b + 1 - B)

        def apart(eng):
            eng.sem_inc(passed[eng.engine], 1)

        def sem_heads_free(eng, sub, b, k):
            if sub.dve_frees:
                eng.wait_ge(dhead_done, at(sub, "dhead", b, k))
            else:
                eng.wait_ge(exp_done, at(sub, "head", b, k))

        def pairs(eng, body):
            body(0, True)
            with eng.Fori(1, B // 2) as pair:
                b0 = pair * 2
                body(b0, False)

        def steps(b0, first):
            for s in range(8):
                before = [None if first and s < k else (b0 + (s - k) // 4, (s - k) % 4, (s - k) // 4 % 2)
                          for k in (1, 2)]
                yield (b0 + s // 4, s % 4, s // 4), before[0], before[1], not (first and s < 4)

        @block.sync
        def _(sp):
            sp.dma_start(x_res[:, :, :], x.rearrange("b t d -> t b d")).then_inc(x_in, 16)
            sp.dma_start(cst[:, :], consts).then_inc(consts_in, 16)
            sp.dma_start(wat[0][:, 0:ATTNS[0].cols], packs[0]).then_inc(weights_in[0], 16)
            sp.dma_start(wat[1][:, 0:ATTNS[1].cols], packs[1]).then_inc(weights_in[1], 16)
            sp.dma_start(ffs[:, :], ffn_small).then_inc(consts_in, 16)

            def ring_load(n):
                m = n - RSLOTS
                if 0 <= m < RING_X:
                    sub, e = (SUBS[2], m // 2) if m < RING_L1 else (SUBS[5], (m - RING_L1) // 2)
                    if m % 2 == 0:
                        sp.wait_ge(up_ready, START + sub.base["up"] + 16 * (e + 1))
                    else:
                        sp.wait_ge(dn_ready, START + sub.base["dn"] + 8 + 8 * (e + 1))
                elif RING_X <= m < RING_GLU:
                    sp.wait_ge(y_ready, at(SUBS[10], "batch", B - 1, 1))
                elif m >= RING_GLU:
                    layer, k = (0, 8) if m < RING_H1 else (1, 2 * (m - RING_H1) + 2) if m < RING_H2 else \
                        (2, 2 * (m - RING_H2) + 2)
                    sp.wait_ge(up_ready, START + SUBS[11].base["up"] + (32 if layer == 0 else 32 + 16 * (layer - 1) + 2 * k))
                sp.dma_start(wring[:, n % RSLOTS, :], ring_dram[n, :, :]).then_inc(ring_in[n % RSLOTS], 16)

            def context(sub, second):
                before = ATTNS[:sub.order]
                last = [a for a in before if a.ctx]

                def load(b, p, first):
                    if first and not second and last:
                        sp.wait_ge(proj_ready, at(last[-1], "proj", B - 1, int(last[-1].per["proj"])))
                    elif first and not second:
                        pass
                    elif first:
                        sp.wait_ge(kprep_ready, at(sub, "kprep", B - 2 + p, 2))
                    elif not second:
                        sp.wait_ge(kprep_ready, at(sub, "kprep", b - 2, 2))
                    else:
                        sp.wait_ge(proj_ready, at(sub, "proj", b - 1, 0))
                    apart(sp)
                    if sub.mask and not second and not first:
                        sp.wait_ge(row_ready, b - 1)
                        apart(sp)
                    if sub.mask and not second:
                        sp.dma_start(maskb[:, p, :], mask[bass.ds(b, 1), :].to_broadcast([T, S2])).then_inc(mask_in[p], 16)
                    sp.dma_start(ctxb[:, p, :, :], ctxT[bass.ds(b, 1), :, :, :].rearrange("o k c n -> (o k) c n"))\
                        .then_inc(ctx_in[p], 16)

                def body(b0, first):
                    load(b0, 0, first)
                    load(b0 + 1, 1, first)
                pairs(sp, body)

            for n in range(RSLOTS):
                ring_load(n)
            for sub in SUBS:
                if isinstance(sub, Attn):
                    if sub.ctx:
                        context(sub, 0)
                        context(sub, 1)
                    if sub.order + 2 < len(ATTNS):
                        sp.wait_ge(xt_ready, xt_at(sub, B - 1))
                        nxt = ATTNS[sub.order + 2]
                        sp.dma_start(wat[sub.slot][:, 0:nxt.cols], packs[nxt.order]).then_inc(weights_in[nxt.order], 16)
                else:
                    for n in {2: range(4, 20), 5: range(20, 36), 8: (), 11: range(36, RING_ALL)}[sub.index]:
                        ring_load(n)
            for b in range(B):
                sp.wait_ge(xres_done, START + SUBS[11].base["row"] + b + 1)
                sp.dma_start(out[b, :, :], x_res[:, b, :]).then_inc(out_done, 16)
            sp.wait_ge(out_done, 16 * B)

        @block.tensor
        def _(pe):
            ident = c("ident")
            for s in (proj_ready, kprep_ready, knorm_ready, head_ready, t_ready, pv_done, y_ready, xt_ready, up_ready,
                      dn_ready, q_T):
                pe.sem_inc(s, START)

            def ctx_wait(sub, second, b, p):
                pe.wait_ge(ctx_in[p], 64 * (2 * sub.ctx_before + second) + 8 * (b - p) + 16)

            def k_prep(sub):
                wk = w(sub, "wk", KC).rearrange("p (c n) -> p c n", c=2)

                def one(b, p):
                    ctx_wait(sub, 0, b, p)
                    for m in range(2):
                        pe.wait_ge(kprep_done, at(sub, "kprep", b, m + 1) - 2)
                        for k in range(2):
                            mm = pe.matmul(PROJ[m][:, 0:S2], wk[:, k, 128 * m:128 * m + 128], ctxb[:, p, k, :],
                                           start=(k == 0), stop=(k == 1))
                        mm.then_inc(kprep_ready, 1)
                    if sub.qk_norm:
                        pe.wait_ge(kprep_done, at(sub, "kprep", b, 2))
                        pe.wait_ge(knorm_done, START + b)
                        for m in range(2):
                            mm = pe.matmul(SCORE[0][0:T, 0:S2], c("ones"), qsq[:, m, :], start=(m == 0), stop=(m == 1))
                        mm.then_inc(knorm_ready, 1)

                with pe.Fori(0, B // 2) as pair:
                    b0 = pair * 2
                    one(b0, 0)
                    one(b0 + 1, 1)
                pe.wait_ge(kprep_done, at(sub, "kprep", B, 0))
                if sub.qk_norm:
                    pe.wait_ge(knorm_done, START + B)

            def project(sub, b, p):
                pe.wait_ge(xtb_ready, at(sub, "batch", b, 1))
                wq = w(sub, "wq").rearrange("p (c n) -> p c n", c=2)
                wk = w(sub, "wk", sub.kdim).rearrange("p (c n) -> p c n", c=2)
                wv = w(sub, "wv", sub.kdim).rearrange("p (c n) -> p c n", c=2)
                for i, item in enumerate(sub.items):
                    pe.wait_ge(proj_done, at(sub, "proj", b, i + 1) - 2)
                    ps = PROJ[(p * len(sub.items) + i) % 2]
                    if item in ("q", "k"):
                        wx = wq if item == "q" else wk
                        for m in range(sub.qc // 128):
                            for k in range(2):
                                mm = pe.matmul(ps[:, m * T:(m + 1) * T], wx[:, k, 128 * m:128 * m + 128],
                                               xTb[:, p, k, :], start=(k == 0), stop=(k == 1))
                    elif item == "qrow":
                        for k in range(2):
                            mm = pe.matmul(ps[0:T, 0:DM], xTb[:, p, k, :], wq[:, k, :], start=(k == 0), stop=(k == 1))
                    elif item in ("rq", "rk"):
                        pe.wait_ge(proj_done, at(sub, "proj", b, 2))
                        src = qT if item == "rq" else kT
                        for m in range(2):
                            mm = pe.matmul(ps[:, m * T:(m + 1) * T], w(sub, "rot"), src[:, p, m, :], start=True, stop=True)
                    elif item[0] == "v" and sub.ctx:
                        t = int(item[1])
                        if t == 0:
                            ctx_wait(sub, 1, b, p)
                        for k in range(2):
                            mm = pe.matmul(ps[0:KT, 0:DM], ctxb[:, p, k, t * KT:(t + 1) * KT], wv[:, k, :],
                                           start=(k == 0), stop=(k == 1))
                    elif item[0] == "v":
                        for k in range(2):
                            mm = pe.matmul(ps[0:T, 0:sub.qc], xTb[:, p, k, :], wv[:, k, :], start=(k == 0), stop=(k == 1))
                    else:
                        side, m = "qk".index(item[1]), int(item[2])
                        pe.wait_ge(proj_done, at(sub, "proj", b, 2))
                        if item[0] == "n":
                            pe.wait_ge(sq_ready, 2 * b + side + 1)
                        tab = w(sub, "ones2" if item[0] == "n" else "rf")
                        src = rT[:, p, side, m, :] if item[0] == "n" else (qT, kT)[side][:, p, m, :]
                        for u in range(4):
                            mm = pe.matmul(ps[:, u * T:(u + 1) * T], tab[:, 128 * u:128 * u + 128], src,
                                           start=True, stop=True)
                    mm.then_inc(proj_ready, 1)

            def scores(sub, b, g, p):
                if g == 0:
                    pe.wait_ge(qblk_ready, at(sub, "batch", b, 1))
                    if sub.rope:
                        pe.wait_ge(rot_step, 6 * b + 6)
                    if sub.feats:
                        pe.wait_ge(feat_ready, 4 * b + 4)
                    if "k" in sub.items:
                        pe.wait_ge(proj_done, at(sub, "proj", b, 2))
                for j in range(4):
                    h = 4 * g + j
                    sem_heads_free(pe, sub, b, h - 1)
                    ch = h // sub.hpc
                    if sub.ctx:
                        keys = kall[:, ch, bass.ds(b * S2, S2)]
                    else:
                        keys = (fk if sub.feats else kT)[:, p, ch, :]
                    pe.matmul(SCORE[j % 2][0:T, 0:sub.keys], qblk[:, p, h, :], keys,
                              start=True, stop=True).then_inc(head_ready, 1)

            def transposes(sub, b, g, p):
                pe.wait_ge(norm_done, at(sub, "group", b, g + 1))
                for t in range(sub.tiles):
                    n = g * sub.tiles + t
                    pe.wait_ge(t_done, at(sub, "pt", b, n + 1) - 2)
                    for j in range(2 if sub.diff else 4):
                        src = wd[:, g % 2, j, :] if sub.diff else pr[:, g % 2, j, t * sub.rows:(t + 1) * sub.rows]
                        mm = pe.transpose(PT[n % 2][0:sub.rows, j * T:(j + 1) * T], src, ident[0:T, 0:T])
                    mm.then_inc(t_ready, 1)

            def values(sub, b, g, p):
                pe.wait_ge(t_done, at(sub, "pt", b, (g + 1) * sub.tiles))
                if g == 0:
                    pe.wait_ge(ot_done, at(sub, "batch", b, 0))
                    if sub.mlp:
                        pe.wait_ge(hid_done, START + b)
                    pe.wait_ge(proj_done, at(sub, "proj", b, sub.items.index(f"v{sub.tiles - 1}") + 1))
                    pe.wait_ge(v_zero, 1)
                if sub.diff:
                    for i in range(2):
                        h = 2 * g + i
                        mm = pe.matmul(OT[0:T, 64 * h:64 * h + 64], pts[0:T, g % 2, 0, i * T:(i + 1) * T],
                                       vd[:, p, 64 * h:64 * h + 64], start=True, stop=True)
                else:
                    for j in range(4):
                        h = 4 * g + j
                        for t in range(sub.tiles):
                            mm = pe.matmul(OT[32 * j:32 * j + 32, g * T:(g + 1) * T],
                                           vbuf[0:sub.rows, p, t, 32 * h:32 * h + 32],
                                           pts[0:sub.rows, g % 2, t, j * T:(j + 1) * T],
                                           start=(t == 0), stop=(t == sub.tiles - 1))
                mm.then_inc(pv_done, 1)

            def out_proj(sub, b, p):
                if sub.diff:
                    pe.wait_ge(o_step, 7 * b + 7)
                    for k in range(4):
                        mm = pe.transpose(OT[:, k * T:(k + 1) * T], on[:, p, 128 * k:128 * k + 128], ident[0:T, 0:T])
                    mm.then_inc(onT_ready, 1)
                pe.wait_ge(ot_done, at(sub, "batch", b, 1))
                if sub.mlp:
                    if isinstance(b, int):
                        pe.wait_ge(ring_in[RING_X % RSLOTS], 16 * (RING_X // RSLOTS + 1))
                        pe.wait_ge(ring_in[(RING_X + 1) % RSLOTS], 16 * (RING_X // RSLOTS + 1))
                    w1 = wring[:, RING_X % RSLOTS, :].rearrange("p (k n) -> p k n", k=4)
                    for m in range(4):
                        for k in range(4):
                            mm = pe.matmul(OT[:, m * T:(m + 1) * T], w1[:, k, 128 * m:128 * m + 128], oT[:, p, k, :],
                                           start=(k == 0), stop=(k == 3))
                    mm.then_inc(hid_ready, 1)
                    pe.wait_ge(hid_done, START + b + 1)
                    src, wo = hT, wring[:, (RING_X + 1) % RSLOTS, 0:4 * DM].rearrange("p (k n) -> p k n", k=4)
                else:
                    src, wo = oT, w(sub, "wo").rearrange("p (k n) -> p k n", k=4)
                pe.wait_ge(xt_done, xt_at(sub, b) - 1)
                for k in range(4):
                    mm = pe.matmul(TL[0:T, 0:DM], src[:, p, k, :], wo[:, k, :], start=(k == 0), stop=(k == 3))
                mm.then_inc(y_ready, 1)

            def rows_t(sub, b, p):
                pe.wait_ge(xln_ready, at(sub, "row", b, 1))
                pe.wait_ge(xt_done, xt_at(sub, b) - 1)
                for k in range(2):
                    mm = pe.transpose(TL[:, DM + k * T:DM + (k + 1) * T], xln[:, p, 128 * k:128 * k + 128], ident[0:T, 0:T])
                mm.then_inc(xt_ready, 1)

            def attention(sub):
                pe.wait_ge(weights_in[sub.order], 16)
                if sub.order:
                    last = ATTNS[sub.order - 1]
                    sem_heads_free(pe, last, B, 0)
                    pe.wait_ge(proj_done, at(last, "proj", B, 0))
                if sub.index and isinstance(SUBS[sub.index - 1], Ffn):
                    pe.wait_ge(dn_done, START + SUBS[sub.index - 1].base["dn"] + int(SUBS[sub.index - 1].per["dn"] * B))
                if sub.ctx:
                    k_prep(sub)

                def body(b0, first):
                    for (b, g, p), one, two, tail in steps(b0, first):
                        if g == 0:
                            project(sub, b, p)
                        else:
                            scores(sub, b, g, p)
                        if one:
                            transposes(sub, *one)
                        if g == 2 and tail:
                            out_proj(sub, b - 1, 1 - p)
                        if two:
                            values(sub, *two)
                        if g == 0:
                            scores(sub, b, g, p)
                        if g == 3 and tail:
                            rows_t(sub, b - 1, 1 - p)
                pairs(pe, body)
                transposes(sub, B - 1, 3, 1)
                values(sub, B - 1, 2, 1)
                values(sub, B - 1, 3, 1)
                out_proj(sub, B - 1, 1)
                rows_t(sub, B - 1, 1)

            def ring_wait(n):
                pe.wait_ge(ring_in[n % RSLOTS], 16 * (n // RSLOTS + 1))

            def experts(sub, router, bias, ring):
                pe.wait_ge(xt_done, xt_at(SUBS[sub.index - 1], B - 1))
                n = sub.index // 3
                for t in range(B):
                    for k in range(2):
                        mm = pe.matmul(bank[0][0:T, 8 * t:8 * t + 8], xT[:, k, t * T:(t + 1) * T],
                                       f(router)[:, 8 * k:8 * k + 8], start=(k == 0), stop=(k == 1))
                mm.then_inc(rt_ready, 1)
                pe.wait_ge(wt_ready, n + 1)
                for t in range(B):
                    mm = pe.transpose(bank[1 + t // 4][0:8, t % 4 * T:(t % 4 + 1) * T], wts[:, t, :], ident[0:T, 0:T])
                mm.then_inc(wt_T, 1)
                pe.wait_ge(wt_done, n + 1)
                db, ub = START + sub.base["dn"], START + sub.base["up"]
                for t in range(B):
                    pe.wait_ge(dn_done, db + t - 3)
                    pe.matmul(bank[4 + t % 4][0:T, 0:DM], wtT[:, t * T:(t + 1) * T], f(bias, 8),
                              start=True, stop=True).then_inc(dn_ready, 1)
                if n:
                    for t in range(B):
                        pe.wait_ge(xs_ready, t + 1)
                        if t >= 2:
                            pe.wait_ge(xs_done, t - 1)
                        for k in range(2):
                            mm = pe.transpose(bank[2 + t % 2][:, k * T:(k + 1) * T], xs[:, t % 2, 128 * k:128 * k + 128],
                                              ident[0:T, 0:T])
                        mm.then_inc(xs_T, 1)
                    pe.wait_ge(xs_done, B)

                def one(e0, p):
                    e = e0 + p
                    pe.wait_ge(ring_in[2 * p], 16 * (ring // RSLOTS + 1) + 8 * e0)
                    wu = wring[:, 2 * p, :].rearrange("p (k n) -> p k n", k=2)
                    wdn = wring[:, 2 * p + 1, :].rearrange("p (k n) -> p k n", k=8)
                    for u in range(2):
                        for m in range(8):
                            pe.wait_ge(up_done, ub + 16 * e + 8 * u + m - 3)
                            for k in range(2):
                                mm = pe.matmul(bank[m % 4][:, 0:HALF], wu[:, k, 128 * m:128 * m + 128],
                                               xT[:, k, u * HALF:(u + 1) * HALF], start=(k == 0), stop=(k == 1))
                            mm.then_inc(up_ready, 1)
                    pe.wait_ge(ring_in[2 * p + 1], 16 * (ring // RSLOTS + 1) + 8 * e0)
                    for t in range(B):
                        if t % 4 == 0:
                            pe.wait_ge(up_done, ub + 16 * e + 2 * t + 8)
                        pe.wait_ge(dn_done, db + 8 + 8 * e + t - 3)
                        for k in range(8):
                            mm = pe.matmul(bank[4 + t % 4][0:T, 0:DM], hidh[:, t // 4, k, t % 4 * T:(t % 4 + 1) * T],
                                           wdn[:, k, :], start=(k == 0), stop=(k == 7))
                        mm.then_inc(dn_ready, 1)

                with pe.Fori(0, EXPERTS // 2) as pair:
                    e0 = pair * 2
                    one(e0, 0)
                    one(e0, 1)

            def new_rows(sub):
                with pe.Fori(0, B // 2) as pair:
                    b0 = pair * 2
                    for p in range(2):
                        rows_t(sub, b0 + p, p)

            def quantised(sub):
                pe.wait_ge(xt_done, xt_at(SUBS[sub.index - 1], B - 1))
                pe.wait_ge(rq_step, 9)
                for m in range(2):
                    pe.matmul(bank[1][0:T, 128 * m:128 * m + 128], c("ones"), diag[:, m, :], start=True, stop=True)
                    for k in range(2):
                        mm = pe.transpose(bank[0][:, 256 * k + 128 * m:256 * k + 128 * m + 128],
                                          rqf[:, m, 128 * k:128 * k + 128], ident)
                mm.then_inc(rq_T, 1)
                pe.wait_ge(rq_done, 2)

                def one(b, p):
                    pe.wait_ge(q_step, START + 9 * b + 9)
                    pe.wait_ge(q_done, START + b - 1)
                    for k in range(2):
                        mm = pe.transpose(bank[2 + p][:, k * T:(k + 1) * T], qf[:, p, 128 * k:128 * k + 128], ident[0:T, 0:T])
                    mm.then_inc(q_T, 1)
                    pe.wait_ge(q_done, START + b + 1)
                    pe.wait_ge(dn_done, START + sub.base["dn"] + b - 1)
                    for k in range(2):
                        mm = pe.matmul(bank[4 + p][0:T, 0:DM], qbT[:, p, k, :], rqT[:, k, :], start=(k == 0), stop=(k == 1))
                    mm.then_inc(dn_ready, 1)
                    rows_t(sub, b, p)
                with pe.Fori(0, B // 2) as pair:
                    b0 = pair * 2
                    one(b0, 0)
                    one(b0 + 1, 1)

            def glu(sub):
                pe.wait_ge(xt_done, xt_at(SUBS[sub.index - 1], B - 1))
                ub, db = START + sub.base["up"], START + sub.base["dn"]
                ring_wait(RING_GLU)
                ring_wait(RING_GLU + 1)
                for i in range(16):
                    m, u = i // 2, i % 2
                    if i >= 2:
                        pe.wait_ge(glu_done, i - 1)
                    for s in range(2):
                        wx = wring[:, (RING_GLU + s) % RSLOTS, :].rearrange("p (k n) -> p k n", k=2)
                        for k in range(2):
                            mm = pe.matmul(bank[2 * (i % 2) + s][:, 0:HALF], wx[:, k, 128 * m:128 * m + 128],
                                           xT[:, k, u * HALF:(u + 1) * HALF], start=(k == 0), stop=(k == 1))
                        mm.then_inc(up_ready, 1)
                for layer, ring in ((0, RING_H1), (1, RING_H2)):
                    pe.wait_ge(glu_done, 16)
                    for i in range(16):
                        m, u = i // 2, i % 2
                        if i % 4 == 0:
                            ring_wait(ring + m // 2)
                        n = 16 * layer + i
                        pe.wait_ge(up_done, ub + 16 + (16 * layer if i < 4 else n - 3))
                        wx = wring[:, (ring + m // 2) % RSLOTS, :].rearrange("p (k n) -> p k n", k=8)
                        for k in range(8):
                            mm = pe.matmul(bank[i % 4][:, 0:HALF], wx[:, k, m % 2 * 128:m % 2 * 128 + 128],
                                           hid[:, layer, k, u * HALF:(u + 1) * HALF], start=(k == 0), stop=(k == 7))
                        mm.then_inc(up_ready, 1)
                ring_wait(RING_W3)
                pe.wait_ge(up_done, ub + 48)
                w3 = wring[:, RING_W3 % RSLOTS, :].rearrange("p (k n) -> p k n", k=8)
                for t in range(B):
                    pe.wait_ge(dn_done, db + t - 3)
                    for k in range(8):
                        mm = pe.matmul(bank[4 + t % 4][0:T, 0:DM], hid[:, 0, k, t * T:(t + 1) * T], w3[:, k, :],
                                       start=(k == 0), stop=(k == 7))
                    mm.then_inc(dn_ready, 1)

            pe.wait_ge(x_in, 16)
            pe.wait_ge(consts_in, 32)
            for b in range(B):
                pe.wait_ge(xt_done, START + b)
                for k in range(2):
                    mm = pe.transpose(TL[:, DM + k * T:DM + (k + 1) * T], x_res[:, b, 128 * k:128 * k + 128], ident[0:T, 0:T])
                mm.then_inc(xt_ready, 1)
            for sub in SUBS:
                if isinstance(sub, Attn):
                    attention(sub)
                elif sub.index in (2, 5):
                    experts(sub, "L0_router" if sub.index == 2 else "L1_router", "L0_bdown" if sub.index == 2 else "L1_b2",
                            RING_L0 if sub.index == 2 else RING_L1)
                    new_rows(sub)
                elif sub.index == 8:
                    quantised(sub)
                else:
                    glu(sub)

        @block.scalar
        def _(act):
            for s, n in ((proj_done, 0), (kprep_done, 0), (exp_done, 0), (xt_done, 0), (up_done, 0), (hid_done, 0),
                         (knorm_done, 0), (q_done, 0)):
                act.sem_inc(s, START)

            def k_prep(sub):
                def one(b, p):
                    for m in range(2):
                        act.wait_ge(kprep_ready, at(sub, "kprep", b, m + 1))
                        ins = nc.scalar.activation(kall[:, m, bass.ds(b * S2, S2)], PROJ[m][:, 0:S2], ACT.Identity,
                                                   bias=w(sub, "bk")[:, m:m + 1])
                        if sub.qk_norm:
                            act.wait_ge(knorm_ready, START + b)
                            ins = nc.scalar.activation(qsq[:, m, :], PROJ[m][:, 0:S2], ACT.Square,
                                                       bias=w(sub, "bk")[:, m:m + 1])
                        ins.then_inc(kprep_done, 1)
                    if sub.qk_norm:
                        act.wait_ge(knorm_ready, START + b + 1)
                        nc.scalar.activation(rowb[:, bass.ds(b, 1), :].rearrange("p o n -> p (o n)"),
                                             SCORE[0][0:T, 0:S2], ACT.Sqrt).then_inc(knorm_done, 1)
                with act.Fori(0, B // 2) as pair:
                    b0 = pair * 2
                    one(b0, 0)
                    one(b0 + 1, 1)

            def items(sub, b, p):
                func = ACT.Exp if sub.kind == "causal" else ACT.Identity
                for i, item in enumerate(sub.items):
                    act.wait_ge(proj_ready, at(sub, "proj", b, i + 1))
                    ps = PROJ[(p * len(sub.items) + i) % 2]
                    if item == "q":
                        act.wait_ge(qblk_ready, at(sub, "batch", b, -1))
                        nq = sub.qc // 128
                        for m in range(nq):
                            ins = nc.scalar.activation(qT[:, p, m, :], ps[:, m * T:(m + 1) * T], func,
                                                       bias=w(sub, "bq")[:, m:m + 1])
                    elif item == "k":
                        act.wait_ge(head_ready, START + HEADS * (B * sub.order + b - 1))
                        for m in range(sub.qc // 128):
                            ins = nc.scalar.activation(kT[:, p, m, :], ps[:, m * T:(m + 1) * T], func,
                                                       bias=w(sub, "bk")[:, m:m + 1])
                    elif item[0] == "v":
                        if item == "v0":
                            act.wait_ge(pv_done, at(sub, "group", b, 0) - GROUPS)
                            act.wait_ge(v_zero, 1)
                        t = int(item[1])
                        if sub.diff:
                            ins = nc.scalar.copy(vd[:, p, :], ps[0:T, 0:512])
                        else:
                            ins = nc.scalar.copy(
                                vbuf[0:sub.rows, p, t, :].rearrange("p (h e) -> p h e", e=32)[:, :, 0:16],
                                ps[0:sub.rows, 0:DM].rearrange("p (h e) -> p h e", e=16))
                    elif item == "qrow":
                        ins = nc.scalar.copy(qrow[:, p, 0, :], ps[0:T, 0:DM])
                    elif item in ("rq", "rk"):
                        ins = nc.scalar.copy(rT[:, p, "qk".index(item[1]), :, :],
                                             ps[:, 0:2 * T].rearrange("p (m n) -> p m n", m=2))
                    else:
                        u = 2 * "qk".index(item[1]) + int(item[2])
                        if item[0] == "n":
                            ins = nc.scalar.activation(nT[:, u, :], ps[:, 0:4 * T], ACT.Sqrt)
                        else:
                            ins = nc.scalar.activation(pj[:, u, :], ps[:, 0:4 * T], ACT.Copy, scale=0.125)
                    ins.then_inc(proj_done, 1)
                if sub.feats:
                    for u in range(4):
                        act.wait_ge(fsub_ready, 4 * b + u + 1)
                        dst = (fq, fk)[u // 2][:, p, 4 * (u % 2):4 * (u % 2) + 4, :]
                        nc.scalar.activation(dst, pj[:, u, :].rearrange("p (m n) -> p m n", m=4), ACT.Exp)\
                            .then_inc(feat_ready, 1)

            def exps(sub, b, g, p):
                if sub.kind != "softmax":
                    return
                act.wait_ge(t_ready, at(sub, "pt", b, (g - 1) * sub.tiles))
                for j in range(4):
                    h = 4 * g + j
                    act.wait_ge(max_ready, at(sub, "head", b, h + 1))
                    src = sc[:, j % 2, 0:sub.keys] if sub.dve_frees else SCORE[j % 2][0:T, 0:sub.keys]
                    nc.scalar.activation(pr[:, g % 2, j, 0:sub.keys], src, ACT.Exp, bias=nm[:, p, h:h + 1],
                                         scale=qn[:, p, 4:5] if sub.qk_norm else sub.scale,
                                         accum_out=ls[:, p, h:h + 1]).then_inc(exp_done, 1)
                if sub.clip:
                    nc.scalar.activation(fl[:, p, 4 * g:4 * g + 4], nm[:, p, 4 * g:4 * g + 4], ACT.Exp,
                                         bias=c("clampcol", T)).then_inc(floor_ready, 1)

            def hidden(sub, b, p):
                act.wait_ge(hid_ready, b + 1)
                for m in range(4):
                    ins = nc.scalar.activation(hT[:, p, m, :], OT[:, m * T:(m + 1) * T], ACT.Relu,
                                               bias=w(sub, "b1")[:, m:m + 1])
                ins.then_inc(hid_done, 1)

            def rows_in(sub_row, b):
                act.wait_ge(xt_ready, START + sub_row + b + 1)
                for k in range(2):
                    ins = nc.scalar.copy(xT[:, k, bass.ds(b * T, T)], TL[:, DM + k * T:DM + (k + 1) * T])
                ins.then_inc(xt_done, 1)

            def attention(sub):
                act.wait_ge(weights_in[sub.order], 16)
                if sub.ctx:
                    k_prep(sub)

                def body(b0, first):
                    for (b, g, p), one, two, tail in steps(b0, first):
                        if g == 0:
                            items(sub, b, p)
                        exps(sub, b, g, p)
                        if sub.mlp and g == 2 and tail:
                            hidden(sub, b - 1, 1 - p)
                        if g == 3 and tail:
                            rows_in(B + sub.base["row"], b - 1)
                pairs(act, body)
                if sub.mlp:
                    hidden(sub, B - 1, 1)
                rows_in(B + sub.base["row"], B - 1)

            def experts(sub, bias, func):
                n = sub.index // 3
                act.wait_ge(rt_step[n], 20)
                nc.scalar.activation(ex[:, :, :], ex[:, :, :], ACT.Exp).then_inc(rt_exp, 1)
                act.wait_ge(wt_T, n + 1)
                nc.scalar.copy(wtT[:, 0:HALF], bank[1][0:8, 0:HALF])
                nc.scalar.copy(wtT[:, HALF:2 * HALF], bank[2][0:8, 0:HALF]).then_inc(wt_done, 1)
                if n:
                    for t in range(B):
                        act.wait_ge(xs_T, t + 1)
                        nc.scalar.copy(xT[:, :, t * T:(t + 1) * T],
                                       bank[2 + t % 2][:, 0:2 * T].rearrange("p (m n) -> p m n", m=2)).then_inc(xs_done, 1)
                ub, db = START + sub.base["up"], START + sub.base["dn"]

                def one(e0, p):
                    e = e0 + p
                    nc.scalar.copy(bup[:, p, :], f(bias)[:, bass.ds(8 * e, 8)]).then_inc(bup_ready, 1)
                    act.wait_ge(bup_ready, 8 * n + e + 1)
                    for u in range(2):
                        act.wait_ge(dn_ready, db + 8 * e + 4 * u + 4)
                        for m in range(8):
                            act.wait_ge(up_ready, ub + 16 * e + 8 * u + m + 1)
                            nc.scalar.activation(hidh[:, u, m, :], bank[m % 4][:, 0:HALF], func,
                                                 bias=bup[:, p, m:m + 1]).then_inc(up_done, 1)
                with act.Fori(0, EXPERTS // 2) as pair:
                    e0 = pair * 2
                    one(e0, 0)
                    one(e0, 1)

            def new_rows(sub):
                with act.Fori(0, B // 2) as pair:
                    b0 = pair * 2
                    for p in range(2):
                        rows_in(B + sub.base["row"], b0 + p)

            def quantised(sub):
                act.wait_ge(rq_T, 1)
                nc.scalar.copy(rqT[:, :, :], bank[0][:, 0:512].rearrange("p (k n) -> p k n", k=2)).then_inc(rq_done, 1)
                nc.scalar.copy(rsb[:, :], bank[1][0:T, 0:DM]).then_inc(rq_done, 1)

                def one(b, p):
                    act.wait_ge(q_T, START + b + 1)
                    act.wait_ge(dn_ready, START + sub.base["dn"] + b - 1)
                    nc.scalar.copy(qbT[:, p, :, :], bank[2 + p][:, 0:2 * T].rearrange("p (m n) -> p m n", m=2))\
                        .then_inc(q_done, 1)
                    rows_in(B + sub.base["row"], b)
                with act.Fori(0, B // 2) as pair:
                    b0 = pair * 2
                    one(b0, 0)
                    one(b0 + 1, 1)

            def glu(sub):
                ub = START + sub.base["up"]
                for i in range(16):
                    m = i // 2
                    act.wait_ge(up_ready, ub + 2 * i + 1)
                    if i >= 4:
                        act.wait_ge(glu_done, i - 3)
                    nc.scalar.activation(tmp[:, i % 4, :], bank[2 * (i % 2)][:, 0:HALF], ACT.Silu,
                                         scale=f("s1")[:, m:m + 1]).then_inc(up_done, 1)
                for layer, key in ((0, "sh1"), (1, "sh2")):
                    for i in range(16):
                        m, u = i // 2, i % 2
                        act.wait_ge(up_ready, ub + 32 + 16 * layer + i + 1)
                        nc.scalar.activation(hid[:, 1 - layer, m, u * HALF:(u + 1) * HALF], bank[i % 4][:, 0:HALF], ACT.Gelu,
                                             scale=f(key)[:, m:m + 1]).then_inc(up_done, 1)

            for b in range(B):
                rows_in(0, b)
            act.wait_ge(lam_step, 2)
            nc.scalar.activation(lamt[:, 34:36], lamt[:, 32:34], ACT.Exp).then_inc(lam_exp, 1)
            for sub in SUBS:
                if isinstance(sub, Attn):
                    attention(sub)
                elif sub.index in (2, 5):
                    experts(sub, "L0_bup" if sub.index == 2 else "L1_b1", ACT.Gelu if sub.index == 2 else ACT.Relu)
                    new_rows(sub)
                elif sub.index == 8:
                    quantised(sub)
                else:
                    glu(sub)

        @block.vector
        def _(dve):
            for s in (t_done, ot_done, dhead_done, mstep, max_ready, norm_done, inv_step, ln_dve, xln_ready, dn_done, q_step,
                      qn_step, ln_in):
                dve.sem_inc(s, START)

            def heads(sub, b, g, p):
                for j in range(4):
                    h = 4 * g + j
                    dve.wait_ge(head_ready, START + HEADS * (B * sub.order + b) + h + 1)
                    ps = SCORE[j % 2][0:T, 0:sub.keys]
                    if sub.kind != "softmax":
                        if j == 0:
                            dve.wait_ge(t_ready, at(sub, "pt", b, (g - 1) * sub.tiles))
                        dve.tensor_tensor_reduce(pr[:, g % 2, j, 0:T], ps, c("causal" if sub.kind == "causal" else "ones", T),
                                                 1.0, 0.0, ALU.mult, ALU.add, ls[:, p, h:h + 1]).then_inc(dhead_done, 1)
                        continue
                    if sub.dve_frees:
                        dve.wait_ge(exp_done, at(sub, "head", b, h - 1))
                        apart(dve)
                        dve.tensor_tensor_reduce(sc[:, j % 2, :], ps, rowf[:, p, :], 1.0, LOWEST,
                                                 ALU.add if sub.mask else ALU.mult, ALU.max,
                                                 mx[:, p, h:h + 1]).then_inc(dhead_done, 1)
                        dve.wait_ge(dhead_done, at(sub, "dhead", b, h + 1))
                    else:
                        dve.reduce_max(mx[:, p, h:h + 1], ps, AX_X).then_inc(mstep, 1)
                        dve.wait_ge(mstep, START + plain(sub) * B * HEADS + b * HEADS + h + 1)
                    if sub.clip:
                        dve.tensor_scalar(nm2[:, p, h:h + 1], mx[:, p, h:h + 1], -sub.scale, CLAMP, ALU.mult, ALU.min)\
                            .then_inc(mclip, 1)
                        dve.wait_ge(mclip, HEADS * b + h + 1)
                        ins = dve.tensor_scalar(nm[:, p, h:h + 1], nm2[:, p, h:h + 1], -CLAMP, None, ALU.max)
                    elif sub.qk_norm:
                        ins = dve.tensor_scalar(nm[:, p, h:h + 1], mx[:, p, h:h + 1], qn[:, p, 4:5], -1.0, ALU.mult, ALU.mult)
                    else:
                        ins = dve.tensor_scalar(nm[:, p, h:h + 1], mx[:, p, h:h + 1], -sub.scale, None, ALU.mult)
                    ins.then_inc(max_ready, 1)

            def plain(sub):
                return sum(a.kind == "softmax" and not a.dve_frees for a in ATTNS[:sub.order])

            def norm(sub, b, g, p):
                hs = slice(4 * g, 4 * g + 4)
                if sub.kind == "softmax":
                    dve.wait_ge(exp_done, at(sub, "head", b, 4 * g + 4))
                else:
                    dve.wait_ge(dhead_done, at(sub, "dhead", b, 4 * g + 4))
                if sub.clip:
                    dve.wait_ge(floor_ready, GROUPS * b + g + 1)
                    for j in range(4):
                        h = 4 * g + j
                        ins = dve.tensor_scalar(pr[:, g % 2, j, :], pr[:, g % 2, j, :], 1.0, fl[:, p, h:h + 1], ALU.min, ALU.max)
                    ins.then_inc(clip_done, 1)
                    dve.wait_ge(clip_done, GROUPS * b + g + 1)
                    dve.reduce_sum(ls[:, p, hs], pr[:, g % 2, :, :], AX_X).then_inc(sum_done, 1)
                    dve.wait_ge(sum_done, GROUPS * b + g + 1)
                k = sub.per["inv"] // GROUPS
                step = Steps(dve, inv_step, at(sub, "inv", b, g * k), k)
                if sub.kind == "linear":
                    step(dve.tensor_scalar(mx[:, p, hs], ls[:, p, hs], 1e-6, None, ALU.add))
                    step(dve.reciprocal(rv[:, p, hs], mx[:, p, hs]))
                else:
                    step(dve.reciprocal(rv[:, p, hs], ls[:, p, hs]))
                if sub.diff:
                    odd = rv[:, p, :].rearrange("p (i two) -> p i two", two=2)[:, 2 * g:2 * g + 2, 1]
                    step(dve.tensor_scalar(odd, odd, lamt[:, 38:39], None, ALU.mult))
                    dve.wait_ge(t_ready, at(sub, "pt", b, g - 1))
                    for i in range(2):
                        h = 4 * g + 2 * i
                        ins = dve.tensor_scalar(pr[:, g % 2, 2 * i, 0:T], pr[:, g % 2, 2 * i, 0:T], rv[:, p, h:h + 1], None, ALU.mult)
                    ins.then_inc(wd_step, 1)
                    dve.wait_ge(wd_step, GROUPS * b + g + 1)
                    for i in range(2):
                        h = 4 * g + 2 * i
                        ins = dve.scalar_tensor_tensor(out=wd[:, g % 2, i, :], in0=pr[:, g % 2, 2 * i + 1, 0:T],
                                                       scalar=rv[:, p, h + 1:h + 2], in1=pr[:, g % 2, 2 * i, 0:T],
                                                       op0=ALU.mult, op1=ALU.add)
                else:
                    for j in range(4):
                        h = 4 * g + j
                        ins = dve.tensor_scalar(pr[:, g % 2, j, 0:sub.keys], pr[:, g % 2, j, 0:sub.keys], rv[:, p, h:h + 1],
                                                None, ALU.mult)
                ins.then_inc(norm_done, 1)

            def tiles_in(sub, b, g, p):
                dve.wait_ge(pv_done, at(sub, "group", b, g - 1))
                n = (2 if sub.diff else 4) * T
                for t in range(sub.tiles):
                    k = g * sub.tiles + t
                    dve.wait_ge(t_ready, at(sub, "pt", b, k + 1))
                    dve.tensor_copy(pts[0:sub.rows, g % 2, t, 0:n], PT[k % 2][0:sub.rows, 0:n]).then_inc(t_done, 1)

            def output_in(sub, b, p):
                dve.wait_ge(pv_done, at(sub, "group", b, 4))
                if sub.diff:
                    step = Steps(dve, o_step, 7 * b, 7)
                    step(dve.tensor_copy(on[:, p, :], OT[0:T, :]))
                    step(dve.tensor_tensor(osq[:, :], on[:, p, :], on[:, p, :], ALU.mult))
                    step(dve.reduce_sum(rms[:, p, 0, :], osq[:, :].rearrange("p (h e) -> p h e", h=8), AX_X))
                    dve.wait_ge(o_pool, 2 * b + 2)
                    step(dve.tensor_scalar(rms[:, p, 3, :], rms[:, p, 2, :], 1e-8, None, ALU.add))
                    step(dve.reciprocal(rms[:, p, 4, :], rms[:, p, 3, :]))
                    oh = on[:, p, :].rearrange("p (h e) -> p h e", h=8)
                    step(dve.tensor_tensor(oh, oh, rms[:, p, 4, :].unsqueeze(2).to_broadcast([T, 8, 64]), ALU.mult))
                    step(dve.tensor_tensor(oh, oh, gam[:, :].unsqueeze(1).to_broadcast([T, 8, 64]), ALU.mult))
                else:
                    dve.wait_ge(y_ready, at(sub, "batch", b, -1))
                    if sub.mlp:
                        dve.wait_ge(hid_done, START + b - 1)
                    dve.tensor_tensor(oT[:, p, :, :], OT[:, 0:4 * T].rearrange("p (g n) -> p g n", g=4),
                                      w(sub, "bvT").unsqueeze(2).to_broadcast([128, 4, T]), ALU.add).then_inc(ot_done, 1)

            def stats(sub, b, p, unit):
                v = START + 3 * (sub.base["ln"] + int(sub.per["ln"]) * b + unit)
                dve.wait_ge(ln_dve, v + 1)
                dve.bn_stats(st[:, p, :], res[:, p, :]).then_inc(ln_dve, 1)
                dve.wait_ge(ln_dve, v + 2)
                apart(dve)
                dve.bn_aggr(mv[:, p, 0:2], st[:, p, :]).then_inc(ln_dve, 1)

            def normed(sub, b, p, unit, dst):
                u = sub.base["ln"] + int(sub.per["ln"]) * b + unit
                dve.wait_ge(ln_pool, START + 2 * u + 2)
                return dve.tensor_scalar(dst, res[:, p, :], mv[:, p, 0:1], mv[:, p, 3:4], ALU.subtract, ALU.mult)

            def rows_out(sub, b, p):
                dve.wait_ge(xt_ready, xt_at(sub, b) - 2)
                dve.wait_ge(xres_done, at(sub, "row", b, -1))
                normed(sub, b, p, int(sub.per["ln"]) - 1, xln[:, p, :]).then_inc(xln_ready, 1)

            def ln_first(sub, b, p):
                if sub.diff:
                    dve.wait_ge(onT_ready, b + 1)
                    dve.wait_ge(y_ready, at(sub, "batch", b, -1))
                    dve.tensor_copy(oT[:, p, :, :], OT[:, 0:4 * T].rearrange("p (g n) -> p g n", g=4)).then_inc(ot_done, 1)
                dve.wait_ge(y_ready, at(sub, "batch", b, 1))
                dve.wait_ge(xb_ready, at(sub, "batch", b, 1))
                dve.tensor_tensor(res[:, p, :], TL[0:T, 0:DM], xb[:, p, :], ALU.add).then_inc(ln_dve, 1)
                stats(sub, b, p, 0)

            def ln_second(sub, b, p):
                if sub.qk_norm:
                    step = Steps(dve, ln_in, START + 3 * b, 3)
                    step(normed(sub, b, p, 0, junk[:, :]))
                    step(dve.tensor_tensor(junk[:, :], junk[:, :], w(sub, "ln_g", T), ALU.mult))
                    step(dve.tensor_tensor(junk[:, :], junk[:, :], w(sub, "ln_b", T), ALU.add))
                    wait_xres(dve, sub, b)
                    dve.tensor_tensor(res[:, p, :], junk[:, :], x_res[:, bass.ds(b, 1), :].rearrange("p o n -> p (o n)"),
                                      ALU.add).then_inc(ln_dve, 1)
                    stats(sub, b, p, 1)
                rows_out(sub, b, p)

            def prepare(sub, b, p):
                if sub.mask or sub.qk_norm:
                    dve.tensor_copy(rowf[:, p, :], rowb[:, bass.ds(b, 1), :].rearrange("p o n -> p (o n)")).then_inc(rowf_ready, 1)
                    dve.wait_ge(rowf_ready, (B if sub.qk_norm else 0) + b + 1)
                if sub.rope:
                    step = Steps(dve, rot_step, 6 * b, 6)
                    cos = w(sub, "cos").unsqueeze(1).to_broadcast([128, 2, T])
                    sin = w(sub, "sin").unsqueeze(1).to_broadcast([128, 2, T])
                    for s, src in enumerate((qT, kT)):
                        dve.wait_ge(proj_done, at(sub, "proj", b, 4 + s))
                        if s == 0:
                            dve.wait_ge(proj_done, at(sub, "proj", b, 5))
                        step(dve.tensor_tensor(rT[:, p, s, :, :], rT[:, p, s, :, :], sin, ALU.mult))
                        step(dve.tensor_tensor(src[:, p, 0:2, :], src[:, p, 0:2, :], cos, ALU.mult))
                        step(dve.tensor_tensor(src[:, p, 0:2, :], src[:, p, 0:2, :], rT[:, p, s, :, :], ALU.add))
                if sub.feats:
                    for u in range(4):
                        dve.wait_ge(proj_done, at(sub, "proj", b, 3 + 2 * u + 2))
                        dve.tensor_tensor(pj[:, u, :], pj[:, u, :], nT[:, u, :], ALU.subtract).then_inc(fsub_ready, 1)
                if sub.qk_norm:
                    dve.wait_ge(qrow_ready, b + 1)
                    dve.wait_ge(exp_done, at(sub, "head", b, -HEADS))
                    step = Steps(dve, qn_step, START + 4 * b, 4)
                    step(dve.tensor_tensor_reduce(junk[:, :], qrow[:, p, 1, :], qrow[:, p, 1, :], 1.0, 0.0, ALU.mult, ALU.add,
                                                  qn[:, p, 0:1]))
                    dve.wait_ge(qn_root, b + 1)
                    step(dve.tensor_scalar(qn[:, p, 2:3], qn[:, p, 1:2], 1e-12, None, ALU.max))
                    step(dve.reciprocal(qn[:, p, 3:4], qn[:, p, 2:3]))
                    step(dve.tensor_scalar(qn[:, p, 4:5], qn[:, p, 3:4], sub.scale, None, ALU.mult))

            def key_rows(sub):
                r0 = B if sub.qk_norm else 0

                def one(b, p):
                    row = rowb[:, bass.ds(b, 1), :].rearrange("p o n -> p (o n)")
                    if sub.mask:
                        dve.wait_ge(mask_in[p], 8 * (b - p) + 16)
                        dve.tensor_scalar(row, maskb[:, p, :], BIG, -BIG, ALU.mult, ALU.add).then_inc(row_ready, 1)
                    else:
                        dve.wait_ge(knorm_done, START + b + 1)
                        dve.tensor_scalar(row, row, 1e-12, None, ALU.max).then_inc(row_step, 1)
                        dve.wait_ge(row_step, b + 1)
                        apart(dve)
                        dve.reciprocal(row, row).then_inc(row_ready, 1)
                with dve.Fori(0, B // 2) as pair:
                    b0 = pair * 2
                    one(b0, 0)
                    one(b0 + 1, 1)
                dve.wait_ge(row_ready, r0 + B)

            def attention(sub):
                dve.wait_ge(weights_in[sub.order], 16)
                if sub.mask or sub.qk_norm:
                    dve.wait_ge(xt_done, xt_at(SUBS[sub.index - 1], B - 1))
                    key_rows(sub)

                def body(b0, first):
                    for (b, g, p), one, two, tail in steps(b0, first):
                        if g == 0:
                            if one:
                                tiles_in(sub, *one)
                            prepare(sub, b, p)
                            heads(sub, b, g, p)
                        else:
                            heads(sub, b, g, p)
                            if g == 3 and tail and not sub.qk_norm:
                                ln_second(sub, b - 1, 1 - p)
                            tiles_in(sub, *one)
                        if g == 1 and tail:
                            output_in(sub, b - 1, 1 - p)
                        norm(sub, b, g, p)
                        if g == 2 and tail:
                            ln_first(sub, b - 1, 1 - p)
                        if g == 3 and tail and sub.qk_norm:
                            ln_second(sub, b - 1, 1 - p)
                pairs(dve, body)
                tiles_in(sub, B - 1, 3, 1)
                output_in(sub, B - 1, 1)
                ln_first(sub, B - 1, 1)
                ln_second(sub, B - 1, 1)

            def experts(sub, key):
                n = sub.index // 3
                dve.wait_ge(rt_ready, n + 1)
                step = Steps(dve, rt_step[n], 0, 50)

                def bc(a, k=8):
                    return a.unsqueeze(2).to_broadcast([T, B, k])
                ps = bank[0][0:T, 0:8 * B].rearrange("p (t e) -> p t e", e=8)
                if n:
                    step(dve.tensor_tensor(lg[:, :, :], ps, f("gate_b", T).unsqueeze(1).to_broadcast([T, B, 8]), ALU.add))
                else:
                    step(dve.tensor_copy(lg[:, :, :], ps))
                for t in range(B):
                    step(dve.max(top[:, t, :], lg[:, t, :]))
                for t in range(B):
                    step(dve.max_index(topi[:, t, :], top[:, t, :], lg[:, t, :]))
                step(dve.tensor_copy(ti[:, :, :], topi[:, :, 0:2]))
                step(dve.tensor_tensor(ex[:, :, 0:8], lg[:, :, :], bc(top[:, :, 0]), ALU.subtract))
                step(dve.tensor_tensor(ex[:, :, 8], top[:, :, 1], top[:, :, 0], ALU.subtract))
                assert step.n == 20
                iota = c("iota", T).unsqueeze(1).to_broadcast([T, B, 8])
                step(dve.tensor_tensor(oh0[:, :, :], iota, bc(ti[:, :, 0]), ALU.is_equal))
                step(dve.tensor_tensor(oh1[:, :, :], iota, bc(ti[:, :, 1]), ALU.is_equal))
                dve.wait_ge(rt_exp, n + 1)
                if n == 0:
                    step(dve.tensor_scalar(gw[:, 0, :], ex[:, :, 8], 1.0, None, ALU.add))
                    step(dve.reciprocal(gw[:, 1, :], gw[:, 0, :]))
                    step(dve.tensor_tensor(gw[:, 2, :], gw[:, 1, :], ex[:, :, 8], ALU.mult))
                else:
                    step(dve.reduce_sum(gw[:, 0, :], ex[:, :, 0:8], AX_X))
                    step(dve.reciprocal(gw[:, 1, :], gw[:, 0, :]))
                    step(dve.tensor_tensor(gw[:, 2, :], gw[:, 1, :], ex[:, :, 8], ALU.mult))
                    step(dve.tensor_tensor(gw[:, 3, :], ti[:, :, 1], ti[:, :, 0], ALU.is_gt))
                    step(dve.tensor_scalar(gw[:, 4, :], gw[:, 2, :], 0.0, None, ALU.is_gt))
                    step(dve.tensor_tensor(gw[:, 3, :], gw[:, 3, :], gw[:, 4, :], ALU.mult))
                    step(dve.tensor_scalar(gw[:, 4, :], gw[:, 3, :], -1.0, 1.0, ALU.mult, ALU.add))
                    step(dve.tensor_tensor(gw[:, 2, :], gw[:, 2, :], gw[:, 3, :], ALU.mult))
                    step(dve.tensor_tensor(gw[:, 1, :], gw[:, 1, :], gw[:, 4, :], ALU.mult))
                    step(dve.tensor_tensor(gw[:, 5, :], gw[:, 1, :], gw[:, 2, :], ALU.add))
                first, second = (gw[:, 1, :], gw[:, 2, :]) if n == 0 else (gw[:, 4, :], gw[:, 3, :])
                step(dve.tensor_tensor(oh0[:, :, :], oh0[:, :, :], bc(first), ALU.mult))
                step(dve.tensor_tensor(oh1[:, :, :], oh1[:, :, :], bc(second), ALU.mult))
                dve.tensor_tensor(wts[:, :, :], oh0[:, :, :], oh1[:, :, :], ALU.add).then_inc(wt_ready, 1)
                dve.wait_ge(wt_ready, n + 1)
                db = START + sub.base["dn"]
                for t in range(B):
                    dve.wait_ge(dn_ready, db + t + 1)
                    dve.tensor_copy(acc[:, t, :], bank[4 + t % 4][0:T, 0:DM]).then_inc(dn_done, 1)
                if n:
                    wait_xres(dve, sub, B - 1)
                    for t in range(B):
                        if t >= 2:
                            dve.wait_ge(xs_T, t - 1)
                        dve.tensor_scalar(xs[:, t % 2, :], x_res[:, t, :], gw[:, 5, t:t + 1], None, ALU.mult).then_inc(xs_ready, 1)

                def one(e0, p):
                    e = e0 + p
                    dve.tensor_copy(wcol[:, p, :], wts[:, :, bass.ds(e, 1)].rearrange("p t o -> p (t o)")).then_inc(col_ready, 1)
                    dve.wait_ge(col_ready, 8 * n + e + 1)
                    for t in range(B):
                        dve.wait_ge(dn_ready, db + 8 + 8 * e + t + 1)
                        dve.wait_ge(dn_done, db + 8 * e + t + 1)
                        dve.scalar_tensor_tensor(out=acc[:, t, :], in0=bank[4 + t % 4][0:T, 0:DM], scalar=wcol[:, p, t:t + 1],
                                                 in1=acc[:, t, :], op0=ALU.mult, op1=ALU.add).then_inc(dn_done, 1)
                with dve.Fori(0, EXPERTS // 2) as pair:
                    e0 = pair * 2
                    one(e0, 0)
                    one(e0, 1)
                dve.wait_ge(dn_done, db + 8 + 8 * EXPERTS)
                with dve.Fori(0, B // 2) as pair:
                    b0 = pair * 2
                    for p in range(2):
                        b = b0 + p
                        wait_xres(dve, sub, b)
                        dve.tensor_tensor(res[:, p, :], acc[:, bass.ds(b, 1), :].rearrange("p o n -> p (o n)"),
                                          x_res[:, bass.ds(b, 1), :].rearrange("p o n -> p (o n)"), ALU.add).then_inc(ln_dve, 1)
                        stats(sub, b, p, 0)
                        rows_out(sub, b, p)

            def quantised(sub):
                step = Steps(dve, rq_step, 0, 9)
                rT_ = f("rhsT").rearrange("p (m d) -> p m d", m=2)
                step(dve.tensor_reduce(qs[:, :, 0], rT_, AX_X, ALU.max))
                step(dve.tensor_reduce(qs[:, :, 1], rT_, AX_X, ALU.min))
                step(dve.tensor_scalar(qs[:, :, 2], qs[:, :, 1], -1.0, None, ALU.mult))
                step(dve.tensor_tensor(qs[:, :, 3], qs[:, :, 0], qs[:, :, 2], ALU.max))
                step(dve.tensor_scalar(qs[:, :, 4], qs[:, :, 3], 1e-12, 1.0 / 127.0, ALU.max, ALU.mult))
                step(dve.reciprocal(qs[:, :, 5], qs[:, :, 4]))
                for m in range(2):
                    dve.tensor_scalar(diag[:, m, :], c("ident"), qs[:, m, 4:5], None, ALU.mult)
                    ins = dve.tensor_scalar(rqf[:, m, :], rT_[:, m, :], qs[:, m, 5:6], MAGIC, ALU.mult, ALU.add)
                step(ins)
                step(dve.tensor_scalar(rqf[:, :, :], rqf[:, :, :], -MAGIC, None, ALU.add))
                step(dve.tensor_scalar(rqf[:, :, :], rqf[:, :, :], 127.0, -127.0, ALU.min, ALU.max))
                dve.wait_ge(rq_done, 2)

                def one(b, p):
                    wait_xres(dve, sub, b)
                    dve.wait_ge(q_T, START + b - 1)
                    step = Steps(dve, q_step, START + 9 * b, 9)
                    xr = x_res[:, bass.ds(b, 1), :].rearrange("p o n -> p (o n)")
                    q = qs[0:T, p, :]
                    apart(dve)
                    step(dve.tensor_reduce(q[:, 0:1], xr, AX_X, ALU.max))
                    apart(dve)
                    step(dve.tensor_reduce(q[:, 1:2], xr, AX_X, ALU.min))
                    step(dve.tensor_scalar(q[:, 2:3], q[:, 1:2], -1.0, None, ALU.mult))
                    step(dve.tensor_tensor(q[:, 3:4], q[:, 0:1], q[:, 2:3], ALU.max))
                    step(dve.tensor_scalar(q[:, 4:5], q[:, 3:4], 1e-12, 1.0 / 127.0, ALU.max, ALU.mult))
                    step(dve.reciprocal(q[:, 5:6], q[:, 4:5]))
                    step(dve.tensor_scalar(qf[:, p, :], xr, q[:, 5:6], MAGIC, ALU.mult, ALU.add))
                    step(dve.tensor_scalar(qf[:, p, :], qf[:, p, :], -MAGIC, None, ALU.add))
                    step(dve.tensor_scalar(qf[:, p, :], qf[:, p, :], 127.0, -127.0, ALU.min, ALU.max))
                    dve.wait_ge(dn_ready, START + sub.base["dn"] + b + 1)
                    dve.scalar_tensor_tensor(out=junk[:, :], in0=bank[4 + p][0:T, 0:DM], scalar=q[:, 4:5], in1=rsb[:, :],
                                             op0=ALU.mult, op1=ALU.mult).then_inc(dn_done, 1)
                    dve.wait_ge(dn_done, START + sub.base["dn"] + b + 1)
                    dve.tensor_tensor(res[:, p, :], junk[:, :], xr, ALU.add).then_inc(ln_dve, 1)
                    stats(sub, b, p, 0)
                    rows_out(sub, b, p)
                with dve.Fori(0, B // 2) as pair:
                    b0 = pair * 2
                    one(b0, 0)
                    one(b0 + 1, 1)

            def glu(sub):
                ub, db = START + sub.base["up"], START + sub.base["dn"]
                for i in range(16):
                    m, u = i // 2, i % 2
                    dve.wait_ge(up_ready, ub + 2 * i + 2)
                    dve.wait_ge(up_done, ub + i + 1)
                    dve.scalar_tensor_tensor(out=hid[:, 0, m, u * HALF:(u + 1) * HALF], in0=bank[2 * (i % 2) + 1][:, 0:HALF],
                                             scalar=f("s2")[:, m:m + 1], in1=tmp[:, i % 4, :], op0=ALU.mult, op1=ALU.mult)\
                        .then_inc(glu_done, 1)
                for b in range(B):
                    p = b % 2
                    wait_xres(dve, sub, b)
                    dve.wait_ge(dn_ready, db + b + 1)
                    dve.tensor_tensor(junk[:, :], bank[4 + b % 4][0:T, 0:DM], f("s3row", T), ALU.mult).then_inc(dn_done, 1)
                    dve.wait_ge(dn_done, db + b + 1)
                    dve.tensor_tensor(res[:, p, :], junk[:, :], x_res[:, b, :], ALU.add).then_inc(ln_dve, 1)
                    stats(sub, b, p, 0)
                    dve.wait_ge(xres_done, at(sub, "row", b, -1))
                    normed(sub, b, p, 0, xln[:, p, :]).then_inc(xln_ready, 1)

            dve.wait_ge(weights_in[0], 16)
            a0 = w(ATTNS[0], "lam", T)
            for i in range(2):
                dve.tensor_tensor_reduce(junk[:, 32 * i:32 * i + 32], a0[:, 64 * i:64 * i + 32], a0[:, 64 * i + 32:64 * i + 64],
                                         1.0, 0.0, ALU.mult, ALU.add, lamt[:, 32 + i:33 + i]).then_inc(lam_step, 1)
            dve.tensor_scalar(gam[:, :], w(ATTNS[0], "gamma", T), 1.0 - LAMBDA_INIT, None, ALU.mult).then_inc(lam_step, 1)
            dve.wait_ge(lam_exp, 1)
            dve.tensor_tensor(lamt[:, 37:38], lamt[:, 35:36], lamt[:, 34:35], ALU.subtract).then_inc(lam_step, 1)
            dve.wait_ge(lam_step, 4)
            dve.tensor_scalar(lamt[:, 38:39], lamt[:, 37:38], -LAMBDA_INIT, None, ALU.add).then_inc(lam_step, 1)
            dve.wait_ge(lam_step, 5)
            for sub in SUBS:
                if isinstance(sub, Attn):
                    attention(sub)
                elif sub.index in (2, 5):
                    experts(sub, None)
                elif sub.index == 8:
                    quantised(sub)
                else:
                    glu(sub)

        @block.gpsimd
        def _(pool):
            for s in (xtb_ready, qblk_ready, xb_ready, ln_pool, xres_done):
                pool.sem_inc(s, START)
            nc.gpsimd.memset(vbuf[:, :, :, :], 0.0).then_inc(v_zero, 1)
            pool.wait_ge(consts_in, 32)

            def start_batch(sub, b, p):
                wait_rows(pool, sub, b)
                pool.wait_ge(proj_ready, at(sub, "proj", b - 1, 0))
                apart(pool)
                nc.gpsimd.tensor_copy(xTb[:, p, :, :], xT[:, :, bass.ds(b * T, T)]).then_inc(xtb_ready, 1)

            def spread(sub, b, p):
                if sub.feats:
                    for s, src in enumerate((qT, kT)):
                        pool.wait_ge(proj_done, at(sub, "proj", b, s + 1))
                        nc.gpsimd.tensor_tensor(rT[:, p, s, :, :], src[:, p, 0:2, :], src[:, p, 0:2, :], ALU.mult)\
                            .then_inc(sq_ready, 1)
                    pool.wait_ge(feat_ready, 4 * b + 2)
                    src = fq[:, p, :, :]
                elif sub.rope:
                    pool.wait_ge(rot_step, 6 * b + 3)
                    src = qT[:, p, 0:2, :]
                else:
                    pool.wait_ge(proj_done, at(sub, "proj", b, 1))
                    src = qT[:, p, 0:sub.chunks, :]
                pool.wait_ge(head_ready, START + HEADS * (B * sub.order + b - 1))
                n, k = sub.chunks, sub.hpc
                for m in range(n):
                    ins = nc.gpsimd.tensor_tensor(qblk[:, p, k * m:k * m + k, :],
                                                  src[:, m, :].unsqueeze(1).to_broadcast([128, k, T]),
                                                  w(sub, "headmask").unsqueeze(2).to_broadcast([128, k, T]), ALU.mult)
                ins.then_inc(qblk_ready, 1)

            def residual(sub, b, p):
                pool.wait_ge(ln_dve, START + 3 * ln_unit(sub, b - 2) + 1)
                if sub.qk_norm:
                    pool.wait_ge(proj_done, at(sub, "proj", b, 2))
                    nc.gpsimd.tensor_tensor(qrow[:, p, 1, :], qrow[:, p, 0, :], w(sub, "bqrow", T), ALU.add).then_inc(qrow_ready, 1)
                    pool.wait_ge(qrow_ready, b + 1)
                    nc.gpsimd.tensor_tensor(xb[:, p, :], qrow[:, p, 1, :], w(sub, "bo", T), ALU.add).then_inc(xb_ready, 1)
                    pool.wait_ge(qn_step, START + 4 * b + 1)
                    nc.gpsimd.tensor_tensor(qn[:, p, 1:2], qn[:, p, 0:1], c("plus_half", T)[:, 0:1], ALU.pow).then_inc(qn_root, 1)
                else:
                    wait_xres(pool, sub, b)
                    nc.gpsimd.tensor_tensor(xb[:, p, :], x_res[:, bass.ds(b, 1), :].rearrange("p o n -> p (o n)"),
                                            w(sub, "bo", T), ALU.add).then_inc(xb_ready, 1)

            def ln_root(sub, b, p, unit):
                u = sub.base["ln"] + int(sub.per["ln"]) * b + unit
                pool.wait_ge(ln_dve, START + 3 * u + 3)
                nc.gpsimd.tensor_tensor(mv[:, p, 2:3], mv[:, p, 1:2], c("eps", T), ALU.add).then_inc(ln_pool, 1)
                pool.wait_ge(ln_pool, START + 2 * u + 1)
                nc.gpsimd.tensor_tensor(mv[:, p, 3:4], mv[:, p, 2:3], c("minus_half", T)[:, 0:1], ALU.pow).then_inc(ln_pool, 1)

            def keep_rows(sub, b, p):
                pool.wait_ge(xln_ready, at(sub, "row", b, 1))
                apart(pool)
                nc.gpsimd.tensor_copy(x_res[:, bass.ds(b, 1), :].rearrange("p o n -> p (o n)"), xln[:, p, :])\
                    .then_inc(xres_done, 1)

            def attention(sub):
                pool.wait_ge(weights_in[sub.order], 16)
                if sub.order:
                    pool.wait_ge(proj_ready, at(ATTNS[sub.order - 1], "proj", B, 0))
                if sub.index and isinstance(SUBS[sub.index - 1], Ffn):
                    wait_rows(pool, sub, B - 1)

                def tail_step(g, b, p):
                    if g == 1 and sub.diff:
                        pool.wait_ge(o_step, 7 * b + 3)
                        apart(pool)
                        nc.gpsimd.tensor_scalar(rms[:, p, 1, :], rms[:, p, 0, :], 1.0 / 64, None, ALU.mult).then_inc(o_pool, 1)
                        pool.wait_ge(o_pool, 2 * b + 1)
                        nc.gpsimd.tensor_tensor(rms[:, p, 2, :], rms[:, p, 1, :], c("plus_half", T), ALU.pow).then_inc(o_pool, 1)
                    if g == 2:
                        ln_root(sub, b, p, 0)
                    if g == 3:
                        if sub.qk_norm:
                            ln_root(sub, b, p, 1)
                        keep_rows(sub, b, p)

                def body(b0, first):
                    for (b, g, p), one, two, tail in steps(b0, first):
                        if g == 0:
                            start_batch(sub, b, p)
                            spread(sub, b, p)
                            residual(sub, b, p)
                        elif tail:
                            tail_step(g, b - 1, 1 - p)
                pairs(pool, body)
                for g in (1, 2, 3):
                    tail_step(g, B - 1, 1)

            def feed_forward(sub):
                with pool.Fori(0, B // 2) as pair:
                    b0 = pair * 2
                    for p in range(2):
                        ln_root(sub, b0 + p, p, 0)
                        keep_rows(sub, b0 + p, p)

            for sub in SUBS:
                if isinstance(sub, Attn):
                    attention(sub)
                else:
                    feed_forward(sub)


def _columns_of(vector, rows=128):
    return np.ascontiguousarray(vector.reshape(-1, rows).T)


def _chunks(weight, rows=128):
    k, n = weight.shape[0] // rows, weight.shape[1]
    out = np.zeros((128, k * n), np.float32)
    out[:rows] = weight.reshape(k, rows, n).transpose(1, 0, 2).reshape(rows, k * n)
    return out


def _strips(weight):
    n = weight.shape[1]
    out = np.zeros((4, 32, 4, n), np.float32)
    out[:, 0:16] = weight.reshape(4, 4, 16, n).transpose(1, 2, 0, 3)
    return out.reshape(128, 4 * n)


def _pack(sub, parts):
    out = np.zeros((128, sub.cols), np.float32)
    r = np.arange(128)
    parts["headmask"] = (r[:, None] // (128 // sub.hpc) == np.arange(sub.hpc)[None, :]).astype(np.float32)
    for key, a in parts.items():
        at, n = sub.at[key]
        if a.ndim == 1:
            a = np.broadcast_to(a, (128, a.shape[0]))
        out[:a.shape[0], at:at + a.shape[1]] = a
    return out


def _rope_tables():
    i = np.arange(T)
    inv = (1.0 / 10000.0 ** (np.arange(2, dtype=np.float32) / np.float32(2.0))).astype(np.float32)
    cos, sin = np.ones((16, T), np.float32), np.zeros((16, T), np.float32)
    frame = i // 256
    rest = i - 256 * frame
    for s, pos in enumerate((frame, rest // 16, rest - 16 * (rest // 16))):
        for d in range(4):
            freq = (pos.astype(np.float32) * inv[d % 2]).astype(np.float32)
            cos[4 * s + d], sin[4 * s + d] = np.cos(freq), np.sin(freq)
    rot = np.zeros((128, 128), np.float32)
    for k in range(0, 128, 2):
        rot[k + 1, k], rot[k, k + 1] = -1.0, 1.0
    return np.tile(cos, (8, 1)), np.tile(sin, (8, 1)), rot


def kernel(**inputs):
    import concourse.bacc as bacc
    from concourse.bass_utils import run_bass_kernel_spmd

    a = {k: np.asarray(v) for k, v in inputs.items()}

    consts = np.zeros((128, CONST_COLS), np.float32)
    for key, value in (("ident", np.eye(128)), ("iota", np.broadcast_to(np.arange(8), (128, 8))),
                       ("causal", np.tril(np.ones((128, 128)))[:, 0:T]), ("ones", np.ones((128, T))),
                       ("clampcol", np.full((128, 1), -CLAMP)), ("eps", np.full((128, 1), LN_EPS)),
                       ("minus_half", np.full((128, 8), -0.5)), ("plus_half", np.full((128, 8), 0.5))):
        at, n = CONST_AT[key]
        consts[:, at:at + n] = value

    ffn_small = np.zeros((128, FFN_COLS), np.float32)

    def put(key, value):
        at, n = FFN_AT[key]
        ffn_small[:value.shape[0], at:at + n] = value

    put("L0_router", _chunks(a["L0_ffn_w_router"].T))
    put("L0_bup", _columns_of(a["L0_ffn_b_up"].reshape(-1)))
    put("L0_bdown", a["L0_ffn_b_down"])
    put("L1_router", _chunks(a["L1_ffn_gate_w"]))
    put("gate_b", np.broadcast_to(a["L1_ffn_gate_b"], (128, 8)))
    put("L1_b1", _columns_of(a["L1_ffn_b1"].reshape(-1)))
    put("L1_b2", a["L1_ffn_b2"])
    put("rhsT", _chunks(a["L2_ffn_rhs"].T))
    for key, name in (("s1", "w1_s"), ("s2", "w2_s"), ("sh1", "h1_s"), ("sh2", "h2_s")):
        put(key, _columns_of(a["L3_ffn_" + name]))
    put("s3row", np.broadcast_to(a["L3_ffn_w3_s"], (128, DM)))

    def qkv(sub, wq, wk, wv):
        rows = KC if sub.ctx else 128
        return {"wq": _chunks(wq), "wk": _chunks(wk, rows), "wv": _chunks(wv, rows)}

    def biases(name):
        return {"bq": _columns_of(a[name + "_bq"]), "bk": _columns_of(a[name + "_bk"]),
                "bvT": _strips(a[name + "_bv"].reshape(-1, 1))}

    cos, sin, rot = _rope_tables()
    rf, ones2 = np.zeros((4, 128, 128), np.float32), np.zeros((4, 128, 128), np.float32)
    for u in range(4):
        for i in range(2):
            h = 2 * u + i
            rf[u, 16 * h:16 * h + 16, 64 * i:64 * i + 64] = a["L3_attn_random_features"].T
            ones2[u, 16 * h:16 * h + 16, 64 * i:64 * i + 64] = 1.0
    side_by_side = lambda t: t.transpose(1, 0, 2).reshape(128, -1)
    s = {x.name: x for x in ATTNS}
    w_kv, w_qkv = a["L0_attn_Wkv"], a["L3_attn_w_qkv"].T
    parts = {
        "L0_attn": {**qkv(s["L0_attn"], a["L0_attn_Wq"], w_kv[:, :512], w_kv[:, 512:]), "wo": _chunks(a["L0_attn_Wout"]),
                    "lam": np.concatenate([a["L0_attn_lambda_" + k] for k in ("q1", "k1", "q2", "k2")]),
                    "gamma": a["L0_attn_gamma"]},
        "L0_xattn": {**qkv(s["L0_xattn"], a["L0_xattn_Wq"], a["L0_xattn_Wk"], a["L0_xattn_Wv"]), **biases("L0_xattn"),
                     "wo": _strips(a["L0_xattn_Wo"]), "bo": a["L0_xattn_bo"]},
        "L1_attn": {**qkv(s["L1_attn"], a["L1_attn_Wq"], a["L1_attn_Wk"], a["L1_attn_Wv"]), **biases("L1_attn"),
                    "wo": _strips(a["L1_attn_Wo"]), "bo": a["L1_attn_bo"], "cos": cos, "sin": sin, "rot": rot},
        "L1_xattn": {**qkv(s["L1_xattn"], a["L1_xattn_Wq"], a["L1_xattn_Wk"], a["L1_xattn_Wv"]),
                     "wo": _strips(a["L1_xattn_Wo"])},
        "L2_attn": {**qkv(s["L2_attn"], a["L2_attn_Wq"].T, a["L2_attn_Wk"].T, a["L2_attn_Wv"].T), **biases("L2_attn"),
                    "wo": _strips(a["L2_attn_Wo"].T), "bo": a["L2_attn_bo"]},
        "L2_xattn": {**qkv(s["L2_xattn"], a["L2_xattn_Wq"], a["L2_xattn_Wk"], a["L2_xattn_Wv"]), **biases("L2_xattn"),
                     "wo": _strips(a["L2_xattn_Wo"]), "bo": a["L2_xattn_bo"], "bqrow": a["L2_xattn_bq"],
                     "ln_g": a["L2_xattn_ln_gamma"], "ln_b": a["L2_xattn_ln_beta"]},
        "L3_attn": {**qkv(s["L3_attn"], w_qkv[:, :256], w_qkv[:, 256:512], w_qkv[:, 512:]),
                    "wo": _strips(a["L3_attn_w_out"].T), "bo": a["L3_attn_b_out"],
                    "rf": side_by_side(rf), "ones2": side_by_side(ones2)},
        "L3_xattn": {**qkv(s["L3_xattn"], a["L3_xattn_Wq"], a["L3_xattn_Wk"], a["L3_xattn_Wv"]), **biases("L3_xattn"),
                     "b1": _columns_of(a["L3_xattn_b1"]), "bo": a["L3_xattn_b2"]},
    }
    packs = [_pack(x, parts[x.name]) for x in ATTNS]

    ring = np.zeros((RING_ALL, 128, RCOLS), np.float32)
    for e in range(EXPERTS):
        ring[RING_L0 + 2 * e] = _chunks(a["L0_ffn_w_up"][e].T)
        ring[RING_L0 + 2 * e + 1] = _chunks(a["L0_ffn_w_down"][e].T)
        ring[RING_L1 + 2 * e] = _chunks(a["L1_ffn_w1"][e])
        ring[RING_L1 + 2 * e + 1] = _chunks(a["L1_ffn_w2"][e])
    ring[RING_X] = _strips(a["L3_xattn_W1"])
    ring[RING_X + 1, :, 0:4 * DM] = _chunks(a["L3_xattn_W2"])
    ring[RING_GLU], ring[RING_GLU + 1] = _chunks(a["L3_ffn_w1_w"].T), _chunks(a["L3_ffn_w2_w"].T)
    for j in range(4):
        ring[RING_H1 + j] = _chunks(a["L3_ffn_h1_w"].T[:, 256 * j:256 * j + 256])
        ring[RING_H2 + j] = _chunks(a["L3_ffn_h2_w"].T[:, 256 * j:256 * j + 256])
    ring[RING_W3] = _chunks(a["L3_ffn_w3_w"].T)

    arrays = {"ctxT": np.ascontiguousarray(a["ctx_768"].reshape(B, S2, 2, KC).transpose(0, 3, 2, 1)),
              "mask": a["mask_BxS2_bf1"], "x": a["x"], "consts": consts, "ffn_small": ffn_small, "ring": ring}
    arrays.update({f"pack{i}": p for i, p in enumerate(packs)})

    nc = bacc.Bacc("TRN2", target_bir_lowering=False, num_devices=1)
    dram = {k: nc.dram_tensor("in_" + k, v.shape, mybir.dt.from_np(v.dtype), kind="ExternalInput").ap()
            for k, v in arrays.items()}
    out = nc.dram_tensor("out", (B, T, DM), F32, kind="ExternalOutput").ap()
    decoder(nc, dram["ctxT"], dram["mask"], dram["x"], dram["consts"], dram["ffn_small"],
            [dram[f"pack{i}"] for i in range(len(packs))], dram["ring"], out)
    r = run_bass_kernel_spmd(nc, [{"in_" + k: v for k, v in arrays.items()}], core_ids=[0])
    return r.results[0]["out"]
```

```python
import math
from contextlib import ExitStack

import numpy as np
import concourse.bass as bass
from concourse import mybir

F32 = mybir.dt.float32
BF16 = mybir.dt.bfloat16
U32 = mybir.dt.uint32
U8 = mybir.dt.uint8
ALU = mybir.AluOpType
ACT = mybir.ActivationFunctionType
AX_X = mybir.AxisListType.X

B, T, DM = 8, 112, 256
S2, KC, KT = 375, 96, 125
HEADS, GROUPS = 16, 4
EXPERTS, HID, HALF = 8, 1024, 448
START = 64
LN_EPS = 1e-5
LAMBDA_INIT = 0.8 - 0.6 * math.exp(-0.3 * 1)
CLAMP = 10000.0
BIG = float(2.0 ** 126)
LOWEST = -3.0e38
MAGIC = float(1.5 * 2 ** 23)


class Attn:

    def __init__(self, name, ctx=False, chunks=2, heads_per_chunk=8, scale=0.25, kind="softmax",
                 clip=False, mask=False, qk_norm=False, diff=False, rope=False, feats=False, mlp=False):
        self.name, self.ctx, self.chunks, self.hpc = name, ctx, chunks, heads_per_chunk
        self.scale, self.kind, self.clip, self.mask, self.qk_norm = scale, kind, clip, mask, qk_norm
        self.diff, self.rope, self.feats, self.mlp = diff, rope, feats, mlp
        self.keys = S2 if ctx else T
        self.tiles = 3 if ctx else 1
        self.rows = KT if ctx else T
        self.kdim = KC if ctx else 128
        self.qc = 512 if diff else 256
        self.items = ["q"] + ([] if ctx else ["k"]) + (["qrow"] if qk_norm else [])
        self.items += [f"v{t}" for t in range(self.tiles)]
        if rope:
            self.items += ["rq", "rk"]
        if feats:
            self.items += [f"{what}{s}{m}" for s in "qk" for m in range(2) for what in ("n", "p")]
        self.lag = 1 if ctx else 2
        self.out_at = (self.lag, 1)
        self.y_at = (0, 2) if diff else (self.lag + 1, 1)
        self.ln_at = (3, 1) if ctx else (1, 2) if diff else (0, 2)
        self.rows_at = (2, 2) if diff else (0, 2) if ctx else (1, 2)
        self.first_items = self.items.index(f"v{self.tiles - 1}") + 1
        dve_frees = kind != "softmax" or clip or mask or qk_norm
        self.dve_frees = dve_frees
        self.per = {"proj": len(self.items), "head": HEADS if kind == "softmax" else 0,
                    "dhead": HEADS if dve_frees else 0, "group": GROUPS, "pt": GROUPS * self.tiles,
                    "rsum": GROUPS if kind != "softmax" else 0,
                    "batch": 1, "ln": 2 if qk_norm else 1, "row": 1, "kprep": 2 if ctx else 0,
                    "inv": GROUPS * (2 if diff or kind == "linear" else 1), "mstep": HEADS}
        cols = [("wq", 2 * self.qc), ("wk", 2 * self.qc), ("wv", 2 * self.qc), ("headmask", heads_per_chunk),
                ("bq", 4), ("bk", 4), ("bvT", 4), ("bo", DM)]
        cols += [("b1", 4)] if mlp else [("wo", 4 * DM)]
        if diff:
            cols += [("lam", 4 * 32), ("gamma", 64)]
        if qk_norm:
            cols += [("bqrow", DM), ("ln_g", DM), ("ln_b", DM)]
        if rope:
            cols += [("rot", 128), ("cos", T), ("sin", T)]
        if feats:
            cols += [("rf", 4 * 128), ("ones2", 4 * 128)]
        self.at, n = {}, 0
        for key, width in cols:
            self.at[key] = (n, width)
            n += width
        self.cols = n


    def part(self, n):
        every = list(enumerate(self.items))
        return every[self.first_items:] if n else every[:self.first_items]


class Ffn:

    def __init__(self, name, dn, up=0):
        self.name = name
        self.per = {"ln": 1, "row": 1, "dn": dn / B, "up": up / B}


SUBS = [
    Attn("L0_attn", chunks=4, heads_per_chunk=4, scale=32 ** -0.5, diff=True),
    Attn("L0_xattn", ctx=True, clip=True),
    Ffn("L0_ffn", dn=8 + 8 * EXPERTS, up=16 * EXPERTS),
    Attn("L1_attn", rope=True),
    Attn("L1_xattn", ctx=True, mask=True),
    Ffn("L1_ffn", dn=8 + 8 * EXPERTS, up=16 * EXPERTS),
    Attn("L2_attn", kind="causal"),
    Attn("L2_xattn", ctx=True, qk_norm=True),
    Ffn("L2_ffn", dn=8),
    Attn("L3_attn", kind="linear", chunks=8, heads_per_chunk=2, feats=True),
    Attn("L3_xattn", ctx=True, mlp=True),
    Ffn("L3_ffn", dn=8, up=2 * 16),
]
UNITS = ("rsum", "proj", "head", "dhead", "group", "pt", "batch", "ln", "row", "kprep", "inv", "mstep", "dn", "up")
for _i, _s in enumerate(SUBS):
    _s.index = _i
    _s.base = {u: int(sum(a.per.get(u, 0) * B for a in SUBS[:_i])) for u in UNITS}
ATTNS = [s for s in SUBS if isinstance(s, Attn)]
for _i, _s in enumerate(ATTNS):
    _s.slot = _i % 2
    _s.order = _i
    _s.ctx_before = sum(a.ctx for a in ATTNS[:_i])
SLOT_COLS = [max(a.cols for a in ATTNS if a.slot == s) for s in range(2)]

RSLOTS, RCOLS = 4, 2048
RING_L0, RING_L1, RING_X, RING_GLU, RING_H1, RING_H2, RING_W3, RING_ALL = 0, 16, 32, 34, 36, 40, 44, 45


def columns(*parts):
    where, n = {}, 0
    for key, width in parts:
        where[key] = (n, width)
        n += width
    return where, n


CONST_AT, CONST_COLS = columns(("ident", 128), ("iota", 8), ("causal", T), ("ones", T),
                               ("eps", 1), ("minus_half", 8), ("plus_half", 8))
FFN_AT, FFN_COLS = columns(("L0_router", 16), ("L0_bup", 64), ("L0_bdown", DM), ("L1_router", 16), ("gate_b", 8),
                           ("L1_b1", 64), ("L1_b2", DM), ("rhsT", 2 * DM), ("s1", 8), ("s2", 8), ("sh1", 8),
                           ("sh2", 8), ("s3row", DM))


class Steps:

    def __init__(self, eng, sem, base, length):
        self.eng, self.sem, self.base, self.length, self.n = eng, sem, base, length, 0

    def __call__(self, instruction):
        self.n += 1
        assert self.n <= self.length
        instruction.then_inc(self.sem, 1)
        self.eng.wait_ge(self.sem, self.base + self.n)


def decoder(nc, ctxT, mask, x, consts, ffn_small, packs, ring_dram, out):
    ctx = ExitStack()
    with ctx:
        def sb(name, shape, dt=F32):
            return ctx.enter_context(nc.sbuf_tensor(name, shape, dt))

        def sem(name):
            return ctx.enter_context(nc.semaphore(name))

        cst = sb("cst", [128, CONST_COLS])
        ffs = sb("ffs", [128, FFN_COLS])
        wat = [sb(f"wat{s}", [128, SLOT_COLS[s]]) for s in range(2)]
        x_res = sb("x_res", [T, B, DM])
        xT = sb("xT", [128, 2, B * T])
        wring = sb("wring", [128, RSLOTS, RCOLS])
        vbuf = sb("vbuf", [KT, 2, 3, HEADS * 32])
        xb = sb("xb", [T, 2, DM])
        res = sb("res", [T, 2, DM])
        xln = sb("xln", [T, 2, DM])
        st = sb("st", [T, 2, 6])
        mv = sb("mv", [T, 2, 4])
        xTb = sb("xTb", [128, 2, 2, T])

        def carve(arena, name):
            at = [0]

            def take(rows, *dims):
                n = int(np.prod(dims))
                a = arena[0:rows, at[0]:at[0] + n]
                at[0] += n
                assert at[0] <= arena.shape[1], (name, at[0])
                if len(dims) == 1:
                    return a
                names = "abcd"[:len(dims)]
                sizes = {k: v for k, v in zip(names, dims)}
                return a.rearrange(f"p ({' '.join(names)}) -> p {' '.join(names)}", **sizes)
            return take

        big = sb("big", [128, 14336])
        take = carve(big, "big attention")
        kall = take(128, 2, B * S2)
        rowb = take(T, B, S2)
        pts = take(KT, 2, 3, 4 * T)
        rowf = take(T, 2, S2)
        qsq = take(128, 2, S2)
        qrow = take(T, 2, 2, DM)
        take = carve(big, "big features")
        fq = take(128, 2, 8, T)
        fk = take(128, 2, 8, T)
        nT = take(128, 4, 4 * T)
        pj = take(128, 4, 4 * T)
        rT = take(128, 2, 2, 2, T)
        kT = take(128, 2, 4, T)
        take = carve(big, "big hidden")
        take(128, 2 * B * S2)
        hT = take(128, 2, 4, T)
        hid = big[:, 0:14336].rearrange("p (u m n) -> p u m n", u=2, m=8)
        hidh = big[:, 0:7168].rearrange("p (u m n) -> p u m n", u=2, m=8)

        arena = sb("arena", [128, 9200])
        take = carve(arena, "arena attention")
        qT = take(128, 2, 4, T)
        qblk = take(128, 2, HEADS, T)
        pr = take(T, 2, 4, S2)
        sc = take(T, 2, S2)
        oT = take(128, 2, 4, T)
        take = carve(big, "big differential")
        take(128, 6000)
        take(T, 3000 + 2688)
        vd = take(T, 2, 512)
        wd = take(T, 2, 2, T)
        take2 = carve(big, "big differential 2")
        on = take2(T, 2, 512)
        osq = take2(T, 512)
        take = carve(arena, "arena feed-forward")
        acc = take(T, B, DM)
        tmp = take(128, 4, HALF)
        lg = take(T, B, 8)
        top = take(T, B, 8)
        topx = take(T, B, 8)
        topi = topx.bitcast(U32)
        ti = take(T, B, 2)
        oh0, oh1 = take(T, B, 8), take(T, B, 8)
        wts = take(T, B, 8)
        ex = take(T, B, 9)
        gw = take(T, 6, B)
        wtT = take(8, B * T)
        wcol = take(T, 2, B)
        bup = take(128, 2, 8)
        xs = take(T, 2, DM)
        qf = take(T, 2, DM)
        rqf = take(128, 2, DM)
        diag = take(128, 2, 128)
        rsb = take(T, DM)
        qs = take(128, 2, 8)
        qbT = take(128, 2 * T).bitcast(BF16).rearrange("p (a b c) -> p a b c", a=2, b=2)
        rqT = take(128, DM).bitcast(BF16).rearrange("p (a b) -> p a b", a=2)
        junk = sb("junk", [T, DM])

        ctxb = sb("ctxb", [KC, 2, 2, S2])
        maskb = sb("maskb", [T, 2, S2], U8)
        mx = sb("mx", [T, 2, HEADS])
        nm = sb("nm", [T, 2, HEADS])
        ls = sb("ls", [T, 2, HEADS])
        rv = sb("rv", [T, 2, HEADS])
        lamt = sb("lamt", [T, 40])
        gam = sb("gam", [T, 64])
        rms = sb("rms", [T, 2, 5, 8])
        qn = sb("qn", [T, 2, 5])

        bank = [ctx.enter_context(nc.psum_tensor(f"bank{i}", [128, 512], F32)) for i in range(8)]
        PROJ, SCORE, PT, OT, TL = bank[0:2], bank[2:4], bank[4:6], bank[6], bank[7]

        def c(key, rows=128):
            a, n = CONST_AT[key]
            return cst[0:rows, a:a + n]

        def f(key, rows=128):
            a, n = FFN_AT[key]
            return ffs[0:rows, a:a + n]

        def w(sub, key, rows=128):
            a, n = sub.at[key]
            return wat[sub.slot][0:rows, a:a + n]

        consts_in, x_in = sem("consts_in"), sem("x_in")
        mask_in = [sem("mask_in0"), sem("mask_in1")]
        weights_in = [sem(f"weights_in_{a.name}") for a in ATTNS]
        ring_in = [sem(f"ring_in{i}") for i in range(RSLOTS)]
        ctx_in = [sem("ctx_in0"), sem("ctx_in1")]
        out_done = sem("out_done")
        passed = {e.engine: sem(f"passed_{n}") for n, e in (("sp", nc.sync), ("dve", nc.vector), ("pool", nc.gpsimd))}
        proj_ready, proj_done = sem("proj_ready"), sem("proj_done")
        kprep_ready, kprep_done = sem("kprep_ready"), sem("kprep_done")
        knorm_ready, knorm_done = sem("knorm_ready"), sem("knorm_done")
        row_step, row_ready = sem("row_step"), sem("row_ready")
        rowf_ready = sem("rowf_ready")
        xtb_ready = sem("xtb_ready")
        qblk_ready = sem("qblk_ready")
        rot_step = sem("rot_step")
        sq_ready = sem("sq_ready")
        fsub_ready, feat_ready = sem("fsub_ready"), sem("feat_ready")
        qrow_ready = sem("qrow_ready")
        qn_step, qn_root = sem("qn_step"), sem("qn_root")
        head_ready = sem("head_ready")
        dhead_done = sem("dhead_done")
        mstep = sem("mstep")
        max_ready = sem("max_ready")
        exp_done = sem("exp_done")
        rsum_done = sem("rsum_done")
        inv_step, wd_step = sem("inv_step"), sem("wd_step")
        norm_done = sem("norm_done")
        t_ready, t_done = sem("t_ready"), sem("t_done")
        pv_done = sem("pv_done")
        o_step, o_pool = sem("o_step"), sem("o_pool")
        onT_ready = sem("onT_ready")
        ot_done = sem("ot_done")
        hid_ready, hid_done = sem("hid_ready"), sem("hid_done")
        y_ready = sem("y_ready")
        xb_ready = sem("xb_ready")
        ln_dve, ln_pool = sem("ln_dve"), sem("ln_pool")
        ln_in = sem("ln_in")
        xln_ready, xres_done = sem("xln_ready"), sem("xres_done")
        xt_ready, xt_done = sem("xt_ready"), sem("xt_done")
        lam_step, lam_exp = sem("lam_step"), sem("lam_exp")
        v_zero = sem("v_zero")
        rt_ready, rt_step, rt_exp = sem("rt_ready"), [sem("rt_step0"), sem("rt_step1")], sem("rt_exp")
        wt_ready, wt_T, wt_done = sem("wt_ready"), sem("wt_T"), sem("wt_done")
        xs_ready, xs_T, xs_done = sem("xs_ready"), sem("xs_T"), sem("xs_done")
        up_ready, up_done = sem("up_ready"), sem("up_done")
        dn_ready, dn_done = sem("dn_ready"), sem("dn_done")
        col_ready, bup_ready = sem("col_ready"), sem("bup_ready")
        glu_done = sem("glu_done")
        rq_step, rq_T, rq_done = sem("rq_step"), sem("rq_T"), sem("rq_done")
        q_step, q_T, q_done = sem("q_step"), sem("q_T"), sem("q_done")

        block = ctx.enter_context(nc.Block())

        def at(sub, unit, b, k):
            return START + sub.base[unit] + int(sub.per[unit]) * b + k

        def xt_at(sub, b):
            return START + B + sub.base["row"] + b + 1

        def ln_unit(sub, b):
            if isinstance(b, int) and b < 0 and sub.index:
                sub, b = SUBS[sub.index - 1], B + b
            return sub.base["ln"] + int(sub.per["ln"]) * b

        def wait_rows(eng, sub, b):
            eng.wait_ge(xt_done, START + sub.base["row"] + b + 1)

        def wait_xres(eng, sub, b):
            if sub.index == 0:
                eng.wait_ge(x_in, 16)
            else:
                eng.wait_ge(xres_done, START + sub.base["row"] + b + 1 - B)

        def apart(eng):
            eng.sem_inc(passed[eng.engine], 1)

        def sem_heads_free(eng, sub, b, k):
            if sub.dve_frees:
                eng.wait_ge(dhead_done, at(sub, "dhead", b, k))
            else:
                eng.wait_ge(exp_done, at(sub, "head", b, k))

        def pairs(eng, body):
            body(0, True)
            with eng.Fori(1, B // 2) as pair:
                b0 = pair * 2
                body(b0, False)

        def pipeline(eng, step):
            def run(b0, first, last, count=8):
                for s in range(count):
                    b, g, p = b0 + s // 4, s % 4, s // 4
                    back = [None] * 4
                    for k in range(4):
                        if not (first and s < k) and not (isinstance(b0, int) and 4 * b0 + s - k >= 4 * B):
                            back[k] = (b0 + (s - k) // 4, (s - k) % 4, (s - k) // 4 % 2)
                    step(b, g, p, back, more=not (last and p == 1) and count == 8,
                         tail=not (first and p == 0) and not (count < 8 and p == 1), far=not first)
            run(0, True, False)
            with eng.Fori(1, B // 2 - 1) as pair:
                run(pair * 2, False, False)
            run(B - 2, False, True)
            run(B, False, True, 7)

        @block.sync
        def _(sp):
            sp.dma_start(x_res[:, :, :], x.rearrange("b t d -> t b d")).then_inc(x_in, 16)
            sp.dma_start(cst[:, :], consts).then_inc(consts_in, 16)
            sp.dma_start(wat[0][:, 0:ATTNS[0].cols], packs[0]).then_inc(weights_in[0], 16)
            sp.dma_start(wat[1][:, 0:ATTNS[1].cols], packs[1]).then_inc(weights_in[1], 16)
            sp.dma_start(ffs[:, :], ffn_small).then_inc(consts_in, 16)

            def ring_load(n):
                m = n - RSLOTS
                if 0 <= m < RING_X:
                    sub, e = (SUBS[2], m // 2) if m < RING_L1 else (SUBS[5], (m - RING_L1) // 2)
                    if m % 2 == 0:
                        sp.wait_ge(up_ready, START + sub.base["up"] + 16 * (e + 1))
                    else:
                        sp.wait_ge(dn_ready, START + sub.base["dn"] + 8 + 8 * (e + 1))
                elif RING_X <= m < RING_GLU:
                    sp.wait_ge(y_ready, at(SUBS[10], "batch", B - 1, 1))
                elif m >= RING_GLU:
                    layer, k = (0, 8) if m < RING_H1 else (1, 2 * (m - RING_H1) + 2) if m < RING_H2 else \
                        (2, 2 * (m - RING_H2) + 2)
                    sp.wait_ge(up_ready, START + SUBS[11].base["up"] + (32 if layer == 0 else 32 + 16 * (layer - 1) + 2 * k))
                sp.dma_start(wring[:, n % RSLOTS, :], ring_dram[n, :, :]).then_inc(ring_in[n % RSLOTS], 16)

            def context(sub, second):
                before = ATTNS[:sub.order]
                last = [a for a in before if a.ctx]

                def load(b, p, first):
                    if first and not second and last:
                        sp.wait_ge(proj_ready, at(last[-1], "proj", B - 1, int(last[-1].per["proj"])))
                    elif first and not second:
                        pass
                    elif first:
                        sp.wait_ge(kprep_ready, at(sub, "kprep", B - 2 + p, 2))
                    elif not second:
                        sp.wait_ge(kprep_ready, at(sub, "kprep", b - 2, 2))
                    else:
                        sp.wait_ge(proj_ready, at(sub, "proj", b - 1, 0))
                    apart(sp)
                    if sub.mask and not second and not first:
                        sp.wait_ge(row_ready, b - 1)
                        apart(sp)
                    if sub.mask and not second:
                        sp.dma_start(maskb[:, p, :], mask[bass.ds(b, 1), :].to_broadcast([T, S2])).then_inc(mask_in[p], 16)
                    sp.dma_start(ctxb[:, p, :, :], ctxT[bass.ds(b, 1), :, :, :].rearrange("o k c n -> (o k) c n"))\
                        .then_inc(ctx_in[p], 16)

                def body(b0, first):
                    load(b0, 0, first)
                    load(b0 + 1, 1, first)
                pairs(sp, body)

            for n in range(RSLOTS):
                ring_load(n)
            for sub in SUBS:
                if isinstance(sub, Attn):
                    if sub.ctx:
                        context(sub, 0)
                        context(sub, 1)
                    if sub.order + 2 < len(ATTNS):
                        sp.wait_ge(xt_ready, xt_at(sub, B - 1))
                        nxt = ATTNS[sub.order + 2]
                        sp.dma_start(wat[sub.slot][:, 0:nxt.cols], packs[nxt.order]).then_inc(weights_in[nxt.order], 16)
                else:
                    for n in {2: range(4, 20), 5: range(20, 36), 8: (), 11: range(36, RING_ALL)}[sub.index]:
                        ring_load(n)
            for b in range(B):
                sp.wait_ge(xres_done, START + SUBS[11].base["row"] + b + 1)
                sp.dma_start(out[b, :, :], x_res[:, b, :]).then_inc(out_done, 16)
            sp.wait_ge(out_done, 16 * B)

        @block.tensor
        def _(pe):
            ident = c("ident")
            for s in (proj_ready, kprep_ready, knorm_ready, head_ready, t_ready, pv_done, y_ready, xt_ready, up_ready,
                      dn_ready, q_T):
                pe.sem_inc(s, START)

            def ctx_wait(sub, second, b, p):
                pe.wait_ge(ctx_in[p], 64 * (2 * sub.ctx_before + second) + 8 * (b - p) + 16)

            def k_prep(sub):
                wk = w(sub, "wk", KC).rearrange("p (c n) -> p c n", c=2)

                def one(b, p):
                    ctx_wait(sub, 0, b, p)
                    for m in range(2):
                        pe.wait_ge(kprep_done, at(sub, "kprep", b, m + 1) - 2)
                        for k in range(2):
                            mm = pe.matmul(PROJ[m][:, 0:S2], wk[:, k, 128 * m:128 * m + 128], ctxb[:, p, k, :],
                                           start=(k == 0), stop=(k == 1))
                        mm.then_inc(kprep_ready, 1)
                    if sub.qk_norm:
                        pe.wait_ge(kprep_done, at(sub, "kprep", b, 2))
                        pe.wait_ge(knorm_done, START + b)
                        for m in range(2):
                            mm = pe.matmul(SCORE[0][0:T, 0:S2], c("ones"), qsq[:, m, :], start=(m == 0), stop=(m == 1))
                        mm.then_inc(knorm_ready, 1)

                with pe.Fori(0, B // 2) as pair:
                    b0 = pair * 2
                    one(b0, 0)
                    one(b0 + 1, 1)
                pe.wait_ge(kprep_done, at(sub, "kprep", B, 0))
                if sub.qk_norm:
                    pe.wait_ge(knorm_done, START + B)

            def project(sub, b, p, part):
                if part == 0:
                    pe.wait_ge(xtb_ready, at(sub, "batch", b, 1))
                wq = w(sub, "wq").rearrange("p (c n) -> p c n", c=2)
                wk = w(sub, "wk", sub.kdim).rearrange("p (c n) -> p c n", c=2)
                wv = w(sub, "wv", sub.kdim).rearrange("p (c n) -> p c n", c=2)
                for i, item in sub.part(part):
                    pe.wait_ge(proj_done, at(sub, "proj", b, i + 1) - 2)
                    ps = PROJ[(p * len(sub.items) + i) % 2]
                    if item in ("q", "k"):
                        wx = wq if item == "q" else wk
                        for m in range(sub.qc // 128):
                            for k in range(2):
                                mm = pe.matmul(ps[:, m * T:(m + 1) * T], wx[:, k, 128 * m:128 * m + 128],
                                               xTb[:, p, k, :], start=(k == 0), stop=(k == 1))
                    elif item == "qrow":
                        for k in range(2):
                            mm = pe.matmul(ps[0:T, 0:DM], xTb[:, p, k, :], wq[:, k, :], start=(k == 0), stop=(k == 1))
                    elif item in ("rq", "rk"):
                        pe.wait_ge(proj_done, at(sub, "proj", b, 2))
                        src = qT if item == "rq" else kT
                        for m in range(2):
                            mm = pe.matmul(ps[:, m * T:(m + 1) * T], w(sub, "rot"), src[:, p, m, :], start=True, stop=True)
                    elif item[0] == "v" and sub.ctx:
                        t = int(item[1])
                        if t == 0:
                            ctx_wait(sub, 1, b, p)
                        for k in range(2):
                            mm = pe.matmul(ps[0:KT, 0:DM], ctxb[:, p, k, t * KT:(t + 1) * KT], wv[:, k, :],
                                           start=(k == 0), stop=(k == 1))
                    elif item[0] == "v":
                        for k in range(2):
                            mm = pe.matmul(ps[0:T, 0:sub.qc], xTb[:, p, k, :], wv[:, k, :], start=(k == 0), stop=(k == 1))
                    else:
                        side, m = "qk".index(item[1]), int(item[2])
                        pe.wait_ge(proj_done, at(sub, "proj", b, 2))
                        if item[0] == "n":
                            pe.wait_ge(sq_ready, 2 * b + side + 1)
                        tab = w(sub, "ones2" if item[0] == "n" else "rf")
                        src = rT[:, p, side, m, :] if item[0] == "n" else (qT, kT)[side][:, p, m, :]
                        for u in range(4):
                            mm = pe.matmul(ps[:, u * T:(u + 1) * T], tab[:, 128 * u:128 * u + 128], src,
                                           start=True, stop=True)
                    mm.then_inc(proj_ready, 1)

            def scores_wait(sub, b):
                pe.wait_ge(qblk_ready, at(sub, "batch", b, 1))
                if sub.rope:
                    pe.wait_ge(rot_step, 6 * b + 6)
                if sub.feats:
                    pe.wait_ge(feat_ready, 4 * b + 4)
                if "k" in sub.items:
                    pe.wait_ge(proj_done, at(sub, "proj", b, 2))

            def scores(sub, b, g, p, js=range(4)):
                if g == 0 and js[0] == 0:
                    scores_wait(sub, b)
                for j in js:
                    h = 4 * g + j
                    ch = h // sub.hpc
                    if sub.ctx:
                        sem_heads_free(pe, sub, b, h - 1)
                        pe.matmul(SCORE[j % 2][0:T, 0:S2], qblk[:, p, h, :], kall[:, ch, bass.ds(b * S2, S2)],
                                  start=True, stop=True).then_inc(head_ready, 1)
                    else:
                        if j == 0:
                            sem_heads_free(pe, sub, b, h - 4)
                        mm = pe.matmul(SCORE[g % 2][0:T, j * T:(j + 1) * T], qblk[:, p, h, :],
                                       (fk if sub.feats else kT)[:, p, ch, :], start=True, stop=True)
                        if j == 3:
                            mm.then_inc(head_ready, 4)

            def transposes(sub, b, g, p, tiles=None):
                pe.wait_ge(norm_done, at(sub, "group", b, g + 1))
                for t in range(sub.tiles) if tiles is None else tiles:
                    n = g * sub.tiles + t
                    pe.wait_ge(t_done, at(sub, "pt", b, n + 1) - 2)
                    for j in range(2 if sub.diff else 4):
                        src = wd[:, g % 2, j, :] if sub.diff else pr[:, g % 2, j, t * sub.rows:(t + 1) * sub.rows]
                        mm = pe.transpose(PT[n % 2][0:sub.rows, j * T:(j + 1) * T], src, ident[0:T, 0:T])
                    mm.then_inc(t_ready, 1)

            def values(sub, b, g, p):
                pe.wait_ge(t_done, at(sub, "pt", b, (g + 1) * sub.tiles))
                if g == 0:
                    if sub.diff:
                        if not isinstance(b, int) or b > 0:
                            pe.wait_ge(o_step, 7 * b - 6)
                    else:
                        pe.wait_ge(ot_done, at(sub, "batch", b, 0))
                    if sub.mlp:
                        pe.wait_ge(hid_done, START + b)
                    pe.wait_ge(proj_done, at(sub, "proj", b, sub.items.index(f"v{sub.tiles - 1}") + 1))
                    pe.wait_ge(v_zero, 1)
                if sub.diff:
                    for i in range(2):
                        h = 2 * g + i
                        mm = pe.matmul(OT[0:T, 64 * h:64 * h + 64], pts[0:T, g % 2, 0, i * T:(i + 1) * T],
                                       vd[:, p, 64 * h:64 * h + 64], start=True, stop=True)
                else:
                    for j in range(4):
                        h = 4 * g + j
                        for t in range(sub.tiles):
                            mm = pe.matmul(OT[32 * j:32 * j + 32, g * T:(g + 1) * T],
                                           vbuf[0:sub.rows, p, t, 32 * h:32 * h + 32],
                                           pts[0:sub.rows, g % 2, t, j * T:(j + 1) * T],
                                           start=(t == 0), stop=(t == sub.tiles - 1))
                mm.then_inc(pv_done, 1)

            def normed_output_t(sub, b, p):
                pe.wait_ge(o_step, 7 * b + 7)
                pe.wait_ge(xt_done, xt_at(sub, b) - 1)
                for k in range(4):
                    mm = pe.transpose(TL[:, k * T:(k + 1) * T], on[:, p, 128 * k:128 * k + 128], ident[0:T, 0:T])
                mm.then_inc(onT_ready, 1)

            def out_proj(sub, b, p):
                pe.wait_ge(ot_done, at(sub, "batch", b, 1))
                if sub.mlp:
                    if isinstance(b, int):
                        pe.wait_ge(ring_in[RING_X % RSLOTS], 16 * (RING_X // RSLOTS + 1))
                        pe.wait_ge(ring_in[(RING_X + 1) % RSLOTS], 16 * (RING_X // RSLOTS + 1))
                    w1 = wring[:, RING_X % RSLOTS, :].rearrange("p (k n) -> p k n", k=4)
                    for m in range(4):
                        for k in range(4):
                            mm = pe.matmul(OT[:, m * T:(m + 1) * T], w1[:, k, 128 * m:128 * m + 128], oT[:, p, k, :],
                                           start=(k == 0), stop=(k == 3))
                    mm.then_inc(hid_ready, 1)
                    pe.wait_ge(hid_done, START + b + 1)
                    src, wo = hT, wring[:, (RING_X + 1) % RSLOTS, 0:4 * DM].rearrange("p (k n) -> p k n", k=4)
                else:
                    src, wo = oT, w(sub, "wo").rearrange("p (k n) -> p k n", k=4)
                pe.wait_ge(xt_done, xt_at(sub, b) - 1)
                for k in range(4):
                    mm = pe.matmul(TL[0:T, 0:DM], src[:, p, k, :], wo[:, k, :], start=(k == 0), stop=(k == 3))
                mm.then_inc(y_ready, 1)

            def rows_t(sub, b, p):
                pe.wait_ge(xln_ready, at(sub, "row", b, 1))
                pe.wait_ge(xt_done, xt_at(sub, b) - 1)
                for k in range(2):
                    mm = pe.transpose(TL[:, DM + k * T:DM + (k + 1) * T], xln[:, p, 128 * k:128 * k + 128], ident[0:T, 0:T])
                mm.then_inc(xt_ready, 1)

            def attention(sub):
                pe.wait_ge(weights_in[sub.order], 16)
                if sub.order:
                    last = ATTNS[sub.order - 1]
                    sem_heads_free(pe, last, B, 0)
                    pe.wait_ge(proj_done, at(last, "proj", B, 0))
                if sub.index and isinstance(SUBS[sub.index - 1], Ffn):
                    pe.wait_ge(dn_done, START + SUBS[sub.index - 1].base["dn"] + int(SUBS[sub.index - 1].per["dn"] * B))
                if sub.ctx:
                    k_prep(sub)

                for part in range(2):
                    project(sub, 0, 0, part)

                def step(b, g, p, back, more, tail, far):
                    if sub.mlp and (g, 1) == sub.y_at and tail:
                        out_proj(sub, b - 1, 1 - p)
                    if sub.ctx:
                        if back[0]:
                            scores(sub, b, g, p, (0, 1))
                        if back[sub.lag + 1]:
                            values(sub, *back[sub.lag + 1])
                        if back[0]:
                            scores(sub, b, g, p, (2,))
                        if back[sub.lag]:
                            transposes(sub, *back[sub.lag], tiles=(0,))
                        if back[0]:
                            scores(sub, b, g, p, (3,))
                        if back[sub.lag]:
                            transposes(sub, *back[sub.lag], tiles=(1, 2))
                    else:
                        if back[0]:
                            scores(sub, b, g, p)
                        if back[sub.lag]:
                            transposes(sub, *back[sub.lag])
                        if back[sub.lag + 1]:
                            values(sub, *back[sub.lag + 1])
                    if (g, 2) == sub.rows_at and far:
                        rows_t(sub, b - 2, p)
                    if g == sub.lag and more:
                        project(sub, b + 1, 1 - p, 0)
                        project(sub, b + 1, 1 - p, 1)
                    if sub.diff and g == 3 and tail:
                        normed_output_t(sub, b - 1, 1 - p)
                    if (g, 2) == sub.y_at and far:
                        out_proj(sub, b - 2, p)
                    if (g, 1) == sub.y_at and tail and not sub.mlp:
                        out_proj(sub, b - 1, 1 - p)
                pipeline(pe, step)

            def ring_wait(n):
                pe.wait_ge(ring_in[n % RSLOTS], 16 * (n // RSLOTS + 1))

            def experts(sub, router, bias, ring):
                pe.wait_ge(xt_done, xt_at(SUBS[sub.index - 1], B - 1))
                n = sub.index // 3
                for t in range(B):
                    for k in range(2):
                        mm = pe.matmul(bank[0][0:T, 8 * t:8 * t + 8], xT[:, k, t * T:(t + 1) * T],
                                       f(router)[:, 8 * k:8 * k + 8], start=(k == 0), stop=(k == 1))
                mm.then_inc(rt_ready, 1)
                pe.wait_ge(wt_ready, n + 1)
                for t in range(B):
                    mm = pe.transpose(bank[1 + t // 4][0:8, t % 4 * T:(t % 4 + 1) * T], wts[:, t, :], ident[0:T, 0:T])
                mm.then_inc(wt_T, 1)
                pe.wait_ge(wt_done, n + 1)
                db, ub = START + sub.base["dn"], START + sub.base["up"]
                for t in range(B):
                    pe.wait_ge(dn_done, db + t - 3)
                    pe.matmul(bank[4 + t % 4][0:T, 0:DM], wtT[:, t * T:(t + 1) * T], f(bias, 8),
                              start=True, stop=True).then_inc(dn_ready, 1)
                if n:
                    for t in range(B):
                        pe.wait_ge(xs_ready, t + 1)
                        if t >= 2:
                            pe.wait_ge(xs_done, t - 1)
                        for k in range(2):
                            mm = pe.transpose(bank[2 + t % 2][:, k * T:(k + 1) * T], xs[:, t % 2, 128 * k:128 * k + 128],
                                              ident[0:T, 0:T])
                        mm.then_inc(xs_T, 1)
                    pe.wait_ge(xs_done, B)

                def one(e0, p):
                    e = e0 + p
                    pe.wait_ge(ring_in[2 * p], 16 * (ring // RSLOTS + 1) + 8 * e0)
                    wu = wring[:, 2 * p, :].rearrange("p (k n) -> p k n", k=2)
                    wdn = wring[:, 2 * p + 1, :].rearrange("p (k n) -> p k n", k=8)
                    for u in range(2):
                        for m in range(8):
                            pe.wait_ge(up_done, ub + 16 * e + 8 * u + m - 3)
                            for k in range(2):
                                mm = pe.matmul(bank[m % 4][:, 0:HALF], wu[:, k, 128 * m:128 * m + 128],
                                               xT[:, k, u * HALF:(u + 1) * HALF], start=(k == 0), stop=(k == 1))
                            mm.then_inc(up_ready, 1)
                    pe.wait_ge(ring_in[2 * p + 1], 16 * (ring // RSLOTS + 1) + 8 * e0)
                    for t in range(B):
                        if t % 4 == 0:
                            pe.wait_ge(up_done, ub + 16 * e + 2 * t + 8)
                        pe.wait_ge(dn_done, db + 8 + 8 * e + t - 3)
                        for k in range(8):
                            mm = pe.matmul(bank[4 + t % 4][0:T, 0:DM], hidh[:, t // 4, k, t % 4 * T:(t % 4 + 1) * T],
                                           wdn[:, k, :], start=(k == 0), stop=(k == 7))
                        mm.then_inc(dn_ready, 1)

                with pe.Fori(0, EXPERTS // 2) as pair:
                    e0 = pair * 2
                    one(e0, 0)
                    one(e0, 1)

            def new_rows(sub):
                with pe.Fori(0, B // 2) as pair:
                    b0 = pair * 2
                    for p in range(2):
                        rows_t(sub, b0 + p, p)

            def quantised(sub):
                pe.wait_ge(xt_done, xt_at(SUBS[sub.index - 1], B - 1))
                pe.wait_ge(rq_step, 9)
                for m in range(2):
                    pe.matmul(bank[1][0:T, 128 * m:128 * m + 128], c("ones"), diag[:, m, :], start=True, stop=True)
                    for k in range(2):
                        mm = pe.transpose(bank[0][:, 256 * k + 128 * m:256 * k + 128 * m + 128],
                                          rqf[:, m, 128 * k:128 * k + 128], ident)
                mm.then_inc(rq_T, 1)
                pe.wait_ge(rq_done, 2)

                def one(b, p):
                    pe.wait_ge(q_step, START + 9 * b + 9)
                    pe.wait_ge(q_done, START + b - 1)
                    for k in range(2):
                        mm = pe.transpose(bank[2 + p][:, k * T:(k + 1) * T], qf[:, p, 128 * k:128 * k + 128], ident[0:T, 0:T])
                    mm.then_inc(q_T, 1)
                    pe.wait_ge(q_done, START + b + 1)
                    pe.wait_ge(dn_done, START + sub.base["dn"] + b - 1)
                    for k in range(2):
                        mm = pe.matmul(bank[4 + p][0:T, 0:DM], qbT[:, p, k, :], rqT[:, k, :], start=(k == 0), stop=(k == 1))
                    mm.then_inc(dn_ready, 1)
                    rows_t(sub, b, p)
                with pe.Fori(0, B // 2) as pair:
                    b0 = pair * 2
                    one(b0, 0)
                    one(b0 + 1, 1)

            def glu(sub):
                pe.wait_ge(xt_done, xt_at(SUBS[sub.index - 1], B - 1))
                ub, db = START + sub.base["up"], START + sub.base["dn"]
                ring_wait(RING_GLU)
                ring_wait(RING_GLU + 1)
                for i in range(16):
                    m, u = i // 2, i % 2
                    if i >= 2:
                        pe.wait_ge(glu_done, i - 1)
                    for s in range(2):
                        wx = wring[:, (RING_GLU + s) % RSLOTS, :].rearrange("p (k n) -> p k n", k=2)
                        for k in range(2):
                            mm = pe.matmul(bank[2 * (i % 2) + s][:, 0:HALF], wx[:, k, 128 * m:128 * m + 128],
                                           xT[:, k, u * HALF:(u + 1) * HALF], start=(k == 0), stop=(k == 1))
                        mm.then_inc(up_ready, 1)
                for layer, ring in ((0, RING_H1), (1, RING_H2)):
                    pe.wait_ge(glu_done, 16)
                    for i in range(16):
                        m, u = i // 2, i % 2
                        if i % 4 == 0:
                            ring_wait(ring + m // 2)
                        n = 16 * layer + i
                        pe.wait_ge(up_done, ub + 16 + (16 * layer if i < 4 else n - 3))
                        wx = wring[:, (ring + m // 2) % RSLOTS, :].rearrange("p (k n) -> p k n", k=8)
                        for k in range(8):
                            mm = pe.matmul(bank[i % 4][:, 0:HALF], wx[:, k, m % 2 * 128:m % 2 * 128 + 128],
                                           hid[:, layer, k, u * HALF:(u + 1) * HALF], start=(k == 0), stop=(k == 7))
                        mm.then_inc(up_ready, 1)
                ring_wait(RING_W3)
                pe.wait_ge(up_done, ub + 48)
                w3 = wring[:, RING_W3 % RSLOTS, :].rearrange("p (k n) -> p k n", k=8)
                for t in range(B):
                    pe.wait_ge(dn_done, db + t - 3)
                    for k in range(8):
                        mm = pe.matmul(bank[4 + t % 4][0:T, 0:DM], hid[:, 0, k, t * T:(t + 1) * T], w3[:, k, :],
                                       start=(k == 0), stop=(k == 7))
                    mm.then_inc(dn_ready, 1)

            pe.wait_ge(x_in, 16)
            pe.wait_ge(consts_in, 32)
            for b in range(B):
                pe.wait_ge(xt_done, START + b)
                for k in range(2):
                    mm = pe.transpose(TL[:, DM + k * T:DM + (k + 1) * T], x_res[:, b, 128 * k:128 * k + 128], ident[0:T, 0:T])
                mm.then_inc(xt_ready, 1)
            for sub in SUBS:
                if isinstance(sub, Attn):
                    attention(sub)
                elif sub.index in (2, 5):
                    experts(sub, "L0_router" if sub.index == 2 else "L1_router", "L0_bdown" if sub.index == 2 else "L1_b2",
                            RING_L0 if sub.index == 2 else RING_L1)
                    new_rows(sub)
                elif sub.index == 8:
                    quantised(sub)
                else:
                    glu(sub)

        @block.scalar
        def _(act):
            for s, n in ((proj_done, 0), (kprep_done, 0), (t_done, 0), (exp_done, 0), (xt_done, 0), (up_done, 0), (hid_done, 0),
                         (knorm_done, 0), (q_done, 0)):
                act.sem_inc(s, START)

            def k_prep(sub):
                def one(b, p):
                    for m in range(2):
                        act.wait_ge(kprep_ready, at(sub, "kprep", b, m + 1))
                        ins = nc.scalar.activation(kall[:, m, bass.ds(b * S2, S2)], PROJ[m][:, 0:S2], ACT.Identity,
                                                   bias=w(sub, "bk")[:, m:m + 1])
                        if sub.qk_norm:
                            act.wait_ge(knorm_ready, START + b)
                            ins = nc.scalar.activation(qsq[:, m, :], PROJ[m][:, 0:S2], ACT.Square,
                                                       bias=w(sub, "bk")[:, m:m + 1])
                        ins.then_inc(kprep_done, 1)
                    if sub.qk_norm:
                        act.wait_ge(knorm_ready, START + b + 1)
                        nc.scalar.activation(rowb[:, bass.ds(b, 1), :].rearrange("p o n -> p (o n)"),
                                             SCORE[0][0:T, 0:S2], ACT.Sqrt).then_inc(knorm_done, 1)
                with act.Fori(0, B // 2) as pair:
                    b0 = pair * 2
                    one(b0, 0)
                    one(b0 + 1, 1)

            def items(sub, b, p, part):
                func = ACT.Exp if sub.kind == "causal" else ACT.Identity
                for i, item in sub.part(part):
                    act.wait_ge(proj_ready, at(sub, "proj", b, i + 1))
                    ps = PROJ[(p * len(sub.items) + i) % 2]
                    if item == "q":
                        act.wait_ge(qblk_ready, at(sub, "batch", b, -1))
                        nq = sub.qc // 128
                        for m in range(nq):
                            ins = nc.scalar.activation(qT[:, p, m, :], ps[:, m * T:(m + 1) * T], func,
                                                       bias=w(sub, "bq")[:, m:m + 1])
                    elif item == "k":
                        act.wait_ge(head_ready, START + HEADS * (B * sub.order + b - 1))
                        for m in range(sub.qc // 128):
                            ins = nc.scalar.activation(kT[:, p, m, :], ps[:, m * T:(m + 1) * T], func,
                                                       bias=w(sub, "bk")[:, m:m + 1])
                    elif item[0] == "v":
                        if item == "v0":
                            act.wait_ge(pv_done, at(sub, "group", b, 0) - GROUPS)
                            act.wait_ge(v_zero, 1)
                        t = int(item[1])
                        if sub.diff:
                            ins = nc.scalar.copy(vd[:, p, :], ps[0:T, 0:512])
                        else:
                            ins = nc.scalar.copy(
                                vbuf[0:sub.rows, p, t, :].rearrange("p (h e) -> p h e", e=32)[:, :, 0:16],
                                ps[0:sub.rows, 0:DM].rearrange("p (h e) -> p h e", e=16))
                    elif item == "qrow":
                        ins = nc.scalar.copy(qrow[:, p, 0, :], ps[0:T, 0:DM])
                    elif item in ("rq", "rk"):
                        ins = nc.scalar.copy(rT[:, p, "qk".index(item[1]), :, :],
                                             ps[:, 0:2 * T].rearrange("p (m n) -> p m n", m=2))
                    else:
                        u = 2 * "qk".index(item[1]) + int(item[2])
                        if item[0] == "n":
                            ins = nc.scalar.activation(nT[:, u, :], ps[:, 0:4 * T], ACT.Sqrt)
                        else:
                            ins = nc.scalar.activation(pj[:, u, :], ps[:, 0:4 * T], ACT.Copy, scale=0.125)
                    ins.then_inc(proj_done, 1)
                if sub.feats and part == 1:
                    for u in range(4):
                        act.wait_ge(fsub_ready, 4 * b + u + 1)
                        dst = (fq, fk)[u // 2][:, p, 4 * (u % 2):4 * (u % 2) + 4, :]
                        nc.scalar.activation(dst, pj[:, u, :].rearrange("p (m n) -> p m n", m=4), ACT.Exp)\
                            .then_inc(feat_ready, 1)

            def exps(sub, b, g, p, js=range(4)):
                if sub.kind != "softmax":
                    return
                if js[0] == 0:
                    act.wait_ge(t_ready, at(sub, "pt", b, (g - 1) * sub.tiles))
                for j in js:
                    h = 4 * g + j
                    if sub.ctx or j == 0:
                        act.wait_ge(max_ready, at(sub, "head", b, h + (1 if sub.ctx else 4)))
                    if not sub.ctx:
                        src = SCORE[g % 2][0:T, j * T:(j + 1) * T]
                    elif sub.dve_frees:
                        src = sc[:, j % 2, :]
                    else:
                        src = SCORE[j % 2][0:T, 0:S2]
                    nc.scalar.activation(pr[:, g % 2, j, 0:sub.keys], src, ACT.Exp, bias=nm[:, p, h:h + 1],
                                         scale=qn[:, p, 4:5] if sub.qk_norm else sub.scale,
                                         accum_out=ls[:, p, h:h + 1]).then_inc(exp_done, 1)

            def tiles_in(sub, b, g, p, tiles):
                if tiles[0] == 0:
                    act.wait_ge(pv_done, at(sub, "group", b, g - 1))
                for t in tiles:
                    k = g * sub.tiles + t
                    act.wait_ge(t_ready, at(sub, "pt", b, k + 1))
                    n = (2 if sub.diff else 4) * T
                    nc.scalar.copy(pts[0:sub.rows, g % 2, t, 0:n], PT[k % 2][0:sub.rows, 0:n]).then_inc(t_done, 1)

            def hidden(sub, b, p):
                act.wait_ge(hid_ready, b + 1)
                for m in range(4):
                    ins = nc.scalar.activation(hT[:, p, m, :], OT[:, m * T:(m + 1) * T], ACT.Relu,
                                               bias=w(sub, "b1")[:, m:m + 1])
                ins.then_inc(hid_done, 1)

            def rows_in(sub_row, b):
                act.wait_ge(xt_ready, START + sub_row + b + 1)
                for k in range(2):
                    ins = nc.scalar.copy(xT[:, k, bass.ds(b * T, T)], TL[:, DM + k * T:DM + (k + 1) * T])
                ins.then_inc(xt_done, 1)

            def attention(sub):
                act.wait_ge(weights_in[sub.order], 16)
                if sub.ctx:
                    k_prep(sub)

                for part in range(2):
                    items(sub, 0, 0, part)

                def step(b, g, p, back, more, tail, far):
                    if sub.mlp and (g, 1) == sub.y_at and tail:
                        hidden(sub, b - 1, 1 - p)
                    if sub.ctx:
                        if back[0]:
                            exps(sub, b, g, p, (0, 1))
                        for t in range(3):
                            if back[sub.lag]:
                                tiles_in(sub, *back[sub.lag], (t,))
                            if back[0] and t < 2:
                                exps(sub, b, g, p, (2 + t,))
                    else:
                        if back[0]:
                            exps(sub, b, g, p)
                        if back[sub.lag]:
                            tiles_in(sub, *back[sub.lag], (0,))
                    if (g, 2) == sub.rows_at and far:
                        rows_in(B + sub.base["row"], b - 2)
                    if g == sub.lag and more:
                        items(sub, b + 1, 1 - p, 0)
                        items(sub, b + 1, 1 - p, 1)
                pipeline(act, step)

            def experts(sub, bias, func):
                n = sub.index // 3
                act.wait_ge(rt_step[n], 20)
                nc.scalar.activation(ex[:, :, :], ex[:, :, :], ACT.Exp).then_inc(rt_exp, 1)
                act.wait_ge(wt_T, n + 1)
                nc.scalar.copy(wtT[:, 0:HALF], bank[1][0:8, 0:HALF])
                nc.scalar.copy(wtT[:, HALF:2 * HALF], bank[2][0:8, 0:HALF]).then_inc(wt_done, 1)
                if n:
                    for t in range(B):
                        act.wait_ge(xs_T, t + 1)
                        nc.scalar.copy(xT[:, :, t * T:(t + 1) * T],
                                       bank[2 + t % 2][:, 0:2 * T].rearrange("p (m n) -> p m n", m=2)).then_inc(xs_done, 1)
                ub, db = START + sub.base["up"], START + sub.base["dn"]

                def one(e0, p):
                    e = e0 + p
                    nc.scalar.copy(bup[:, p, :], f(bias)[:, bass.ds(8 * e, 8)]).then_inc(bup_ready, 1)
                    act.wait_ge(bup_ready, 8 * n + e + 1)
                    for u in range(2):
                        act.wait_ge(dn_ready, db + 8 * e + 4 * u + 4)
                        for m in range(8):
                            act.wait_ge(up_ready, ub + 16 * e + 8 * u + m + 1)
                            nc.scalar.activation(hidh[:, u, m, :], bank[m % 4][:, 0:HALF], func,
                                                 bias=bup[:, p, m:m + 1]).then_inc(up_done, 1)
                with act.Fori(0, EXPERTS // 2) as pair:
                    e0 = pair * 2
                    one(e0, 0)
                    one(e0, 1)

            def new_rows(sub):
                with act.Fori(0, B // 2) as pair:
                    b0 = pair * 2
                    for p in range(2):
                        rows_in(B + sub.base["row"], b0 + p)

            def quantised(sub):
                act.wait_ge(rq_T, 1)
                nc.scalar.copy(rqT[:, :, :], bank[0][:, 0:512].rearrange("p (k n) -> p k n", k=2)).then_inc(rq_done, 1)
                nc.scalar.copy(rsb[:, :], bank[1][0:T, 0:DM]).then_inc(rq_done, 1)

                def one(b, p):
                    act.wait_ge(q_T, START + b + 1)
                    act.wait_ge(dn_ready, START + sub.base["dn"] + b - 1)
                    nc.scalar.copy(qbT[:, p, :, :], bank[2 + p][:, 0:2 * T].rearrange("p (m n) -> p m n", m=2))\
                        .then_inc(q_done, 1)
                    rows_in(B + sub.base["row"], b)
                with act.Fori(0, B // 2) as pair:
                    b0 = pair * 2
                    one(b0, 0)
                    one(b0 + 1, 1)

            def glu(sub):
                ub = START + sub.base["up"]
                for i in range(16):
                    m = i // 2
                    act.wait_ge(up_ready, ub + 2 * i + 1)
                    if i >= 4:
                        act.wait_ge(glu_done, i - 3)
                    nc.scalar.activation(tmp[:, i % 4, :], bank[2 * (i % 2)][:, 0:HALF], ACT.Silu,
                                         scale=f("s1")[:, m:m + 1]).then_inc(up_done, 1)
                for layer, key in ((0, "sh1"), (1, "sh2")):
                    for i in range(16):
                        m, u = i // 2, i % 2
                        act.wait_ge(up_ready, ub + 32 + 16 * layer + i + 1)
                        nc.scalar.activation(hid[:, 1 - layer, m, u * HALF:(u + 1) * HALF], bank[i % 4][:, 0:HALF], ACT.Gelu,
                                             scale=f(key)[:, m:m + 1]).then_inc(up_done, 1)

            for b in range(B):
                rows_in(0, b)
            act.wait_ge(lam_step, 2)
            nc.scalar.activation(lamt[:, 34:36], lamt[:, 32:34], ACT.Exp).then_inc(lam_exp, 1)
            for sub in SUBS:
                if isinstance(sub, Attn):
                    attention(sub)
                elif sub.index in (2, 5):
                    experts(sub, "L0_bup" if sub.index == 2 else "L1_b1", ACT.Gelu if sub.index == 2 else ACT.Relu)
                    new_rows(sub)
                elif sub.index == 8:
                    quantised(sub)
                else:
                    glu(sub)

        @block.vector
        def _(dve):
            for s in (ot_done, dhead_done, mstep, max_ready, norm_done, inv_step, ln_dve, xln_ready, dn_done, q_step,
                      qn_step, ln_in, rsum_done):
                dve.sem_inc(s, START)

            def group_scores(sub, b, g, p):
                hs = slice(4 * g, 4 * g + 4)
                dve.wait_ge(head_ready, START + HEADS * (B * sub.order + b) + 4 * g + 4)
                ps = SCORE[g % 2][0:T, 0:4 * T].rearrange("p (j n) -> p j n", j=4)
                if sub.kind == "softmax":
                    dve.reduce_max(mx[:, p, hs], ps, AX_X).then_inc(mstep, 4)
                    dve.wait_ge(mstep, START + plain(sub) * B * HEADS + b * HEADS + 4 * g + 4)
                    dve.tensor_scalar(nm[:, p, hs], mx[:, p, hs], -sub.scale, None, ALU.mult).then_inc(max_ready, 4)
                    return
                dve.wait_ge(t_ready, at(sub, "pt", b, (g - 1) * sub.tiles))
                dst = pr[:, g % 2, :, 0:T]
                if sub.kind == "causal":
                    tri = c("causal", T).unsqueeze(1).to_broadcast([T, 4, T])
                    dve.tensor_tensor(dst, ps, tri, ALU.mult).then_inc(dhead_done, 4)
                else:
                    dve.tensor_copy(dst, ps).then_inc(dhead_done, 4)
                dve.wait_ge(dhead_done, at(sub, "dhead", b, 4 * g + 4))
                dve.reduce_sum(ls[:, p, hs], dst, AX_X).then_inc(rsum_done, 1)

            def heads(sub, b, g, p, js):
                for j in js:
                    h = 4 * g + j
                    dve.wait_ge(head_ready, START + HEADS * (B * sub.order + b) + h + 1)
                    ps = SCORE[j % 2][0:T, 0:S2]
                    if sub.dve_frees:
                        dve.wait_ge(exp_done, at(sub, "head", b, h - 1))
                        apart(dve)
                    if sub.clip:
                        edge = CLAMP / sub.scale
                        dve.tensor_scalar(sc[:, j % 2, :], ps, edge, -edge, ALU.min, ALU.max).then_inc(dhead_done, 1)
                        dve.wait_ge(dhead_done, at(sub, "dhead", b, h + 1))
                        ps = sc[:, j % 2, :]
                    if sub.mask or sub.qk_norm:
                        dve.tensor_tensor_reduce(sc[:, j % 2, :], ps, rowf[:, p, :], 1.0, LOWEST,
                                                 ALU.add if sub.mask else ALU.mult, ALU.max,
                                                 mx[:, p, h:h + 1]).then_inc(dhead_done, 1)
                        dve.wait_ge(dhead_done, at(sub, "dhead", b, h + 1))
                    else:
                        dve.reduce_max(mx[:, p, h:h + 1], ps, AX_X).then_inc(mstep, 1)
                        dve.wait_ge(mstep, START + plain(sub) * B * HEADS + b * HEADS + h + 1)
                    if sub.qk_norm:
                        ins = dve.tensor_scalar(nm[:, p, h:h + 1], mx[:, p, h:h + 1], qn[:, p, 4:5], -1.0, ALU.mult, ALU.mult)
                    else:
                        ins = dve.tensor_scalar(nm[:, p, h:h + 1], mx[:, p, h:h + 1], -sub.scale, None, ALU.mult)
                    ins.then_inc(max_ready, 1)

            def plain(sub):
                return sum(a.kind == "softmax" and not (a.mask or a.qk_norm) for a in ATTNS[:sub.order])

            def norm(sub, b, g, p):
                hs = slice(4 * g, 4 * g + 4)
                if sub.kind == "softmax":
                    dve.wait_ge(exp_done, at(sub, "head", b, 4 * g + 4))
                else:
                    dve.wait_ge(rsum_done, at(sub, "rsum", b, g + 1))
                k = sub.per["inv"] // GROUPS
                step = Steps(dve, inv_step, at(sub, "inv", b, g * k), k)
                if sub.kind == "linear":
                    step(dve.tensor_scalar(mx[:, p, hs], ls[:, p, hs], 1e-6, None, ALU.add))
                    step(dve.reciprocal(rv[:, p, hs], mx[:, p, hs]))
                else:
                    step(dve.reciprocal(rv[:, p, hs], ls[:, p, hs]))
                if sub.diff:
                    odd = rv[:, p, :].rearrange("p (i two) -> p i two", two=2)[:, 2 * g:2 * g + 2, 1]
                    step(dve.tensor_scalar(odd, odd, lamt[:, 38:39], None, ALU.mult))
                    dve.wait_ge(t_ready, at(sub, "pt", b, g - 1))
                    for i in range(2):
                        h = 4 * g + 2 * i
                        ins = dve.tensor_scalar(pr[:, g % 2, 2 * i, 0:T], pr[:, g % 2, 2 * i, 0:T], rv[:, p, h:h + 1], None, ALU.mult)
                    ins.then_inc(wd_step, 1)
                    dve.wait_ge(wd_step, GROUPS * b + g + 1)
                    for i in range(2):
                        h = 4 * g + 2 * i
                        ins = dve.scalar_tensor_tensor(out=wd[:, g % 2, i, :], in0=pr[:, g % 2, 2 * i + 1, 0:T],
                                                       scalar=rv[:, p, h + 1:h + 2], in1=pr[:, g % 2, 2 * i, 0:T],
                                                       op0=ALU.mult, op1=ALU.add)
                elif not sub.ctx:
                    wts4 = pr[:, g % 2, :, 0:T]
                    ins = dve.tensor_tensor(wts4, wts4, rv[:, p, hs].unsqueeze(2).to_broadcast([T, 4, T]), ALU.mult)
                else:
                    for j in range(4):
                        h = 4 * g + j
                        ins = dve.tensor_scalar(pr[:, g % 2, j, 0:sub.keys], pr[:, g % 2, j, 0:sub.keys], rv[:, p, h:h + 1],
                                                None, ALU.mult)
                ins.then_inc(norm_done, 1)

            def output_in(sub, b, p):
                dve.wait_ge(pv_done, at(sub, "group", b, 4))
                if sub.diff:
                    step = Steps(dve, o_step, 7 * b, 7)
                    step(dve.tensor_copy(on[:, p, :], OT[0:T, :]))
                    step(dve.tensor_tensor(osq[:, :], on[:, p, :], on[:, p, :], ALU.mult))
                    step(dve.reduce_sum(rms[:, p, 0, :], osq[:, :].rearrange("p (h e) -> p h e", h=8), AX_X))
                    dve.wait_ge(o_pool, 2 * b + 2)
                    step(dve.tensor_scalar(rms[:, p, 3, :], rms[:, p, 2, :], 1e-8, None, ALU.add))
                    step(dve.reciprocal(rms[:, p, 4, :], rms[:, p, 3, :]))
                    oh = on[:, p, :].rearrange("p (h e) -> p h e", h=8)
                    step(dve.tensor_tensor(oh, oh, rms[:, p, 4, :].unsqueeze(2).to_broadcast([T, 8, 64]), ALU.mult))
                    step(dve.tensor_tensor(oh, oh, gam[:, :].unsqueeze(1).to_broadcast([T, 8, 64]), ALU.mult))
                else:
                    dve.wait_ge(y_ready, at(sub, "batch", b, -1))
                    if sub.mlp:
                        dve.wait_ge(hid_done, START + b - 1)
                    dve.tensor_tensor(oT[:, p, :, :], OT[:, 0:4 * T].rearrange("p (g n) -> p g n", g=4),
                                      w(sub, "bvT").unsqueeze(2).to_broadcast([128, 4, T]), ALU.add).then_inc(ot_done, 1)

            def stats(sub, b, p, unit):
                v = START + 3 * (sub.base["ln"] + int(sub.per["ln"]) * b + unit)
                dve.wait_ge(ln_dve, v + 1)
                dve.bn_stats(st[:, p, :], res[:, p, :]).then_inc(ln_dve, 1)
                dve.wait_ge(ln_dve, v + 2)
                apart(dve)
                dve.bn_aggr(mv[:, p, 0:2], st[:, p, :]).then_inc(ln_dve, 1)

            def normed(sub, b, p, unit, dst):
                u = sub.base["ln"] + int(sub.per["ln"]) * b + unit
                dve.wait_ge(ln_pool, START + 2 * u + 2)
                return dve.tensor_scalar(dst, res[:, p, :], mv[:, p, 0:1], mv[:, p, 3:4], ALU.subtract, ALU.mult)

            def rows_out(sub, b, p):
                dve.wait_ge(xt_ready, xt_at(sub, b) - 2)
                dve.wait_ge(xres_done, at(sub, "row", b, -1))
                normed(sub, b, p, int(sub.per["ln"]) - 1, xln[:, p, :]).then_inc(xln_ready, 1)

            def normed_output_in(sub, b, p):
                dve.wait_ge(onT_ready, b + 1)
                dve.wait_ge(y_ready, at(sub, "batch", b, -1))
                dve.tensor_copy(oT[:, p, :, :], TL[:, 0:4 * T].rearrange("p (g n) -> p g n", g=4)).then_inc(ot_done, 1)

            def ln_first(sub, b, p):
                dve.wait_ge(y_ready, at(sub, "batch", b, 1))
                dve.wait_ge(xb_ready, at(sub, "batch", b, 1))
                dve.tensor_tensor(res[:, p, :], TL[0:T, 0:DM], xb[:, p, :], ALU.add).then_inc(ln_dve, 1)
                stats(sub, b, p, 0)

            def ln_second(sub, b, p):
                if sub.qk_norm:
                    step = Steps(dve, ln_in, START + 3 * b, 3)
                    step(normed(sub, b, p, 0, junk[:, :]))
                    step(dve.tensor_tensor(junk[:, :], junk[:, :], w(sub, "ln_g", T), ALU.mult))
                    step(dve.tensor_tensor(junk[:, :], junk[:, :], w(sub, "ln_b", T), ALU.add))
                    wait_xres(dve, sub, b)
                    dve.tensor_tensor(res[:, p, :], junk[:, :], x_res[:, bass.ds(b, 1), :].rearrange("p o n -> p (o n)"),
                                      ALU.add).then_inc(ln_dve, 1)
                    stats(sub, b, p, 1)
                rows_out(sub, b, p)

            def prepare(sub, b, p):
                if sub.mask or sub.qk_norm:
                    dve.tensor_copy(rowf[:, p, :], rowb[:, bass.ds(b, 1), :].rearrange("p o n -> p (o n)")).then_inc(rowf_ready, 1)
                    dve.wait_ge(rowf_ready, (B if sub.qk_norm else 0) + b + 1)
                if sub.rope:
                    step = Steps(dve, rot_step, 6 * b, 6)
                    cos = w(sub, "cos").unsqueeze(1).to_broadcast([128, 2, T])
                    sin = w(sub, "sin").unsqueeze(1).to_broadcast([128, 2, T])
                    for s, src in enumerate((qT, kT)):
                        dve.wait_ge(proj_done, at(sub, "proj", b, 4 + s))
                        if s == 0:
                            dve.wait_ge(proj_done, at(sub, "proj", b, 5))
                        step(dve.tensor_tensor(rT[:, p, s, :, :], rT[:, p, s, :, :], sin, ALU.mult))
                        step(dve.tensor_tensor(src[:, p, 0:2, :], src[:, p, 0:2, :], cos, ALU.mult))
                        step(dve.tensor_tensor(src[:, p, 0:2, :], src[:, p, 0:2, :], rT[:, p, s, :, :], ALU.add))
                if sub.feats:
                    for u in range(4):
                        dve.wait_ge(proj_done, at(sub, "proj", b, 3 + 2 * u + 2))
                        dve.tensor_tensor(pj[:, u, :], pj[:, u, :], nT[:, u, :], ALU.subtract).then_inc(fsub_ready, 1)
                if sub.qk_norm:
                    dve.wait_ge(qrow_ready, b + 1)
                    dve.wait_ge(exp_done, at(sub, "head", b, -HEADS))
                    step = Steps(dve, qn_step, START + 4 * b, 4)
                    step(dve.tensor_tensor_reduce(junk[:, :], qrow[:, p, 1, :], qrow[:, p, 1, :], 1.0, 0.0, ALU.mult, ALU.add,
                                                  qn[:, p, 0:1]))
                    dve.wait_ge(qn_root, b + 1)
                    step(dve.tensor_scalar(qn[:, p, 2:3], qn[:, p, 1:2], 1e-12, None, ALU.max))
                    step(dve.reciprocal(qn[:, p, 3:4], qn[:, p, 2:3]))
                    step(dve.tensor_scalar(qn[:, p, 4:5], qn[:, p, 3:4], sub.scale, None, ALU.mult))

            def key_rows(sub):
                r0 = B if sub.qk_norm else 0

                def one(b, p):
                    row = rowb[:, bass.ds(b, 1), :].rearrange("p o n -> p (o n)")
                    if sub.mask:
                        dve.wait_ge(mask_in[p], 8 * (b - p) + 16)
                        dve.tensor_scalar(row, maskb[:, p, :], BIG, -BIG, ALU.mult, ALU.add).then_inc(row_ready, 1)
                    else:
                        dve.wait_ge(knorm_done, START + b + 1)
                        dve.tensor_scalar(row, row, 1e-12, None, ALU.max).then_inc(row_step, 1)
                        dve.wait_ge(row_step, b + 1)
                        apart(dve)
                        dve.reciprocal(row, row).then_inc(row_ready, 1)
                with dve.Fori(0, B // 2) as pair:
                    b0 = pair * 2
                    one(b0, 0)
                    one(b0 + 1, 1)
                dve.wait_ge(row_ready, r0 + B)

            def attention(sub):
                dve.wait_ge(weights_in[sub.order], 16)
                if sub.mask or sub.qk_norm:
                    dve.wait_ge(xt_done, xt_at(SUBS[sub.index - 1], B - 1))
                    key_rows(sub)

                prepare(sub, 0, 0)

                def step(b, g, p, back, more, tail, far):
                    if sub.ctx:
                        if back[0]:
                            heads(sub, b, g, p, (0, 1))
                        if back[1]:
                            norm(sub, *back[1])
                        if back[0]:
                            heads(sub, b, g, p, (2, 3))
                    else:
                        if back[0]:
                            group_scores(sub, b, g, p)
                        if back[1]:
                            norm(sub, *back[1])
                    if (g, 1) == sub.out_at and tail:
                        output_in(sub, b - 1, 1 - p)
                    if g == 3 and tail and sub.diff:
                        normed_output_in(sub, b - 1, 1 - p)
                    for k, there, q in ((1, tail, 1 - p), (2, far, p)):
                        if (g, k) == sub.y_at and there:
                            ln_first(sub, b - k, q)
                        if (g, k) == sub.ln_at and there:
                            ln_second(sub, b - k, q)
                    if g == (3 if sub.qk_norm else 2) and more:
                        prepare(sub, b + 1, 1 - p)
                pipeline(dve, step)

            def experts(sub, key):
                n = sub.index // 3
                dve.wait_ge(rt_ready, n + 1)
                step = Steps(dve, rt_step[n], 0, 50)

                def bc(a, k=8):
                    return a.unsqueeze(2).to_broadcast([T, B, k])
                ps = bank[0][0:T, 0:8 * B].rearrange("p (t e) -> p t e", e=8)
                if n:
                    step(dve.tensor_tensor(lg[:, :, :], ps, f("gate_b", T).unsqueeze(1).to_broadcast([T, B, 8]), ALU.add))
                else:
                    step(dve.tensor_copy(lg[:, :, :], ps))
                for t in range(B):
                    step(dve.max(top[:, t, :], lg[:, t, :]))
                for t in range(B):
                    step(dve.max_index(topi[:, t, :], top[:, t, :], lg[:, t, :]))
                step(dve.tensor_copy(ti[:, :, :], topi[:, :, 0:2]))
                step(dve.tensor_tensor(ex[:, :, 0:8], lg[:, :, :], bc(top[:, :, 0]), ALU.subtract))
                step(dve.tensor_tensor(ex[:, :, 8], top[:, :, 1], top[:, :, 0], ALU.subtract))
                assert step.n == 20
                iota = c("iota", T).unsqueeze(1).to_broadcast([T, B, 8])
                step(dve.tensor_tensor(oh0[:, :, :], iota, bc(ti[:, :, 0]), ALU.is_equal))
                step(dve.tensor_tensor(oh1[:, :, :], iota, bc(ti[:, :, 1]), ALU.is_equal))
                dve.wait_ge(rt_exp, n + 1)
                if n == 0:
                    step(dve.tensor_scalar(gw[:, 0, :], ex[:, :, 8], 1.0, None, ALU.add))
                    step(dve.reciprocal(gw[:, 1, :], gw[:, 0, :]))
                    step(dve.tensor_tensor(gw[:, 2, :], gw[:, 1, :], ex[:, :, 8], ALU.mult))
                else:
                    step(dve.reduce_sum(gw[:, 0, :], ex[:, :, 0:8], AX_X))
                    step(dve.reciprocal(gw[:, 1, :], gw[:, 0, :]))
                    step(dve.tensor_tensor(gw[:, 2, :], gw[:, 1, :], ex[:, :, 8], ALU.mult))
                    step(dve.tensor_tensor(gw[:, 3, :], ti[:, :, 1], ti[:, :, 0], ALU.is_gt))
                    step(dve.tensor_scalar(gw[:, 4, :], gw[:, 2, :], 0.0, None, ALU.is_gt))
                    step(dve.tensor_tensor(gw[:, 3, :], gw[:, 3, :], gw[:, 4, :], ALU.mult))
                    step(dve.tensor_scalar(gw[:, 4, :], gw[:, 3, :], -1.0, 1.0, ALU.mult, ALU.add))
                    step(dve.tensor_tensor(gw[:, 2, :], gw[:, 2, :], gw[:, 3, :], ALU.mult))
                    step(dve.tensor_tensor(gw[:, 1, :], gw[:, 1, :], gw[:, 4, :], ALU.mult))
                    step(dve.tensor_tensor(gw[:, 5, :], gw[:, 1, :], gw[:, 2, :], ALU.add))
                first, second = (gw[:, 1, :], gw[:, 2, :]) if n == 0 else (gw[:, 4, :], gw[:, 3, :])
                step(dve.tensor_tensor(oh0[:, :, :], oh0[:, :, :], bc(first), ALU.mult))
                step(dve.tensor_tensor(oh1[:, :, :], oh1[:, :, :], bc(second), ALU.mult))
                dve.tensor_tensor(wts[:, :, :], oh0[:, :, :], oh1[:, :, :], ALU.add).then_inc(wt_ready, 1)
                dve.wait_ge(wt_ready, n + 1)
                db = START + sub.base["dn"]
                for t in range(B):
                    dve.wait_ge(dn_ready, db + t + 1)
                    dve.tensor_copy(acc[:, t, :], bank[4 + t % 4][0:T, 0:DM]).then_inc(dn_done, 1)
                if n:
                    wait_xres(dve, sub, B - 1)
                    for t in range(B):
                        if t >= 2:
                            dve.wait_ge(xs_T, t - 1)
                        dve.tensor_scalar(xs[:, t % 2, :], x_res[:, t, :], gw[:, 5, t:t + 1], None, ALU.mult).then_inc(xs_ready, 1)

                def one(e0, p):
                    e = e0 + p
                    dve.tensor_copy(wcol[:, p, :], wts[:, :, bass.ds(e, 1)].rearrange("p t o -> p (t o)")).then_inc(col_ready, 1)
                    dve.wait_ge(col_ready, 8 * n + e + 1)
                    for t in range(B):
                        dve.wait_ge(dn_ready, db + 8 + 8 * e + t + 1)
                        dve.wait_ge(dn_done, db + 8 * e + t + 1)
                        dve.scalar_tensor_tensor(out=acc[:, t, :], in0=bank[4 + t % 4][0:T, 0:DM], scalar=wcol[:, p, t:t + 1],
                                                 in1=acc[:, t, :], op0=ALU.mult, op1=ALU.add).then_inc(dn_done, 1)
                with dve.Fori(0, EXPERTS // 2) as pair:
                    e0 = pair * 2
                    one(e0, 0)
                    one(e0, 1)
                dve.wait_ge(dn_done, db + 8 + 8 * EXPERTS)
                with dve.Fori(0, B // 2) as pair:
                    b0 = pair * 2
                    for p in range(2):
                        b = b0 + p
                        wait_xres(dve, sub, b)
                        dve.tensor_tensor(res[:, p, :], acc[:, bass.ds(b, 1), :].rearrange("p o n -> p (o n)"),
                                          x_res[:, bass.ds(b, 1), :].rearrange("p o n -> p (o n)"), ALU.add).then_inc(ln_dve, 1)
                        stats(sub, b, p, 0)
                        rows_out(sub, b, p)

            def quantised(sub):
                step = Steps(dve, rq_step, 0, 9)
                rT_ = f("rhsT").rearrange("p (m d) -> p m d", m=2)
                step(dve.tensor_reduce(qs[:, :, 0], rT_, AX_X, ALU.max))
                step(dve.tensor_reduce(qs[:, :, 1], rT_, AX_X, ALU.min))
                step(dve.tensor_scalar(qs[:, :, 2], qs[:, :, 1], -1.0, None, ALU.mult))
                step(dve.tensor_tensor(qs[:, :, 3], qs[:, :, 0], qs[:, :, 2], ALU.max))
                step(dve.tensor_scalar(qs[:, :, 4], qs[:, :, 3], 1e-12, 1.0 / 127.0, ALU.max, ALU.mult))
                step(dve.reciprocal(qs[:, :, 5], qs[:, :, 4]))
                for m in range(2):
                    dve.tensor_scalar(diag[:, m, :], c("ident"), qs[:, m, 4:5], None, ALU.mult)
                    ins = dve.tensor_scalar(rqf[:, m, :], rT_[:, m, :], qs[:, m, 5:6], MAGIC, ALU.mult, ALU.add)
                step(ins)
                step(dve.tensor_scalar(rqf[:, :, :], rqf[:, :, :], -MAGIC, None, ALU.add))
                step(dve.tensor_scalar(rqf[:, :, :], rqf[:, :, :], 127.0, -127.0, ALU.min, ALU.max))
                dve.wait_ge(rq_done, 2)

                def one(b, p):
                    wait_xres(dve, sub, b)
                    dve.wait_ge(q_T, START + b - 1)
                    step = Steps(dve, q_step, START + 9 * b, 9)
                    xr = x_res[:, bass.ds(b, 1), :].rearrange("p o n -> p (o n)")
                    q = qs[0:T, p, :]
                    apart(dve)
                    step(dve.tensor_reduce(q[:, 0:1], xr, AX_X, ALU.max))
                    apart(dve)
                    step(dve.tensor_reduce(q[:, 1:2], xr, AX_X, ALU.min))
                    step(dve.tensor_scalar(q[:, 2:3], q[:, 1:2], -1.0, None, ALU.mult))
                    step(dve.tensor_tensor(q[:, 3:4], q[:, 0:1], q[:, 2:3], ALU.max))
                    step(dve.tensor_scalar(q[:, 4:5], q[:, 3:4], 1e-12, 1.0 / 127.0, ALU.max, ALU.mult))
                    step(dve.reciprocal(q[:, 5:6], q[:, 4:5]))
                    step(dve.tensor_scalar(qf[:, p, :], xr, q[:, 5:6], MAGIC, ALU.mult, ALU.add))
                    step(dve.tensor_scalar(qf[:, p, :], qf[:, p, :], -MAGIC, None, ALU.add))
                    step(dve.tensor_scalar(qf[:, p, :], qf[:, p, :], 127.0, -127.0, ALU.min, ALU.max))
                    dve.wait_ge(dn_ready, START + sub.base["dn"] + b + 1)
                    dve.scalar_tensor_tensor(out=junk[:, :], in0=bank[4 + p][0:T, 0:DM], scalar=q[:, 4:5], in1=rsb[:, :],
                                             op0=ALU.mult, op1=ALU.mult).then_inc(dn_done, 1)
                    dve.wait_ge(dn_done, START + sub.base["dn"] + b + 1)
                    dve.tensor_tensor(res[:, p, :], junk[:, :], xr, ALU.add).then_inc(ln_dve, 1)
                    stats(sub, b, p, 0)
                    rows_out(sub, b, p)
                with dve.Fori(0, B // 2) as pair:
                    b0 = pair * 2
                    one(b0, 0)
                    one(b0 + 1, 1)

            def glu(sub):
                ub, db = START + sub.base["up"], START + sub.base["dn"]
                for i in range(16):
                    m, u = i // 2, i % 2
                    dve.wait_ge(up_ready, ub + 2 * i + 2)
                    dve.wait_ge(up_done, ub + i + 1)
                    dve.scalar_tensor_tensor(out=hid[:, 0, m, u * HALF:(u + 1) * HALF], in0=bank[2 * (i % 2) + 1][:, 0:HALF],
                                             scalar=f("s2")[:, m:m + 1], in1=tmp[:, i % 4, :], op0=ALU.mult, op1=ALU.mult)\
                        .then_inc(glu_done, 1)
                for b in range(B):
                    p = b % 2
                    wait_xres(dve, sub, b)
                    dve.wait_ge(dn_ready, db + b + 1)
                    dve.tensor_tensor(junk[:, :], bank[4 + b % 4][0:T, 0:DM], f("s3row", T), ALU.mult).then_inc(dn_done, 1)
                    dve.wait_ge(dn_done, db + b + 1)
                    dve.tensor_tensor(res[:, p, :], junk[:, :], x_res[:, b, :], ALU.add).then_inc(ln_dve, 1)
                    stats(sub, b, p, 0)
                    dve.wait_ge(xres_done, at(sub, "row", b, -1))
                    normed(sub, b, p, 0, xln[:, p, :]).then_inc(xln_ready, 1)

            dve.wait_ge(weights_in[0], 16)
            a0 = w(ATTNS[0], "lam", T)
            for i in range(2):
                dve.tensor_tensor_reduce(junk[:, 32 * i:32 * i + 32], a0[:, 64 * i:64 * i + 32], a0[:, 64 * i + 32:64 * i + 64],
                                         1.0, 0.0, ALU.mult, ALU.add, lamt[:, 32 + i:33 + i]).then_inc(lam_step, 1)
            dve.tensor_scalar(gam[:, :], w(ATTNS[0], "gamma", T), 1.0 - LAMBDA_INIT, None, ALU.mult).then_inc(lam_step, 1)
            dve.wait_ge(lam_exp, 1)
            dve.tensor_tensor(lamt[:, 37:38], lamt[:, 35:36], lamt[:, 34:35], ALU.subtract).then_inc(lam_step, 1)
            dve.wait_ge(lam_step, 4)
            dve.tensor_scalar(lamt[:, 38:39], lamt[:, 37:38], -LAMBDA_INIT, None, ALU.add).then_inc(lam_step, 1)
            dve.wait_ge(lam_step, 5)
            for sub in SUBS:
                if isinstance(sub, Attn):
                    attention(sub)
                elif sub.index in (2, 5):
                    experts(sub, None)
                elif sub.index == 8:
                    quantised(sub)
                else:
                    glu(sub)

        @block.gpsimd
        def _(pool):
            for s in (xtb_ready, qblk_ready, xb_ready, ln_pool, xres_done):
                pool.sem_inc(s, START)
            nc.gpsimd.memset(vbuf[:, :, :, :], 0.0).then_inc(v_zero, 1)
            pool.wait_ge(consts_in, 32)

            def start_batch(sub, b, p):
                wait_rows(pool, sub, b)
                pool.wait_ge(proj_ready, at(sub, "proj", b - 1, 0))
                apart(pool)
                nc.gpsimd.tensor_copy(xTb[:, p, :, :], xT[:, :, bass.ds(b * T, T)]).then_inc(xtb_ready, 1)

            def squares(sub, b, p):
                for s, src in enumerate((qT, kT)):
                    pool.wait_ge(proj_done, at(sub, "proj", b, s + 1))
                    nc.gpsimd.tensor_tensor(rT[:, p, s, :, :], src[:, p, 0:2, :], src[:, p, 0:2, :], ALU.mult)\
                        .then_inc(sq_ready, 1)

            def spread(sub, b, p):
                if sub.feats:
                    pool.wait_ge(feat_ready, 4 * b + 2)
                    src = fq[:, p, :, :]
                elif sub.rope:
                    pool.wait_ge(rot_step, 6 * b + 3)
                    src = qT[:, p, 0:2, :]
                else:
                    pool.wait_ge(proj_done, at(sub, "proj", b, 1))
                    src = qT[:, p, 0:sub.chunks, :]
                pool.wait_ge(head_ready, START + HEADS * (B * sub.order + b - 1))
                n, k = sub.chunks, sub.hpc
                for m in range(n):
                    ins = nc.gpsimd.tensor_tensor(qblk[:, p, k * m:k * m + k, :],
                                                  src[:, m, :].unsqueeze(1).to_broadcast([128, k, T]),
                                                  w(sub, "headmask").unsqueeze(2).to_broadcast([128, k, T]), ALU.mult)
                ins.then_inc(qblk_ready, 1)

            def residual(sub, b, p):
                pool.wait_ge(ln_dve, START + 3 * ln_unit(sub, b - 2) + 1)
                if sub.qk_norm:
                    pool.wait_ge(proj_done, at(sub, "proj", b, 2))
                    nc.gpsimd.tensor_tensor(qrow[:, p, 1, :], qrow[:, p, 0, :], w(sub, "bqrow", T), ALU.add).then_inc(qrow_ready, 1)
                    pool.wait_ge(qrow_ready, b + 1)
                    nc.gpsimd.tensor_tensor(xb[:, p, :], qrow[:, p, 1, :], w(sub, "bo", T), ALU.add).then_inc(xb_ready, 1)
                    pool.wait_ge(qn_step, START + 4 * b + 1)
                    nc.gpsimd.tensor_tensor(qn[:, p, 1:2], qn[:, p, 0:1], c("plus_half", T)[:, 0:1], ALU.pow).then_inc(qn_root, 1)
                else:
                    wait_xres(pool, sub, b)
                    nc.gpsimd.tensor_tensor(xb[:, p, :], x_res[:, bass.ds(b, 1), :].rearrange("p o n -> p (o n)"),
                                            w(sub, "bo", T), ALU.add).then_inc(xb_ready, 1)

            def ln_root(sub, b, p, unit):
                u = sub.base["ln"] + int(sub.per["ln"]) * b + unit
                pool.wait_ge(ln_dve, START + 3 * u + 3)
                nc.gpsimd.tensor_tensor(mv[:, p, 2:3], mv[:, p, 1:2], c("eps", T), ALU.add).then_inc(ln_pool, 1)
                pool.wait_ge(ln_pool, START + 2 * u + 1)
                nc.gpsimd.tensor_tensor(mv[:, p, 3:4], mv[:, p, 2:3], c("minus_half", T)[:, 0:1], ALU.pow).then_inc(ln_pool, 1)

            def o_root(sub, b, p):
                pool.wait_ge(o_step, 7 * b + 3)
                apart(pool)
                nc.gpsimd.tensor_scalar(rms[:, p, 1, :], rms[:, p, 0, :], 1.0 / 64, None, ALU.mult).then_inc(o_pool, 1)
                pool.wait_ge(o_pool, 2 * b + 1)
                nc.gpsimd.tensor_tensor(rms[:, p, 2, :], rms[:, p, 1, :], c("plus_half", T), ALU.pow).then_inc(o_pool, 1)

            def keep_rows(sub, b, p):
                pool.wait_ge(xln_ready, at(sub, "row", b, 1))
                apart(pool)
                nc.gpsimd.tensor_copy(x_res[:, bass.ds(b, 1), :].rearrange("p o n -> p (o n)"), xln[:, p, :])\
                    .then_inc(xres_done, 1)

            def attention(sub):
                pool.wait_ge(weights_in[sub.order], 16)
                if sub.order:
                    pool.wait_ge(proj_ready, at(ATTNS[sub.order - 1], "proj", B, 0))
                if sub.index and isinstance(SUBS[sub.index - 1], Ffn):
                    wait_rows(pool, sub, B - 1)

                start_batch(sub, 0, 0)
                if sub.feats:
                    squares(sub, 0, 0)
                spread(sub, 0, 0)
                if sub.qk_norm:
                    residual(sub, 0, 0)
                late = sub.rope or sub.feats

                def step(b, g, p, back, more, tail, far):
                    if g == 0 and more:
                        start_batch(sub, b + 1, 1 - p)
                    if g == 1 and back[0] and not sub.qk_norm:
                        residual(sub, b, p)
                    if g == 2 and tail and sub.diff:
                        o_root(sub, b - 1, 1 - p)
                    if g == 2 and more and sub.feats:
                        squares(sub, b + 1, 1 - p)
                    if g == 2 and more and not late:
                        spread(sub, b + 1, 1 - p)
                    if g == 3 and more and late:
                        spread(sub, b + 1, 1 - p)
                    for k, there, q in ((1, tail, 1 - p), (2, far, p)):
                        if (g, k) == sub.y_at and there:
                            ln_root(sub, b - k, q, 0)
                        if (g, k) == sub.ln_at and there:
                            if sub.qk_norm:
                                ln_root(sub, b - k, q, 1)
                            keep_rows(sub, b - k, q)
                    if g == 3 and more and sub.qk_norm:
                        residual(sub, b + 1, 1 - p)
                pipeline(pool, step)

            def feed_forward(sub):
                with pool.Fori(0, B // 2) as pair:
                    b0 = pair * 2
                    for p in range(2):
                        ln_root(sub, b0 + p, p, 0)
                        keep_rows(sub, b0 + p, p)

            for sub in SUBS:
                if isinstance(sub, Attn):
                    attention(sub)
                else:
                    feed_forward(sub)


def _columns_of(vector, rows=128):
    return np.ascontiguousarray(vector.reshape(-1, rows).T)


def _chunks(weight, rows=128):
    k, n = weight.shape[0] // rows, weight.shape[1]
    out = np.zeros((128, k * n), np.float32)
    out[:rows] = weight.reshape(k, rows, n).transpose(1, 0, 2).reshape(rows, k * n)
    return out


def _strips(weight):
    n = weight.shape[1]
    out = np.zeros((4, 32, 4, n), np.float32)
    out[:, 0:16] = weight.reshape(4, 4, 16, n).transpose(1, 2, 0, 3)
    return out.reshape(128, 4 * n)


def _pack(sub, parts):
    out = np.zeros((128, sub.cols), np.float32)
    r = np.arange(128)
    parts["headmask"] = (r[:, None] // (128 // sub.hpc) == np.arange(sub.hpc)[None, :]).astype(np.float32)
    for key, a in parts.items():
        at, n = sub.at[key]
        if a.ndim == 1:
            a = np.broadcast_to(a, (128, a.shape[0]))
        out[:a.shape[0], at:at + a.shape[1]] = a
    return out


def _rope_tables():
    i = np.arange(T)
    inv = (1.0 / 10000.0 ** (np.arange(2, dtype=np.float32) / np.float32(2.0))).astype(np.float32)
    cos, sin = np.ones((16, T), np.float32), np.zeros((16, T), np.float32)
    frame = i // 256
    rest = i - 256 * frame
    for s, pos in enumerate((frame, rest // 16, rest - 16 * (rest // 16))):
        for d in range(4):
            freq = (pos.astype(np.float32) * inv[d % 2]).astype(np.float32)
            cos[4 * s + d], sin[4 * s + d] = np.cos(freq), np.sin(freq)
    rot = np.zeros((128, 128), np.float32)
    for k in range(0, 128, 2):
        rot[k + 1, k], rot[k, k + 1] = -1.0, 1.0
    return np.tile(cos, (8, 1)), np.tile(sin, (8, 1)), rot


def kernel(**inputs):
    import concourse.bacc as bacc
    from concourse.bass_utils import run_bass_kernel_spmd

    a = {k: np.asarray(v) for k, v in inputs.items()}

    consts = np.zeros((128, CONST_COLS), np.float32)
    for key, value in (("ident", np.eye(128)), ("iota", np.broadcast_to(np.arange(8), (128, 8))),
                       ("causal", np.tril(np.ones((128, 128)))[:, 0:T]), ("ones", np.ones((128, T))),
                       ("eps", np.full((128, 1), LN_EPS)),
                       ("minus_half", np.full((128, 8), -0.5)), ("plus_half", np.full((128, 8), 0.5))):
        at, n = CONST_AT[key]
        consts[:, at:at + n] = value

    ffn_small = np.zeros((128, FFN_COLS), np.float32)

    def put(key, value):
        at, n = FFN_AT[key]
        ffn_small[:value.shape[0], at:at + n] = value

    put("L0_router", _chunks(a["L0_ffn_w_router"].T))
    put("L0_bup", _columns_of(a["L0_ffn_b_up"].reshape(-1)))
    put("L0_bdown", a["L0_ffn_b_down"])
    put("L1_router", _chunks(a["L1_ffn_gate_w"]))
    put("gate_b", np.broadcast_to(a["L1_ffn_gate_b"], (128, 8)))
    put("L1_b1", _columns_of(a["L1_ffn_b1"].reshape(-1)))
    put("L1_b2", a["L1_ffn_b2"])
    put("rhsT", _chunks(a["L2_ffn_rhs"].T))
    for key, name in (("s1", "w1_s"), ("s2", "w2_s"), ("sh1", "h1_s"), ("sh2", "h2_s")):
        put(key, _columns_of(a["L3_ffn_" + name]))
    put("s3row", np.broadcast_to(a["L3_ffn_w3_s"], (128, DM)))

    def qkv(sub, wq, wk, wv):
        rows = KC if sub.ctx else 128
        return {"wq": _chunks(wq), "wk": _chunks(wk, rows), "wv": _chunks(wv, rows)}

    def biases(name):
        return {"bq": _columns_of(a[name + "_bq"]), "bk": _columns_of(a[name + "_bk"]),
                "bvT": _strips(a[name + "_bv"].reshape(-1, 1))}

    cos, sin, rot = _rope_tables()
    rf, ones2 = np.zeros((4, 128, 128), np.float32), np.zeros((4, 128, 128), np.float32)
    for u in range(4):
        for i in range(2):
            h = 2 * u + i
            rf[u, 16 * h:16 * h + 16, 64 * i:64 * i + 64] = a["L3_attn_random_features"].T
            ones2[u, 16 * h:16 * h + 16, 64 * i:64 * i + 64] = 1.0
    side_by_side = lambda t: t.transpose(1, 0, 2).reshape(128, -1)
    s = {x.name: x for x in ATTNS}
    w_kv, w_qkv = a["L0_attn_Wkv"], a["L3_attn_w_qkv"].T
    parts = {
        "L0_attn": {**qkv(s["L0_attn"], a["L0_attn_Wq"], w_kv[:, :512], w_kv[:, 512:]), "wo": _chunks(a["L0_attn_Wout"]),
                    "lam": np.concatenate([a["L0_attn_lambda_" + k] for k in ("q1", "k1", "q2", "k2")]),
                    "gamma": a["L0_attn_gamma"]},
        "L0_xattn": {**qkv(s["L0_xattn"], a["L0_xattn_Wq"], a["L0_xattn_Wk"], a["L0_xattn_Wv"]), **biases("L0_xattn"),
                     "wo": _strips(a["L0_xattn_Wo"]), "bo": a["L0_xattn_bo"]},
        "L1_attn": {**qkv(s["L1_attn"], a["L1_attn_Wq"], a["L1_attn_Wk"], a["L1_attn_Wv"]), **biases("L1_attn"),
                    "wo": _strips(a["L1_attn_Wo"]), "bo": a["L1_attn_bo"], "cos": cos, "sin": sin, "rot": rot},
        "L1_xattn": {**qkv(s["L1_xattn"], a["L1_xattn_Wq"], a["L1_xattn_Wk"], a["L1_xattn_Wv"]),
                     "wo": _strips(a["L1_xattn_Wo"])},
        "L2_attn": {**qkv(s["L2_attn"], a["L2_attn_Wq"].T, a["L2_attn_Wk"].T, a["L2_attn_Wv"].T), **biases("L2_attn"),
                    "wo": _strips(a["L2_attn_Wo"].T), "bo": a["L2_attn_bo"]},
        "L2_xattn": {**qkv(s["L2_xattn"], a["L2_xattn_Wq"], a["L2_xattn_Wk"], a["L2_xattn_Wv"]), **biases("L2_xattn"),
                     "wo": _strips(a["L2_xattn_Wo"]), "bo": a["L2_xattn_bo"], "bqrow": a["L2_xattn_bq"],
                     "ln_g": a["L2_xattn_ln_gamma"], "ln_b": a["L2_xattn_ln_beta"]},
        "L3_attn": {**qkv(s["L3_attn"], w_qkv[:, :256], w_qkv[:, 256:512], w_qkv[:, 512:]),
                    "wo": _strips(a["L3_attn_w_out"].T), "bo": a["L3_attn_b_out"],
                    "rf": side_by_side(rf), "ones2": side_by_side(ones2)},
        "L3_xattn": {**qkv(s["L3_xattn"], a["L3_xattn_Wq"], a["L3_xattn_Wk"], a["L3_xattn_Wv"]), **biases("L3_xattn"),
                     "b1": _columns_of(a["L3_xattn_b1"]), "bo": a["L3_xattn_b2"]},
    }
    packs = [_pack(x, parts[x.name]) for x in ATTNS]

    ring = np.zeros((RING_ALL, 128, RCOLS), np.float32)
    for e in range(EXPERTS):
        ring[RING_L0 + 2 * e] = _chunks(a["L0_ffn_w_up"][e].T)
        ring[RING_L0 + 2 * e + 1] = _chunks(a["L0_ffn_w_down"][e].T)
        ring[RING_L1 + 2 * e] = _chunks(a["L1_ffn_w1"][e])
        ring[RING_L1 + 2 * e + 1] = _chunks(a["L1_ffn_w2"][e])
    ring[RING_X] = _strips(a["L3_xattn_W1"])
    ring[RING_X + 1, :, 0:4 * DM] = _chunks(a["L3_xattn_W2"])
    ring[RING_GLU], ring[RING_GLU + 1] = _chunks(a["L3_ffn_w1_w"].T), _chunks(a["L3_ffn_w2_w"].T)
    for j in range(4):
        ring[RING_H1 + j] = _chunks(a["L3_ffn_h1_w"].T[:, 256 * j:256 * j + 256])
        ring[RING_H2 + j] = _chunks(a["L3_ffn_h2_w"].T[:, 256 * j:256 * j + 256])
    ring[RING_W3] = _chunks(a["L3_ffn_w3_w"].T)

    arrays = {"ctxT": np.ascontiguousarray(a["ctx_768"].reshape(B, S2, 2, KC).transpose(0, 3, 2, 1)),
              "mask": a["mask_BxS2_bf1"], "x": a["x"], "consts": consts, "ffn_small": ffn_small, "ring": ring}
    arrays.update({f"pack{i}": p for i, p in enumerate(packs)})

    nc = bacc.Bacc("TRN2", target_bir_lowering=False, num_devices=1)
    dram = {k: nc.dram_tensor("in_" + k, v.shape, mybir.dt.from_np(v.dtype), kind="ExternalInput").ap()
            for k, v in arrays.items()}
    out = nc.dram_tensor("out", (B, T, DM), F32, kind="ExternalOutput").ap()
    decoder(nc, dram["ctxT"], dram["mask"], dram["x"], dram["consts"], dram["ffn_small"],
            [dram[f"pack{i}"] for i in range(len(packs))], dram["ring"], out)
    r = run_bass_kernel_spmd(nc, [{"in_" + k: v for k, v in arrays.items()}], core_ids=[0])
    return r.results[0]["out"]
```

```python
import math
from contextlib import ExitStack

import numpy as np
import concourse.bass as bass
from concourse import mybir

F32 = mybir.dt.float32
BF16 = mybir.dt.bfloat16
F32R = mybir.dt.float32r
U32 = mybir.dt.uint32
U8 = mybir.dt.uint8
ALU = mybir.AluOpType
ACT = mybir.ActivationFunctionType
AX_X = mybir.AxisListType.X

B, T, DM = 8, 112, 256
S2, KC, KT = 375, 96, 125
HEADS, GROUPS = 16, 4
EXPERTS, HID, HALF = 8, 1024, 448
START = 64
LN_EPS = 1e-5
LAMBDA_INIT = 0.8 - 0.6 * math.exp(-0.3 * 1)
CLAMP = 10000.0
BIG = float(2.0 ** 126)
LOWEST = -3.0e38
MAGIC = float(1.5 * 2 ** 23)


class Attn:

    def __init__(self, name, ctx=False, chunks=2, heads_per_chunk=8, scale=0.25, kind="softmax",
                 clip=False, mask=False, qk_norm=False, diff=False, rope=False, feats=False, mlp=False):
        self.name, self.ctx, self.chunks, self.hpc = name, ctx, chunks, heads_per_chunk
        self.scale, self.kind, self.clip, self.mask, self.qk_norm = scale, kind, clip, mask, qk_norm
        self.diff, self.rope, self.feats, self.mlp = diff, rope, feats, mlp
        self.keys = S2 if ctx else T
        self.tiles = 3 if ctx else 1
        self.rows = KT if ctx else T
        self.kdim = KC if ctx else 128
        self.qc = 512 if diff else 256
        self.items = ["q"] + ([] if ctx else ["k"]) + (["qrow"] if qk_norm else [])
        if rope:
            self.items += ["rq", "rk"]
        if feats:
            self.items += [f"{what}{s}{m}" for s in "qk" for m in range(2) for what in ("n", "p")]
        first_v = len(self.items)
        self.items += [f"v{t}" for t in range(self.tiles)]
        self.lag = 2
        self.out_at = (self.lag, 1)
        self.y_at = (0, 2) if diff else (self.lag + 1, 1)
        self.ln_at = (1, 2) if diff else (0, 2)
        self.rows_at = (2, 2) if diff else (1, 2)
        if feats:
            self.when = {(0, 3): [0, 1], (1, 3): list(range(2, first_v)), (2, 3): [first_v]}
        elif rope:
            self.when = {(1, 3): [0, 1], (2, 3): list(range(2, len(self.items)))}
        elif diff:
            self.when = {(2, 3): [0, 1, 2]}
        else:
            self.when = {(1, 3): [0, 1], (2, 3): [first_v]}
        self.prepare_at = 1 if feats else 3 if qk_norm else 2
        self.spread_at = 3 if rope or feats else 2
        if ctx:
            self.when = {(2, i): [i] for i in range(first_v)}
            self.when.update({(3, i): [first_v + i] for i in range(3)})
        dve_frees = kind != "softmax" or clip or mask or qk_norm
        self.dve_frees = dve_frees
        self.per = {"proj": len(self.items), "head": HEADS if kind == "softmax" else 0,
                    "dhead": HEADS if dve_frees else 0, "group": GROUPS, "pt": GROUPS * self.tiles,
                    "rsum": GROUPS if kind != "softmax" else 0,
                    "batch": 1, "ln": 2 if qk_norm else 1, "row": 1, "kprep": 2 if ctx else 0,
                    "inv": GROUPS * (2 if diff or kind == "linear" else 1)}
        cols = [("wq", 2 * self.qc), ("wk", 2 * self.qc), ("wv", 2 * self.qc), ("headmask", heads_per_chunk),
                ("bq", 4), ("bk", 4), ("bvT", 4), ("bo", DM)]
        cols += [("b1", 4)] if mlp else [("wo", 4 * DM)]
        if diff:
            cols += [("lam", 4 * 32), ("gamma", 64)]
        if qk_norm:
            cols += [("bqrow", DM), ("ln_g", DM), ("ln_b", DM)]
        if rope:
            cols += [("rot", 128), ("cos", T), ("sin", T)]
        if feats:
            cols += [("rf", 4 * 128), ("ones2", 4 * 128)]
        self.at, n = {}, 0
        for key, width in cols:
            self.at[key] = (n, width)
            n += width
        self.cols = n


class Ffn:

    def __init__(self, name, dn, up=0):
        self.name = name
        self.per = {"ln": 1, "row": 1, "dn": dn / B, "up": up / B}


SUBS = [
    Attn("L0_attn", chunks=4, heads_per_chunk=4, scale=32 ** -0.5, diff=True),
    Attn("L0_xattn", ctx=True, clip=True),
    Ffn("L0_ffn", dn=8 + 8 * EXPERTS, up=16 * EXPERTS),
    Attn("L1_attn", rope=True),
    Attn("L1_xattn", ctx=True, mask=True),
    Ffn("L1_ffn", dn=8 + 8 * EXPERTS, up=16 * EXPERTS),
    Attn("L2_attn", kind="causal"),
    Attn("L2_xattn", ctx=True, qk_norm=True),
    Ffn("L2_ffn", dn=8),
    Attn("L3_attn", kind="linear", chunks=8, heads_per_chunk=2, feats=True),
    Attn("L3_xattn", ctx=True, mlp=True),
    Ffn("L3_ffn", dn=8, up=2 * 16),
]
UNITS = ("rsum", "proj", "head", "dhead", "group", "pt", "batch", "ln", "row", "kprep", "inv", "dn", "up")
for _i, _s in enumerate(SUBS):
    _s.index = _i
    _s.base = {u: int(sum(a.per.get(u, 0) * B for a in SUBS[:_i])) for u in UNITS}
ATTNS = [s for s in SUBS if isinstance(s, Attn)]
for _i, _s in enumerate(ATTNS):
    _s.slot = _i % 2
    _s.order = _i
    _s.ctx_before = sum(a.ctx for a in ATTNS[:_i])
SLOT_COLS = [max(a.cols for a in ATTNS if a.slot == s) for s in range(2)]

RSLOTS, RCOLS = 4, 2048
PIECE = RCOLS // 2
GLU_ITEMS = 11
RING_L0, RING_L1, RING_X, RING_GLU, RING_H1, RING_H2, RING_W3, RING_ALL = 0, 16, 32, 34, 36, 40, 44, 45


def columns(*parts):
    where, n = {}, 0
    for key, width in parts:
        where[key] = (n, width)
        n += width
    return where, n


CONST_AT, CONST_COLS = columns(("ident", 128), ("iota", 8), ("causal", T), ("ones", T),
                               ("eps", 1), ("minus_half", 8), ("plus_half", 8))
FFN_AT, FFN_COLS = columns(("L0_router", 16), ("L0_bup", 64), ("L0_bdown", DM), ("L1_router", 16), ("gate_b", 8),
                           ("L1_b1", 64), ("L1_b2", DM), ("rhsT", 2 * DM), ("s1", 8), ("s2", 8), ("sh1", 8),
                           ("sh2", 8), ("s3row", DM))


class Steps:

    def __init__(self, eng, sem, base, length):
        self.eng, self.sem, self.base, self.length, self.n = eng, sem, base, length, 0

    def __call__(self, instruction):
        self.n += 1
        assert self.n <= self.length
        instruction.then_inc(self.sem, 1)
        self.eng.wait_ge(self.sem, self.base + self.n)


def decoder(nc, ctxT, mask, x, consts, ffn_small, packs, ring_dram, out):
    ctx = ExitStack()
    with ctx:
        def sb(name, shape, dt=F32):
            return ctx.enter_context(nc.sbuf_tensor(name, shape, dt))

        def sem(name):
            return ctx.enter_context(nc.semaphore(name))

        cst = sb("cst", [128, CONST_COLS])
        ffs = sb("ffs", [128, FFN_COLS])
        wat = [sb(f"wat{s}", [128, SLOT_COLS[s]]) for s in range(2)]
        x_res = sb("x_res", [T, B, DM])
        xT = sb("xT", [128, 2, B * T])
        vspace = sb("vspace", [128, 6 * HEADS * 32])
        vbuf = vspace[0:KT, :].rearrange("p (a t n) -> p a t n", a=2, t=3)
        landing = vspace[:, 0:2 * PIECE].rearrange("p (s n) -> p s n", s=2)
        xb = sb("xb", [T, 2, DM])
        res = sb("res", [T, 2, DM])
        xln = sb("xln", [T, 2, DM])
        st = sb("st", [T, 2, 6])
        mv = sb("mv", [T, 2, 4])
        xTb = sb("xTb", [128, 2, 2, T])

        def carve(arena, name):
            at = [0]

            def take(rows, *dims):
                n = int(np.prod(dims))
                a = arena[0:rows, at[0]:at[0] + n]
                at[0] += n
                assert at[0] <= arena.shape[1], (name, at[0])
                if len(dims) == 1:
                    return a
                names = "abcd"[:len(dims)]
                sizes = {k: v for k, v in zip(names, dims)}
                return a.rearrange(f"p ({' '.join(names)}) -> p {' '.join(names)}", **sizes)
            return take

        junk = sb("junk", [T, DM])

        ctxb = sb("ctxb", [KC, 2, 2, S2])
        maskb = sb("maskb", [T, 2, S2], U8)
        mx = sb("mx", [T, 2, HEADS])
        nm = sb("nm", [T, 2, HEADS])
        ls = sb("ls", [T, 2, HEADS])
        rv = sb("rv", [T, 2, HEADS])
        lamt = sb("lamt", [T, 40])
        gam = sb("gam", [T, 64])
        rms = sb("rms", [T, 2, 5, 8])
        qn = sb("qn", [T, 2, 5])

        with ExitStack() as turn:
            def shared(name, shape, dt=F32):
                return turn.enter_context(nc.sbuf_tensor(name, shape, dt))

            mlpw = shared("mlpw", [128, 2, RCOLS])
            big = shared("big", [128, 14336])
            take = carve(big, "big attention")
            kall = take(128, 2, B * S2)
            rowb = take(T, B, S2)
            pts = take(KT, 2, 3, 4 * T)
            rowf = take(T, 2, S2)
            qsq = take(128, 2, S2)
            qrow = take(T, 2, 2, DM)
            take = carve(big, "big features")
            fq = take(128, 2, 8, T)
            fk = take(128, 2, 8, T)
            nT = take(128, 4, 4 * T)
            pj = take(128, 4, 4 * T)
            rT = take(128, 2, 2, 2, T)
            kT = take(128, 2, 4, T)
            take = carve(big, "big hidden")
            take(128, 2 * B * S2)
            hT = take(128, 2, 4, T)
            arena = shared("arena", [128, 12950])
            take = carve(arena, "arena attention")
            qT = take(128, 2, 4, T)
            qblk = take(128, 2, HEADS, T)
            pr = take(T, 4, 4, S2)
            sc = take(T, 4, S2)
            oT = take(128, 2, 4, T)
            take = carve(big, "big differential")
            take(128, 6000)
            take(T, 3000 + 2688)
            vd = take(T, 2, 512)
            wd = take(T, 2, 2, T)
            take2 = carve(big, "big differential 2")
            on = take2(T, 2, 512)
            osq = take2(T, 512)
        with ExitStack() as turn:
            def shared(name, shape, dt=F32):
                return turn.enter_context(nc.sbuf_tensor(name, shape, dt))

            wsplit = shared("wsplit", [128, RSLOTS, RCOLS], F32R)
            hid = shared("hid", [128, 2, 2, 8, HALF], F32R)
            xsplit = shared("xsplit", [128, 2, 2, B * T], F32R)
            scratch = shared("scratch", [128, 5616])
            take = carve(scratch, "feed-forward")
            acc = take(T, B, DM)
            tmp = take(128, 4, HALF)
            lg = take(T, B, 8)
            top = take(T, B, 8)
            topx = take(T, B, 8)
            topi = topx.bitcast(U32)
            ti = take(T, B, 2)
            oh0, oh1 = take(T, B, 8), take(T, B, 8)
            wts = take(T, B, 8)
            ex = take(T, B, 9)
            gw = take(T, 6, B)
            wtT = take(8, B * T)
            wcol = take(T, 2, B)
            bup = take(128, 2, 8)
            xs = tmp[0:T, 0:2, 0:DM]
            take = carve(scratch, "quantised")
            qf = take(T, 2, DM)
            rqf = take(128, 2, DM)
            diag = take(128, 2, 128)
            rsb = take(T, DM)
            qs = take(128, 2, 8)
            qbT = take(128, 2 * T).bitcast(BF16).rearrange("p (a b c) -> p a b c", a=2, b=2)
            rqT = take(128, DM).bitcast(BF16).rearrange("p (a b) -> p a b", a=2)

        bank = [ctx.enter_context(nc.psum_tensor(f"bank{i}", [128, 512], F32)) for i in range(8)]
        OT, TL = bank[6], bank[7]

        def proj_bank(sub, p, i):
            return bank[(p * len(sub.items) + i) % 2]

        def score_bank(sub, g, j):
            return bank[2 + (j if sub.ctx else g) % 2]

        def pt_bank(sub, n):
            return bank[4 + n % 2]

        def c(key, rows=128):
            a, n = CONST_AT[key]
            return cst[0:rows, a:a + n]

        def f(key, rows=128):
            a, n = FFN_AT[key]
            return ffs[0:rows, a:a + n]

        def w(sub, key, rows=128):
            a, n = sub.at[key]
            return wat[sub.slot][0:rows, a:a + n]

        consts_in, x_in, ffn_small_in = sem("consts_in"), sem("x_in"), sem("ffn_small_in")
        mask_in = [sem("mask_in0"), sem("mask_in1")]
        weights_in = [sem(f"weights_in_{a.name}") for a in ATTNS]
        mlp_in = sem("mlp_in")
        land_in = [sem(f"land_in{i}") for i in range(2)]
        ctx_in = [sem("ctx_in0"), sem("ctx_in1")]
        out_done = sem("out_done")
        passed = {e.engine: sem(f"passed_{n}") for n, e in (("sp", nc.sync), ("dve", nc.vector), ("pool", nc.gpsimd))}
        proj_ready, proj_done = sem("proj_ready"), sem("proj_done")
        kprep_ready, kprep_done = sem("kprep_ready"), sem("kprep_done")
        knorm_ready, knorm_done = sem("knorm_ready"), sem("knorm_done")
        row_step, row_ready = sem("row_step"), sem("row_ready")
        rowf_ready = sem("rowf_ready")
        xtb_ready = sem("xtb_ready")
        qblk_ready = sem("qblk_ready")
        rot_step = sem("rot_step")
        sq_ready = sem("sq_ready")
        fsub_ready, feat_ready = sem("fsub_ready"), sem("feat_ready")
        qrow_ready = sem("qrow_ready")
        qn_step, qn_root = sem("qn_step"), sem("qn_root")
        head_ready = sem("head_ready")
        dhead_done = sem("dhead_done")
        max_ready = sem("max_ready")
        exp_done = sem("exp_done")
        rsum_done = sem("rsum_done")
        inv_step, wd_step = sem("inv_step"), sem("wd_step")
        norm_done = sem("norm_done")
        t_ready, t_done = sem("t_ready"), sem("t_done")
        pv_done = sem("pv_done")
        o_step, o_pool = sem("o_step"), sem("o_pool")
        onT_ready = sem("onT_ready")
        ot_done = sem("ot_done")
        hid_ready, hid_done = sem("hid_ready"), sem("hid_done")
        y_ready = sem("y_ready")
        xb_ready = sem("xb_ready")
        ln_dve, ln_pool = sem("ln_dve"), sem("ln_pool")
        ln_in = sem("ln_in")
        xln_ready, xres_done = sem("xln_ready"), sem("xres_done")
        xt_ready, xt_done = sem("xt_ready"), sem("xt_done")
        lam_step, lam_exp = sem("lam_step"), sem("lam_exp")
        v_zero = sem("v_zero")
        rt_ready, rt_step, rt_exp = sem("rt_ready"), [sem("rt_step0"), sem("rt_step1")], sem("rt_exp")
        wt_ready, wt_T, wt_done = sem("wt_ready"), sem("wt_T"), sem("wt_done")
        xs_ready, xs_T, xs_done = sem("xs_ready"), sem("xs_T"), sem("xs_done")
        up_ready, up_done = sem("up_ready"), sem("up_done")
        dn_ready, dn_done = sem("dn_ready"), sem("dn_done")
        col_ready, bup_ready = sem("col_ready"), sem("bup_ready")
        glu_done = sem("glu_done")
        w_high, w_split = sem("w_high"), sem("w_split")
        h_high, h_split = sem("h_high"), sem("h_split")
        x_high, x_split = sem("x_high"), sem("x_split")
        rq_step, rq_T, rq_done = sem("rq_step"), sem("rq_T"), sem("rq_done")
        q_step, q_T, q_done = sem("q_step"), sem("q_T"), sem("q_done")

        block = ctx.enter_context(nc.Block())

        def at(sub, unit, b, k):
            return START + sub.base[unit] + int(sub.per[unit]) * b + k

        def xt_at(sub, b):
            return START + B + sub.base["row"] + b + 1

        def ln_unit(sub, b):
            if isinstance(b, int) and b < 0 and sub.index:
                sub, b = SUBS[sub.index - 1], B + b
            return sub.base["ln"] + int(sub.per["ln"]) * b

        def wait_rows(eng, sub, b):
            eng.wait_ge(xt_done, START + sub.base["row"] + b + 1)

        def wait_xres(eng, sub, b):
            if sub.index == 0:
                eng.wait_ge(x_in, 16)
            else:
                eng.wait_ge(xres_done, START + sub.base["row"] + b + 1 - B)

        def apart(eng):
            eng.sem_inc(passed[eng.engine], 1)

        def sem_heads_free(eng, sub, b, k):
            if sub.dve_frees:
                eng.wait_ge(dhead_done, at(sub, "dhead", b, k))
            else:
                eng.wait_ge(exp_done, at(sub, "head", b, k))

        def pairs(eng, body):
            body(0, True)
            with eng.Fori(1, B // 2) as pair:
                b0 = pair * 2
                body(b0, False)

        def pipeline(eng, step):
            def run(b0, first, last, count=8):
                for s in range(count):
                    b, g, p = b0 + s // 4, s % 4, s // 4
                    back = [None] * 4
                    for k in range(4):
                        if not (first and s < k) and not (isinstance(b0, int) and 4 * b0 + s - k >= 4 * B):
                            back[k] = (b0 + (s - k) // 4, (s - k) % 4, (s - k) // 4 % 2)
                    step(b, g, p, back, more=not (last and p == 1) and count == 8,
                         tail=not (first and p == 0) and not (count < 8 and p == 1), far=not first)
            run(0, True, False)
            with eng.Fori(1, B // 2 - 1) as pair:
                run(pair * 2, False, False)
            run(B - 2, False, True)
            run(B, False, True, 7)

        @block.sync
        def _(sp):
            sp.dma_start(cst[:, :], consts).then_inc(consts_in, 16)
            sp.dma_start(x_res[:, :, :], x.rearrange("b t d -> t b d")).then_inc(x_in, 16)
            sp.dma_start(wat[0][:, 0:ATTNS[0].cols], packs[0]).then_inc(weights_in[0], 16)
            sp.dma_start(wat[1][:, 0:ATTNS[1].cols], packs[1]).then_inc(weights_in[1], 16)
            sp.dma_start(ffs[:, :], ffn_small).then_inc(ffn_small_in, 16)

            def pieces(sub, first, items):
                attn = ATTNS[{2: 1, 5: 3, 11: 7}[sub.index]]
                sp.wait_ge(pv_done, at(attn, "group", B - 1, GROUPS))
                for i, item in enumerate(items):
                    for half in range(2):
                        j = first + 2 * i + half
                        sp.wait_ge(w_split, START + j - 1)
                        sp.dma_start(landing[:, half, :], ring_dram[item, :, half * PIECE:(half + 1) * PIECE])\
                            .then_inc(land_in[half], 16)

            def context(sub, second):
                before = ATTNS[:sub.order]
                last = [a for a in before if a.ctx]

                def load(b, p, first):
                    if first and not second and last:
                        sp.wait_ge(proj_ready, at(last[-1], "proj", B - 1, int(last[-1].per["proj"])))
                    elif first and not second:
                        pass
                    elif first:
                        sp.wait_ge(kprep_ready, at(sub, "kprep", B - 2 + p, 2))
                    elif not second:
                        sp.wait_ge(kprep_ready, at(sub, "kprep", b - 2, 2))
                    else:
                        sp.wait_ge(proj_ready, at(sub, "proj", b - 1, 0))
                    apart(sp)
                    if sub.mask and not second and not first:
                        sp.wait_ge(row_ready, b - 1)
                        apart(sp)
                    if sub.mask and not second:
                        sp.dma_start(maskb[:, p, :], mask[bass.ds(b, 1), :].to_broadcast([T, S2])).then_inc(mask_in[p], 16)
                    sp.dma_start(ctxb[:, p, :, :], ctxT[bass.ds(b, 1), :, :, :].rearrange("o k c n -> (o k) c n"))\
                        .then_inc(ctx_in[p], 16)

                def body(b0, first):
                    load(b0, 0, first)
                    load(b0 + 1, 1, first)
                pairs(sp, body)

            def next_weights(sub):
                if sub.order + 2 < len(ATTNS):
                    sp.wait_ge(xt_ready, xt_at(sub, B - 1))
                    nxt = ATTNS[sub.order + 2]
                    sp.dma_start(wat[sub.slot][:, 0:nxt.cols], packs[nxt.order]).then_inc(weights_in[nxt.order], 16)

            for sub in SUBS:
                if isinstance(sub, Attn) and sub.ctx:
                    context(sub, 0)
                    next_weights(SUBS[sub.index - 1])
                    context(sub, 1)
                    nxt = SUBS[sub.index + 1]
                    if nxt.index == 2:
                        pieces(nxt, 0, range(RING_L0, RING_L1))
                    if nxt.index == 5:
                        pieces(nxt, 32, range(RING_L1, RING_X))
                        sp.wait_ge(dn_ready, START + nxt.base["dn"] + 8 + 8 * EXPERTS)
                        for i in range(2):
                            sp.dma_start(mlpw[:, i, :], ring_dram[RING_X + i, :, :]).then_inc(mlp_in, 16)
                    if nxt.index == 11:
                        pieces(nxt, 64, 2 * list(range(RING_GLU, RING_ALL)))
                    next_weights(sub)
            for b in range(B):
                sp.wait_ge(xres_done, START + SUBS[11].base["row"] + b + 1)
                sp.dma_start(out[b, :, :], x_res[:, b, :]).then_inc(out_done, 16)
            sp.wait_ge(out_done, 16 * B)

        @block.tensor
        def _(pe):
            ident = c("ident")
            for s in (proj_ready, kprep_ready, knorm_ready, head_ready, t_ready, pv_done, y_ready, xt_ready, up_ready,
                      dn_ready, q_T):
                pe.sem_inc(s, START)

            def ctx_wait(sub, second, b, p):
                pe.wait_ge(ctx_in[p], 64 * (2 * sub.ctx_before + second) + 8 * (b - p) + 16)

            def k_prep(sub):
                wk = w(sub, "wk", KC).rearrange("p (c n) -> p c n", c=2)

                def one(b, p):
                    ctx_wait(sub, 0, b, p)
                    for m in range(2):
                        pe.wait_ge(kprep_done, at(sub, "kprep", b, m + 1) - 2)
                        for k in range(2):
                            mm = pe.matmul(bank[m][:, 0:S2], wk[:, k, 128 * m:128 * m + 128], ctxb[:, p, k, :],
                                           start=(k == 0), stop=(k == 1))
                        mm.then_inc(kprep_ready, 1)

                def sums(b, p):
                    pe.wait_ge(kprep_done, at(sub, "kprep", b, 2))
                    pe.wait_ge(knorm_done, START + b - 1)
                    for m in range(2):
                        mm = pe.matmul(bank[2 + p][0:T, 0:S2], c("ones"), qsq[:, m, :], start=(m == 0), stop=(m == 1))
                    mm.then_inc(knorm_ready, 1)

                with pe.Fori(0, B // 2) as pair:
                    b0 = pair * 2
                    one(b0, 0)
                    one(b0 + 1, 1)
                    if sub.qk_norm:
                        sums(b0, 0)
                        sums(b0 + 1, 1)
                pe.wait_ge(kprep_done, at(sub, "kprep", B, 0))
                if sub.qk_norm:
                    pe.wait_ge(knorm_done, START + B)

            def project(sub, b, p, which):
                if 0 in which:
                    pe.wait_ge(xtb_ready, at(sub, "batch", b, 1))
                wq = w(sub, "wq").rearrange("p (c n) -> p c n", c=2)
                wk = w(sub, "wk", sub.kdim).rearrange("p (c n) -> p c n", c=2)
                wv = w(sub, "wv", sub.kdim).rearrange("p (c n) -> p c n", c=2)
                for i in which:
                    item = sub.items[i]
                    pe.wait_ge(proj_done, at(sub, "proj", b, i + 1) - 2)
                    ps = proj_bank(sub, p, i)
                    if item in ("q", "k"):
                        wx = wq if item == "q" else wk
                        for m in range(sub.qc // 128):
                            for k in range(2):
                                mm = pe.matmul(ps[:, m * T:(m + 1) * T], wx[:, k, 128 * m:128 * m + 128],
                                               xTb[:, p, k, :], start=(k == 0), stop=(k == 1))
                    elif item == "qrow":
                        for k in range(2):
                            mm = pe.matmul(ps[0:T, 0:DM], xTb[:, p, k, :], wq[:, k, :], start=(k == 0), stop=(k == 1))
                    elif item in ("rq", "rk"):
                        pe.wait_ge(proj_done, at(sub, "proj", b, 2))
                        src = qT if item == "rq" else kT
                        for m in range(2):
                            mm = pe.matmul(ps[:, m * T:(m + 1) * T], w(sub, "rot"), src[:, p, m, :], start=True, stop=True)
                    elif item[0] == "v" and sub.ctx:
                        t = int(item[1])
                        if t == 0:
                            ctx_wait(sub, 1, b, p)
                        for k in range(2):
                            mm = pe.matmul(ps[0:KT, 0:DM], ctxb[:, p, k, t * KT:(t + 1) * KT], wv[:, k, :],
                                           start=(k == 0), stop=(k == 1))
                    elif item[0] == "v":
                        for k in range(2):
                            mm = pe.matmul(ps[0:T, 0:sub.qc], xTb[:, p, k, :], wv[:, k, :], start=(k == 0), stop=(k == 1))
                    else:
                        side, m = "qk".index(item[1]), int(item[2])
                        pe.wait_ge(proj_done, at(sub, "proj", b, 2))
                        if item[0] == "n":
                            pe.wait_ge(sq_ready, 2 * b + side + 1)
                        tab = w(sub, "ones2" if item[0] == "n" else "rf")
                        src = rT[:, p, side, m, :] if item[0] == "n" else (qT, kT)[side][:, p, m, :]
                        for u in range(4):
                            mm = pe.matmul(ps[:, u * T:(u + 1) * T], tab[:, 128 * u:128 * u + 128], src,
                                           start=True, stop=True)
                    mm.then_inc(proj_ready, 1)

            def scores_wait(sub, b):
                pe.wait_ge(qblk_ready, at(sub, "batch", b, 1))
                if sub.rope:
                    pe.wait_ge(rot_step, 6 * b + 6)
                if sub.feats:
                    pe.wait_ge(feat_ready, 4 * b + 4)
                if "k" in sub.items:
                    pe.wait_ge(proj_done, at(sub, "proj", b, 2))

            def scores(sub, b, g, p, js=range(4)):
                if g == 0 and js[0] == 0:
                    scores_wait(sub, b)
                for j in js:
                    h = 4 * g + j
                    ch = h // sub.hpc
                    if sub.ctx:
                        sem_heads_free(pe, sub, b, h - 1)
                        pe.matmul(score_bank(sub, g, j)[0:T, 0:S2], qblk[:, p, h, :], kall[:, ch, bass.ds(b * S2, S2)],
                                  start=True, stop=True).then_inc(head_ready, 1)
                    else:
                        if j == 0:
                            sem_heads_free(pe, sub, b, h - 4)
                        mm = pe.matmul(score_bank(sub, g, j)[0:T, j * T:(j + 1) * T], qblk[:, p, h, :],
                                       (fk if sub.feats else kT)[:, p, ch, :], start=True, stop=True)
                        if j == 3:
                            mm.then_inc(head_ready, 4)

            def transposes(sub, b, g, p, tiles=None):
                pe.wait_ge(norm_done, at(sub, "group", b, g + 1))
                for t in range(sub.tiles) if tiles is None else tiles:
                    n = g * sub.tiles + t
                    pe.wait_ge(t_done, at(sub, "pt", b, n + 1) - 2)
                    for j in range(2 if sub.diff else 4):
                        src = wd[:, g % 2, j, :] if sub.diff else pr[:, g, j, t * sub.rows:(t + 1) * sub.rows]
                        mm = pe.transpose(pt_bank(sub, n)[0:sub.rows, j * T:(j + 1) * T], src, ident[0:T, 0:T])
                    mm.then_inc(t_ready, 1)

            def values(sub, b, g, p, js=range(4)):
                if js[0] == 0:
                    pe.wait_ge(t_done, at(sub, "pt", b, (g + 1) * sub.tiles))
                if g == 0 and js[0] == 0:
                    if sub.diff:
                        if not isinstance(b, int) or b > 0:
                            pe.wait_ge(o_step, 7 * b - 6)
                    else:
                        pe.wait_ge(ot_done, at(sub, "batch", b, 0))
                    if sub.mlp:
                        pe.wait_ge(hid_done, START + b)
                    pe.wait_ge(proj_done, at(sub, "proj", b, sub.items.index(f"v{sub.tiles - 1}") + 1))
                    pe.wait_ge(v_zero, 1 + (sub.index > 2) + (sub.index > 5))
                if sub.diff:
                    for i in range(2):
                        h = 2 * g + i
                        mm = pe.matmul(OT[0:T, 64 * h:64 * h + 64], pts[0:T, g % 2, 0, i * T:(i + 1) * T],
                                       vd[:, p, 64 * h:64 * h + 64], start=True, stop=True)
                else:
                    for j in js:
                        h = 4 * g + j
                        for t in range(sub.tiles):
                            mm = pe.matmul(OT[32 * j:32 * j + 32, g * T:(g + 1) * T],
                                           vbuf[0:sub.rows, p, t, 32 * h:32 * h + 32],
                                           pts[0:sub.rows, g % 2, t, j * T:(j + 1) * T],
                                           start=(t == 0), stop=(t == sub.tiles - 1))
                if js[-1] == 3:
                    mm.then_inc(pv_done, 1)

            def normed_output_t(sub, b, p):
                pe.wait_ge(o_step, 7 * b + 7)
                pe.wait_ge(xt_done, xt_at(sub, b) - 1)
                for k in range(4):
                    mm = pe.transpose(TL[:, k * T:(k + 1) * T], on[:, p, 128 * k:128 * k + 128], ident[0:T, 0:T])
                mm.then_inc(onT_ready, 1)

            def mlp_hidden(sub, b, p):
                pe.wait_ge(ot_done, at(sub, "batch", b, 1))
                if isinstance(b, int):
                    pe.wait_ge(mlp_in, 32)
                w1 = mlpw[:, 0, :].rearrange("p (k n) -> p k n", k=4)
                for m in range(4):
                    for k in range(4):
                        mm = pe.matmul(OT[:, m * T:(m + 1) * T], w1[:, k, 128 * m:128 * m + 128], oT[:, p, k, :],
                                       start=(k == 0), stop=(k == 3))
                mm.then_inc(hid_ready, 1)

            def out_proj(sub, b, p):
                if sub.mlp:
                    pe.wait_ge(hid_done, START + b + 1)
                    src, wo = hT, mlpw[:, 1, 0:4 * DM].rearrange("p (k n) -> p k n", k=4)
                else:
                    pe.wait_ge(ot_done, at(sub, "batch", b, 1))
                    src, wo = oT, w(sub, "wo").rearrange("p (k n) -> p k n", k=4)
                pe.wait_ge(xt_done, xt_at(sub, b) - 1)
                for k in range(4):
                    mm = pe.matmul(TL[0:T, 0:DM], src[:, p, k, :], wo[:, k, :], start=(k == 0), stop=(k == 3))
                mm.then_inc(y_ready, 1)

            def rows_t(sub, b, p, ps=TL):
                pe.wait_ge(xln_ready, at(sub, "row", b, 1))
                pe.wait_ge(xt_done, xt_at(sub, b) - 1)
                for k in range(2):
                    mm = pe.transpose(ps[:, DM + k * T:DM + (k + 1) * T], xln[:, p, 128 * k:128 * k + 128], ident[0:T, 0:T])
                mm.then_inc(xt_ready, 1)

            def attention(sub):
                pe.wait_ge(weights_in[sub.order], 16)
                if sub.order:
                    last = ATTNS[sub.order - 1]
                    sem_heads_free(pe, last, B, 0)
                    pe.wait_ge(proj_done, at(last, "proj", B, 0))
                    pe.wait_ge(t_done, at(last, "pt", B, 0))
                if sub.index and isinstance(SUBS[sub.index - 1], Ffn):
                    pe.wait_ge(dn_done, START + SUBS[sub.index - 1].base["dn"] + int(SUBS[sub.index - 1].per["dn"] * B))
                if sub.ctx:
                    k_prep(sub)

                project(sub, 0, 0, range(len(sub.items)))

                def step(b, g, p, back, more, tail, far):
                    if sub.mlp and (g, 1) == sub.y_at and tail:
                        mlp_hidden(sub, b - 1, 1 - p)
                    if sub.ctx:
                        for j in range(4):
                            if back[0]:
                                scores(sub, b, g, p, (j,))
                            if back[sub.lag] and j < 3:
                                transposes(sub, *back[sub.lag], tiles=(j,))
                            if back[sub.lag + 1] and j in (1, 3):
                                values(sub, *back[sub.lag + 1], (j - 1, j))
                            if more and (g, j) in sub.when:
                                project(sub, b + 1, 1 - p, sub.when[g, j])
                    else:
                        if back[0]:
                            scores(sub, b, g, p)
                        if back[sub.lag]:
                            transposes(sub, *back[sub.lag])
                        if back[sub.lag + 1]:
                            values(sub, *back[sub.lag + 1])
                    if (g, 2) == sub.rows_at and far:
                        rows_t(sub, b - 2, p)
                    if more and not sub.ctx and (g, 3) in sub.when:
                        project(sub, b + 1, 1 - p, sub.when[g, 3])
                    if sub.diff and g == 3 and tail:
                        normed_output_t(sub, b - 1, 1 - p)
                    if (g, 2) == sub.y_at and far:
                        out_proj(sub, b - 2, p)
                    if (g, 1) == sub.y_at and tail:
                        out_proj(sub, b - 1, 1 - p)
                pipeline(pe, step)

            def split_matmul(out, weights, rows, start, stop):
                pe.matmul(out, weights[0], rows[0], start=start, stop=False)
                pe.matmul(out, weights[0], rows[1], start=False, stop=False)
                return pe.matmul(out, weights[1], rows[0], start=False, stop=stop)

            def experts(sub, router, bias):
                pe.wait_ge(ffn_small_in, 16)
                pe.wait_ge(xt_done, xt_at(SUBS[sub.index - 1], B - 1))
                n = sub.index // 3
                for t in range(B):
                    for k in range(2):
                        mm = pe.matmul(bank[0][0:T, 8 * t:8 * t + 8], xT[:, k, t * T:(t + 1) * T],
                                       f(router)[:, 8 * k:8 * k + 8], start=(k == 0), stop=(k == 1))
                mm.then_inc(rt_ready, 1)
                pe.wait_ge(wt_ready, n + 1)
                for t in range(B):
                    mm = pe.transpose(bank[1 + t // 4][0:8, t % 4 * T:(t % 4 + 1) * T], wts[:, t, :], ident[0:T, 0:T])
                mm.then_inc(wt_T, 1)
                pe.wait_ge(wt_done, n + 1)
                db, ub = START + sub.base["dn"], START + sub.base["up"]
                for t in range(B):
                    pe.wait_ge(dn_done, db + t - 3)
                    pe.matmul(bank[4 + t % 4][0:T, 0:DM], wtT[:, t * T:(t + 1) * T], f(bias, 8),
                              start=True, stop=True).then_inc(dn_ready, 1)
                if n:
                    for t in range(B):
                        pe.wait_ge(xs_ready, t + 1)
                        if t >= 2:
                            pe.wait_ge(xs_done, t - 1)
                        for k in range(2):
                            mm = pe.transpose(bank[2 + t % 2][:, k * T:(k + 1) * T], xs[:, t % 2, 128 * k:128 * k + 128],
                                              ident[0:T, 0:T])
                        mm.then_inc(xs_T, 1)
                    pe.wait_ge(xs_done, B)

                def one(e0, p, last=False):
                    e = e0 + p
                    wb = START + 32 * n + 4 * e
                    wu = wsplit[:, 0:2, :].rearrange("p a (k n) -> p a k n", k=2)
                    wdn = wsplit[:, 2:4, :].rearrange("p a (k n) -> p a k n", k=8)
                    pe.wait_ge(w_split, wb + 2)
                    for u in range(2):
                        pe.wait_ge(x_split, 4 * n + 2 * u + 2)
                        for m in range(8):
                            pe.wait_ge(up_done, ub + 16 * e + 8 * u + m - 3)
                            for k in range(2):
                                mm = split_matmul(bank[m % 4][:, 0:HALF],
                                                  [wu[:, a, k, 128 * m:128 * m + 128] for a in range(2)],
                                                  [xsplit[:, a, k, u * HALF:(u + 1) * HALF] for a in range(2)],
                                                  start=(k == 0), stop=(k == 1))
                            mm.then_inc(up_ready, 1)
                    pe.wait_ge(w_split, wb + 4)
                    for t in range(B):
                        if t % 4 == 0:
                            pe.wait_ge(h_split, ub + 16 * e + 2 * t + 8)
                        pe.wait_ge(dn_done, db + 8 + 8 * e + t - 3)
                        for k in range(8):
                            mm = split_matmul(bank[4 + t % 4][0:T, 0:DM],
                                              [hid[:, a, t // 4, k, t % 4 * T:(t % 4 + 1) * T] for a in range(2)],
                                              [wdn[:, a, k, :] for a in range(2)], start=(k == 0), stop=(k == 7))
                        mm.then_inc(dn_ready, 1)
                        if last and t >= 2:
                            rows_t(sub, t - 2, t % 2, bank[t % 2])

                with pe.Fori(0, EXPERTS // 2 - 1) as pair:
                    e0 = pair * 2
                    one(e0, 0)
                    one(e0, 1)
                one(EXPERTS - 2, 0)
                one(EXPERTS - 2, 1, True)
                for t in (B - 2, B - 1):
                    rows_t(sub, t, t % 2, bank[t % 2])

            def quantised(sub):
                pe.wait_ge(xt_done, xt_at(SUBS[sub.index - 1], B - 1))
                pe.wait_ge(rq_step, 9)
                for m in range(2):
                    pe.matmul(bank[1][0:T, 128 * m:128 * m + 128], c("ones"), diag[:, m, :], start=True, stop=True)
                    for k in range(2):
                        mm = pe.transpose(bank[0][:, 256 * k + 128 * m:256 * k + 128 * m + 128],
                                          rqf[:, m, 128 * k:128 * k + 128], ident)
                mm.then_inc(rq_T, 1)
                pe.wait_ge(rq_done, 2)

                with pe.Fori(0, B // 2) as pair:
                    b0 = pair * 2
                    for p in range(2):
                        pe.wait_ge(q_step, START + 9 * b0 + 17 + p)
                        pe.wait_ge(q_done, START + b0 + p - 1)
                        for k in range(2):
                            mm = pe.transpose(bank[2 + p][:, k * T:(k + 1) * T], qf[:, p, 128 * k:128 * k + 128],
                                              ident[0:T, 0:T])
                        mm.then_inc(q_T, 1)
                    for p in range(2):
                        pe.wait_ge(q_done, START + b0 + p + 1)
                        pe.wait_ge(dn_done, START + sub.base["dn"] + b0 + p - 1)
                        for k in range(2):
                            mm = pe.matmul(bank[4 + p][0:T, 0:DM], qbT[:, p, k, :], rqT[:, k, :], start=(k == 0), stop=(k == 1))
                        mm.then_inc(dn_ready, 1)
                    for p in range(2):
                        rows_t(sub, b0 + p, p)

            def glu(sub):
                ub, db, wb = START + sub.base["up"], START + sub.base["dn"], START + 64

                def wait_half(u, i, half):
                    pe.wait_ge(w_split, wb + 2 * (GLU_ITEMS * u + i) + half + 1)

                def item(u, i, k):
                    q = 2 * ((u + i) % 2)
                    return [wsplit[:, q + a, :].rearrange("p (k n) -> p k n", k=k) for a in range(2)]

                for u in range(2):
                    half = slice(u * HALF, (u + 1) * HALF)
                    pe.wait_ge(x_split, 8 + 2 * u + 2)
                    gate = [item(u, i, 2) for i in range(2)]
                    if u:
                        pe.wait_ge(up_done, ub + 24)
                    for m in range(8):
                        if 8 * u + m >= 2:
                            pe.wait_ge(glu_done, 8 * u + m - 1)
                        for i in range(2):
                            for k in range(2):
                                if m == 0:
                                    wait_half(u, i, k)
                                mm = split_matmul(bank[2 * (m % 2) + i][:, 0:HALF],
                                                  [gate[i][a][:, k, 128 * m:128 * m + 128] for a in range(2)],
                                                  [xsplit[:, a, k, half] for a in range(2)], start=(k == 0), stop=(k == 1))
                            mm.then_inc(up_ready, 1)
                    for layer in range(2):
                        for m in range(8):
                            if m % 2 == 0:
                                wx = item(u, 2 + 4 * layer + m // 2, 8)
                            if m >= 4:
                                pe.wait_ge(up_done, ub + 24 * u + 8 + 8 * layer + m - 3)
                            for k in range(8):
                                if m % 2 == 0 and k % 4 == 0:
                                    wait_half(u, 2 + 4 * layer + m // 2, k // 4)
                                if m == 0:
                                    pe.wait_ge(h_split, ub + 24 * u + 8 * layer + k + 1)
                                mm = split_matmul(bank[m % 4][:, 0:HALF],
                                                  [wx[a][:, k, m % 2 * 128:m % 2 * 128 + 128] for a in range(2)],
                                                  [hid[:, a, layer, k, :] for a in range(2)], start=(k == 0), stop=(k == 7))
                            mm.then_inc(up_ready, 1)
                    w3 = item(u, 10, 8)
                    if u == 0:
                        pe.wait_ge(xt_done, xt_at(SUBS[sub.index - 1], B - 1))
                    for t in range(4 * u, 4 * u + 4):
                        pe.wait_ge(dn_done, db + t - 3)
                        for k in range(8):
                            if t == 4 * u and k % 4 == 0:
                                wait_half(u, 10, k // 4)
                            if t == 4 * u:
                                pe.wait_ge(h_split, ub + 24 * u + 16 + k + 1)
                            mm = split_matmul(bank[4 + t % 4][0:T, 0:DM],
                                              [hid[:, a, 0, k, t % 4 * T:(t % 4 + 1) * T] for a in range(2)],
                                              [w3[a][:, k, :] for a in range(2)], start=(k == 0), stop=(k == 7))
                        mm.then_inc(dn_ready, 1)

            pe.wait_ge(x_in, 16)
            pe.wait_ge(consts_in, 16)
            for b in range(B):
                if b >= 4:
                    pe.wait_ge(xt_done, START + b - 3)
                for k in range(2):
                    mm = pe.transpose(bank[4 + b % 4][:, DM + k * T:DM + (k + 1) * T], x_res[:, b, 128 * k:128 * k + 128], ident[0:T, 0:T])
                mm.then_inc(xt_ready, 1)
            for sub in SUBS:
                if isinstance(sub, Attn):
                    attention(sub)
                elif sub.index in (2, 5):
                    experts(sub, "L0_router" if sub.index == 2 else "L1_router", "L0_bdown" if sub.index == 2 else "L1_b2")
                elif sub.index == 8:
                    quantised(sub)
                else:
                    glu(sub)

        @block.scalar
        def _(act):
            for s, n in ((proj_done, 0), (kprep_done, 0), (t_done, 0), (exp_done, 0), (xt_done, 0), (up_done, 0), (hid_done, 0),
                         (knorm_done, 0), (q_done, 0)):
                act.sem_inc(s, START)

            def k_prep(sub):
                def one(b, p):
                    for m in range(2):
                        act.wait_ge(kprep_ready, at(sub, "kprep", b, m + 1))
                        ins = nc.scalar.activation(kall[:, m, bass.ds(b * S2, S2)], bank[m][:, 0:S2], ACT.Identity,
                                                   bias=w(sub, "bk")[:, m:m + 1])
                        if sub.qk_norm:
                            act.wait_ge(knorm_ready, START + b)
                            ins = nc.scalar.activation(qsq[:, m, :], bank[m][:, 0:S2], ACT.Square,
                                                       bias=w(sub, "bk")[:, m:m + 1])
                        ins.then_inc(kprep_done, 1)

                def roots(b, p):
                    act.wait_ge(knorm_ready, START + b + 1)
                    nc.scalar.activation(rowb[:, bass.ds(b, 1), :].rearrange("p o n -> p (o n)"),
                                         bank[2 + p][0:T, 0:S2], ACT.Sqrt).then_inc(knorm_done, 1)

                with act.Fori(0, B // 2) as pair:
                    b0 = pair * 2
                    one(b0, 0)
                    one(b0 + 1, 1)
                    if sub.qk_norm:
                        roots(b0, 0)
                        roots(b0 + 1, 1)

            def items(sub, b, p, which):
                func = ACT.Exp if sub.kind == "causal" else ACT.Identity
                for i in which:
                    item = sub.items[i]
                    act.wait_ge(proj_ready, at(sub, "proj", b, i + 1))
                    ps = proj_bank(sub, p, i)
                    if item == "q":
                        act.wait_ge(qblk_ready, at(sub, "batch", b, -1))
                        nq = sub.qc // 128
                        for m in range(nq):
                            ins = nc.scalar.activation(qT[:, p, m, :], ps[:, m * T:(m + 1) * T], func,
                                                       bias=w(sub, "bq")[:, m:m + 1])
                    elif item == "k":
                        act.wait_ge(head_ready, START + HEADS * (B * sub.order + b - 1))
                        for m in range(sub.qc // 128):
                            ins = nc.scalar.activation(kT[:, p, m, :], ps[:, m * T:(m + 1) * T], func,
                                                       bias=w(sub, "bk")[:, m:m + 1])
                    elif item[0] == "v":
                        if item == "v0":
                            act.wait_ge(pv_done, at(sub, "group", b, 0) - GROUPS)
                            act.wait_ge(v_zero, 1 + (sub.index > 2) + (sub.index > 5))
                        t = int(item[1])
                        if sub.diff:
                            ins = nc.scalar.copy(vd[:, p, :], ps[0:T, 0:512])
                        else:
                            ins = nc.scalar.copy(
                                vbuf[0:sub.rows, p, t, :].rearrange("p (h e) -> p h e", e=32)[:, :, 0:16],
                                ps[0:sub.rows, 0:DM].rearrange("p (h e) -> p h e", e=16))
                    elif item == "qrow":
                        ins = nc.scalar.copy(qrow[:, p, 0, :], ps[0:T, 0:DM])
                    elif item in ("rq", "rk"):
                        ins = nc.scalar.copy(rT[:, p, "qk".index(item[1]), :, :],
                                             ps[:, 0:2 * T].rearrange("p (m n) -> p m n", m=2))
                    else:
                        u = 2 * "qk".index(item[1]) + int(item[2])
                        if item[0] == "n":
                            ins = nc.scalar.activation(nT[:, u, :], ps[:, 0:4 * T], ACT.Sqrt)
                        else:
                            ins = nc.scalar.activation(pj[:, u, :], ps[:, 0:4 * T], ACT.Copy, scale=0.125)
                    ins.then_inc(proj_done, 1)

            def features(sub, b, p):
                for u in range(4):
                    act.wait_ge(fsub_ready, 4 * b + u + 1)
                    dst = (fq, fk)[u // 2][:, p, 4 * (u % 2):4 * (u % 2) + 4, :]
                    nc.scalar.activation(dst, pj[:, u, :].rearrange("p (m n) -> p m n", m=4), ACT.Exp)\
                        .then_inc(feat_ready, 1)

            def exps(sub, b, g, p, js=range(4)):
                if sub.kind != "softmax":
                    return
                if js[0] == 0:
                    act.wait_ge(t_ready, at(sub, "pt", b, (g - 3) * sub.tiles))
                for j in js:
                    h = 4 * g + j
                    if sub.ctx or j == 0:
                        act.wait_ge(max_ready, at(sub, "head", b, h + (1 if sub.ctx else 4)))
                    if not sub.ctx:
                        src = score_bank(sub, g, j)[0:T, j * T:(j + 1) * T]
                    elif sub.dve_frees:
                        src = sc[:, j, :]
                    else:
                        src = score_bank(sub, g, j)[0:T, 0:S2]
                    nc.scalar.activation(pr[:, g, j, 0:sub.keys], src, ACT.Exp, bias=nm[:, p, h:h + 1],
                                         scale=qn[:, p, 4:5] if sub.qk_norm else 1.0,
                                         accum_out=ls[:, p, h:h + 1]).then_inc(exp_done, 1)

            def tiles_in(sub, b, g, p, tiles):
                if tiles[0] == 0:
                    act.wait_ge(pv_done, at(sub, "group", b, g - 1))
                for t in tiles:
                    k = g * sub.tiles + t
                    act.wait_ge(t_ready, at(sub, "pt", b, k + 1))
                    n = (2 if sub.diff else 4) * T
                    nc.scalar.copy(pts[0:sub.rows, g % 2, t, 0:n], pt_bank(sub, k)[0:sub.rows, 0:n]).then_inc(t_done, 1)

            def hidden(sub, b, p):
                act.wait_ge(hid_ready, b + 1)
                for m in range(4):
                    ins = nc.scalar.activation(hT[:, p, m, :], OT[:, m * T:(m + 1) * T], ACT.Relu,
                                               bias=w(sub, "b1")[:, m:m + 1])
                ins.then_inc(hid_done, 1)

            def rows_in(sub_row, b, ps=TL):
                act.wait_ge(xt_ready, START + sub_row + b + 1)
                nc.scalar.copy(xT[:, :, bass.ds(b * T, T)],
                               ps[:, DM:DM + 2 * T].rearrange("p (k n) -> p k n", k=2)).then_inc(xt_done, 1)

            def attention(sub):
                act.wait_ge(weights_in[sub.order], 16)
                if sub.ctx:
                    k_prep(sub)

                items(sub, 0, 0, range(len(sub.items)))
                if sub.feats:
                    features(sub, 0, 0)

                def step(b, g, p, back, more, tail, far):
                    if sub.mlp and (g, 1) == sub.y_at and tail:
                        hidden(sub, b - 1, 1 - p)
                    if sub.ctx:
                        for j in range(4):
                            if back[0]:
                                exps(sub, b, g, p, (j,))
                            if back[sub.lag] and j < 3:
                                tiles_in(sub, *back[sub.lag], (j,))
                            if more and (g, j) in sub.when:
                                items(sub, b + 1, 1 - p, sub.when[g, j])
                    else:
                        if back[0]:
                            exps(sub, b, g, p)
                        if back[sub.lag]:
                            tiles_in(sub, *back[sub.lag], (0,))
                    if (g, 2) == sub.rows_at and far:
                        rows_in(B + sub.base["row"], b - 2)
                    if more and not sub.ctx and (g, 3) in sub.when:
                        items(sub, b + 1, 1 - p, sub.when[g, 3])
                    if more and g == 2 and sub.feats:
                        features(sub, b + 1, 1 - p)
                pipeline(act, step)

            def experts(sub, bias, func):
                act.wait_ge(ffn_small_in, 16)
                n = sub.index // 3
                act.wait_ge(rt_step[n], 20)
                nc.scalar.activation(ex[:, :, :], ex[:, :, :], ACT.Exp).then_inc(rt_exp, 1)
                act.wait_ge(wt_T, n + 1)
                nc.scalar.copy(wtT[:, 0:HALF], bank[1][0:8, 0:HALF])
                nc.scalar.copy(wtT[:, HALF:2 * HALF], bank[2][0:8, 0:HALF]).then_inc(wt_done, 1)
                if n:
                    for t in range(B):
                        act.wait_ge(xs_T, t + 1)
                        nc.scalar.copy(xT[:, :, t * T:(t + 1) * T],
                                       bank[2 + t % 2][:, 0:2 * T].rearrange("p (m n) -> p m n", m=2)).then_inc(xs_done, 1)
                ub = START + sub.base["up"]

                def one(e0, p):
                    e = e0 + p
                    nc.scalar.copy(bup[:, p, :], f(bias)[:, bass.ds(8 * e, 8)]).then_inc(bup_ready, 1)
                    act.wait_ge(bup_ready, 8 * n + e + 1)
                    for c in range(16):
                        act.wait_ge(up_ready, ub + 16 * e + c + 1)
                        act.wait_ge(h_split, ub + 16 * e + c - 3)
                        nc.scalar.activation(tmp[:, c % 4, :], bank[c % 4][:, 0:HALF], func,
                                             bias=bup[:, p, c % 8:c % 8 + 1]).then_inc(up_done, 1)
                with act.Fori(0, EXPERTS // 2) as pair:
                    e0 = pair * 2
                    one(e0, 0)
                    one(e0, 1)

            def new_rows(sub):
                for b in range(B):
                    rows_in(B + sub.base["row"], b, bank[b % 2])

            def quantised(sub):
                act.wait_ge(rq_T, 1)
                nc.scalar.copy(rqT[:, :, :], bank[0][:, 0:512].rearrange("p (k n) -> p k n", k=2)).then_inc(rq_done, 1)
                nc.scalar.copy(rsb[:, :], bank[1][0:T, 0:DM]).then_inc(rq_done, 1)

                with act.Fori(0, B // 2) as pair:
                    b0 = pair * 2
                    for p in range(2):
                        act.wait_ge(q_T, START + b0 + p + 1)
                        act.wait_ge(dn_ready, START + sub.base["dn"] + b0 + p - 1)
                        nc.scalar.copy(qbT[:, p, :, :], bank[2 + p][:, 0:2 * T].rearrange("p (m n) -> p m n", m=2))\
                            .then_inc(q_done, 1)
                    for p in range(2):
                        rows_in(B + sub.base["row"], b0 + p)

            def glu(sub):
                ub = START + sub.base["up"]
                for u in range(2):
                    for m in range(24):
                        c = 24 * u + m
                        if m < 8:
                            act.wait_ge(up_ready, ub + 32 * u + 2 * m + 1)
                            src, func, scale = bank[2 * (m % 2)], ACT.Silu, f("s1")
                        else:
                            act.wait_ge(up_ready, ub + 32 * u + 8 + m + 1)
                            src, func, scale = bank[m % 4], ACT.Gelu, f("sh1" if m < 16 else "sh2")
                        act.wait_ge(h_split, ub + c - 3)
                        nc.scalar.activation(tmp[:, c % 4, :], src[:, 0:HALF], func,
                                             scale=scale[:, m % 8:m % 8 + 1]).then_inc(up_done, 1)

            for b in range(B):
                rows_in(0, b, bank[4 + b % 4])
            act.wait_ge(lam_step, 2)
            nc.scalar.activation(lamt[:, 34:36], lamt[:, 32:34], ACT.Exp).then_inc(lam_exp, 1)
            for sub in SUBS:
                if isinstance(sub, Attn):
                    attention(sub)
                elif sub.index in (2, 5):
                    experts(sub, "L0_bup" if sub.index == 2 else "L1_b1", ACT.Gelu if sub.index == 2 else ACT.Relu)
                    new_rows(sub)
                elif sub.index == 8:
                    quantised(sub)
                else:
                    glu(sub)

        @block.vector
        def _(dve):
            for s in (ot_done, dhead_done, max_ready, norm_done, inv_step, ln_dve, xln_ready, dn_done, q_step,
                      qn_step, ln_in, rsum_done, w_split, h_split):
                dve.sem_inc(s, START)

            def group_scores(sub, b, g, p):
                hs = slice(4 * g, 4 * g + 4)
                dve.wait_ge(head_ready, START + HEADS * (B * sub.order + b) + 4 * g + 4)
                ps = score_bank(sub, g, 0)[0:T, 0:4 * T].rearrange("p (j n) -> p j n", j=4)
                if sub.kind == "softmax":
                    dve.reduce_max(nm[:, p, hs], ps, AX_X, negate=True).then_inc(max_ready, 4)
                    return
                dve.wait_ge(t_ready, at(sub, "pt", b, (g - 3) * sub.tiles))
                dst = pr[:, g, :, 0:T]
                if sub.kind == "causal":
                    tri = c("causal", T).unsqueeze(1).to_broadcast([T, 4, T])
                    dve.tensor_tensor(dst, ps, tri, ALU.mult).then_inc(dhead_done, 4)
                else:
                    dve.tensor_copy(dst, ps).then_inc(dhead_done, 4)
                dve.wait_ge(dhead_done, at(sub, "dhead", b, 4 * g + 4))
                dve.reduce_sum(ls[:, p, hs], dst, AX_X).then_inc(rsum_done, 1)

            def heads(sub, b, g, p, js):
                for j in js:
                    h = 4 * g + j
                    dve.wait_ge(head_ready, START + HEADS * (B * sub.order + b) + h + 1)
                    ps = score_bank(sub, g, j)[0:T, 0:S2]
                    if sub.dve_frees:
                        dve.wait_ge(exp_done, at(sub, "head", b, h - 3))
                        apart(dve)
                    if sub.clip:
                        dve.tensor_scalar(sc[:, j, :], ps, CLAMP, -CLAMP, ALU.min, ALU.max).then_inc(dhead_done, 1)
                        dve.wait_ge(dhead_done, at(sub, "dhead", b, h + 1))
                        ps = sc[:, j, :]
                    if sub.mask or sub.qk_norm:
                        dve.tensor_tensor_reduce(sc[:, j, :], ps, rowf[:, p, :], 1.0, LOWEST,
                                                 ALU.add if sub.mask else ALU.mult, ALU.max,
                                                 mx[:, p, h:h + 1]).then_inc(dhead_done, 1)
                        dve.wait_ge(dhead_done, at(sub, "dhead", b, h + 1))
                    else:
                        ins = dve.reduce_max(nm[:, p, h:h + 1], ps, AX_X, negate=True)
                    if sub.qk_norm:
                        ins = dve.tensor_scalar(nm[:, p, h:h + 1], mx[:, p, h:h + 1], qn[:, p, 4:5], -1.0, ALU.mult, ALU.mult)
                    elif sub.mask:
                        ins = dve.tensor_scalar(nm[:, p, h:h + 1], mx[:, p, h:h + 1], -1.0, None, ALU.mult)
                    ins.then_inc(max_ready, 1)

            def norm(sub, b, g, p):
                hs = slice(4 * g, 4 * g + 4)
                if sub.kind == "softmax":
                    dve.wait_ge(exp_done, at(sub, "head", b, 4 * g + 4))
                else:
                    dve.wait_ge(rsum_done, at(sub, "rsum", b, g + 1))
                k = sub.per["inv"] // GROUPS
                step = Steps(dve, inv_step, at(sub, "inv", b, g * k), k)
                if sub.kind == "linear":
                    step(dve.tensor_scalar(mx[:, p, hs], ls[:, p, hs], 1e-6, None, ALU.add))
                    step(dve.reciprocal(rv[:, p, hs], mx[:, p, hs]))
                else:
                    step(dve.reciprocal(rv[:, p, hs], ls[:, p, hs]))
                if sub.diff:
                    odd = rv[:, p, :].rearrange("p (i two) -> p i two", two=2)[:, 2 * g:2 * g + 2, 1]
                    step(dve.tensor_scalar(odd, odd, lamt[:, 38:39], None, ALU.mult))
                    dve.wait_ge(t_ready, at(sub, "pt", b, g - 1))
                    for i in range(2):
                        h = 4 * g + 2 * i
                        ins = dve.tensor_scalar(pr[:, g, 2 * i, 0:T], pr[:, g, 2 * i, 0:T], rv[:, p, h:h + 1], None, ALU.mult)
                    ins.then_inc(wd_step, 1)
                    dve.wait_ge(wd_step, GROUPS * b + g + 1)
                    for i in range(2):
                        h = 4 * g + 2 * i
                        ins = dve.scalar_tensor_tensor(out=wd[:, g % 2, i, :], in0=pr[:, g, 2 * i + 1, 0:T],
                                                       scalar=rv[:, p, h + 1:h + 2], in1=pr[:, g, 2 * i, 0:T],
                                                       op0=ALU.mult, op1=ALU.add)
                elif not sub.ctx:
                    wts4 = pr[:, g, :, 0:T]
                    ins = dve.tensor_tensor(wts4, wts4, rv[:, p, hs].unsqueeze(2).to_broadcast([T, 4, T]), ALU.mult)
                else:
                    for j in range(4):
                        h = 4 * g + j
                        ins = dve.tensor_scalar(pr[:, g, j, 0:sub.keys], pr[:, g, j, 0:sub.keys], rv[:, p, h:h + 1],
                                                None, ALU.mult)
                ins.then_inc(norm_done, 1)

            def output_in(sub, b, p):
                dve.wait_ge(pv_done, at(sub, "group", b, 4))
                if sub.diff:
                    step = Steps(dve, o_step, 7 * b, 7)
                    step(dve.tensor_copy(on[:, p, :], OT[0:T, :]))
                    step(dve.tensor_tensor(osq[:, :], on[:, p, :], on[:, p, :], ALU.mult))
                    step(dve.reduce_sum(rms[:, p, 0, :], osq[:, :].rearrange("p (h e) -> p h e", h=8), AX_X))
                    dve.wait_ge(o_pool, 2 * b + 2)
                    step(dve.tensor_scalar(rms[:, p, 3, :], rms[:, p, 2, :], 1e-8, None, ALU.add))
                    step(dve.reciprocal(rms[:, p, 4, :], rms[:, p, 3, :]))
                    oh = on[:, p, :].rearrange("p (h e) -> p h e", h=8)
                    step(dve.tensor_tensor(oh, oh, rms[:, p, 4, :].unsqueeze(2).to_broadcast([T, 8, 64]), ALU.mult))
                    step(dve.tensor_tensor(oh, oh, gam[:, :].unsqueeze(1).to_broadcast([T, 8, 64]), ALU.mult))
                else:
                    dve.wait_ge(y_ready, at(sub, "batch", b, -1))
                    if sub.mlp:
                        dve.wait_ge(hid_done, START + b - 1)
                    dve.tensor_tensor(oT[:, p, :, :], OT[:, 0:4 * T].rearrange("p (g n) -> p g n", g=4),
                                      w(sub, "bvT").unsqueeze(2).to_broadcast([128, 4, T]), ALU.add).then_inc(ot_done, 1)

            def stats(sub, b, p, unit):
                v = START + 3 * (sub.base["ln"] + int(sub.per["ln"]) * b + unit)
                dve.wait_ge(ln_dve, v + 1)
                dve.bn_stats(st[:, p, :], res[:, p, :]).then_inc(ln_dve, 1)
                dve.wait_ge(ln_dve, v + 2)
                apart(dve)
                dve.bn_aggr(mv[:, p, 0:2], st[:, p, :]).then_inc(ln_dve, 1)

            def normed(sub, b, p, unit, dst):
                u = sub.base["ln"] + int(sub.per["ln"]) * b + unit
                dve.wait_ge(ln_pool, START + 2 * u + 2)
                return dve.tensor_scalar(dst, res[:, p, :], mv[:, p, 0:1], mv[:, p, 3:4], ALU.subtract, ALU.mult)

            def rows_out(sub, b, p):
                dve.wait_ge(xt_ready, xt_at(sub, b) - 2)
                dve.wait_ge(xres_done, at(sub, "row", b, -1))
                normed(sub, b, p, int(sub.per["ln"]) - 1, xln[:, p, :]).then_inc(xln_ready, 1)

            def normed_output_in(sub, b, p):
                dve.wait_ge(onT_ready, b + 1)
                dve.wait_ge(y_ready, at(sub, "batch", b, -1))
                dve.tensor_copy(oT[:, p, :, :], TL[:, 0:4 * T].rearrange("p (g n) -> p g n", g=4)).then_inc(ot_done, 1)

            def ln_first(sub, b, p):
                dve.wait_ge(y_ready, at(sub, "batch", b, 1))
                dve.wait_ge(xb_ready, at(sub, "batch", b, 1))
                dve.tensor_tensor(res[:, p, :], TL[0:T, 0:DM], xb[:, p, :], ALU.add).then_inc(ln_dve, 1)
                stats(sub, b, p, 0)

            def ln_second(sub, b, p):
                if sub.qk_norm:
                    step = Steps(dve, ln_in, START + 3 * b, 3)
                    step(normed(sub, b, p, 0, junk[:, :]))
                    step(dve.tensor_tensor(junk[:, :], junk[:, :], w(sub, "ln_g", T), ALU.mult))
                    step(dve.tensor_tensor(junk[:, :], junk[:, :], w(sub, "ln_b", T), ALU.add))
                    wait_xres(dve, sub, b)
                    dve.tensor_tensor(res[:, p, :], junk[:, :], x_res[:, bass.ds(b, 1), :].rearrange("p o n -> p (o n)"),
                                      ALU.add).then_inc(ln_dve, 1)
                    stats(sub, b, p, 1)
                rows_out(sub, b, p)

            def prepare(sub, b, p):
                if sub.mask or sub.qk_norm:
                    dve.tensor_copy(rowf[:, p, :], rowb[:, bass.ds(b, 1), :].rearrange("p o n -> p (o n)")).then_inc(rowf_ready, 1)
                    dve.wait_ge(rowf_ready, (B if sub.qk_norm else 0) + b + 1)
                if sub.rope:
                    step = Steps(dve, rot_step, 6 * b, 6)
                    cos = w(sub, "cos").unsqueeze(1).to_broadcast([128, 2, T])
                    sin = w(sub, "sin").unsqueeze(1).to_broadcast([128, 2, T])
                    for s, src in enumerate((qT, kT)):
                        if s == 0:
                            dve.wait_ge(proj_done, at(sub, "proj", b, 4))
                        step(dve.tensor_tensor(rT[:, p, s, :, :], rT[:, p, s, :, :], sin, ALU.mult))
                        step(dve.tensor_tensor(src[:, p, 0:2, :], src[:, p, 0:2, :], cos, ALU.mult))
                        step(dve.tensor_tensor(src[:, p, 0:2, :], src[:, p, 0:2, :], rT[:, p, s, :, :], ALU.add))
                if sub.feats:
                    for u in range(4):
                        dve.wait_ge(proj_done, at(sub, "proj", b, 2 + 2 * u + 2))
                        dve.tensor_tensor(pj[:, u, :], pj[:, u, :], nT[:, u, :], ALU.subtract).then_inc(fsub_ready, 1)

            def q_squares(sub, b, p):
                dve.wait_ge(qrow_ready, b + 1)
                dve.wait_ge(exp_done, at(sub, "head", b, -HEADS))
                dve.tensor_tensor_reduce(junk[:, :], qrow[:, p, 1, :], qrow[:, p, 1, :], 1.0, 0.0, ALU.mult, ALU.add,
                                         qn[:, p, 0:1]).then_inc(qn_step, 1)

            def q_norm(sub, b, p):
                dve.wait_ge(qn_root, b + 1)
                step = Steps(dve, qn_step, START + 4 * b + 1, 3)
                step(dve.tensor_scalar(qn[:, p, 2:3], qn[:, p, 1:2], 1e-12, None, ALU.max))
                step(dve.reciprocal(qn[:, p, 3:4], qn[:, p, 2:3]))
                step(dve.tensor_scalar(qn[:, p, 4:5], qn[:, p, 3:4], sub.scale, None, ALU.mult))

            def key_rows(sub):
                r0 = B if sub.qk_norm else 0

                def one(b, p):
                    row = rowb[:, bass.ds(b, 1), :].rearrange("p o n -> p (o n)")
                    if sub.mask:
                        dve.wait_ge(mask_in[p], 8 * (b - p) + 16)
                        dve.tensor_scalar(row, maskb[:, p, :], BIG, -BIG, ALU.mult, ALU.add).then_inc(row_ready, 1)
                    else:
                        dve.wait_ge(knorm_done, START + b + 1)
                        dve.tensor_scalar(row, row, 1e-12, None, ALU.max).then_inc(row_step, 1)
                        dve.wait_ge(row_step, b + 1)
                        apart(dve)
                        dve.reciprocal(row, row).then_inc(row_ready, 1)
                with dve.Fori(0, B // 2) as pair:
                    b0 = pair * 2
                    one(b0, 0)
                    one(b0 + 1, 1)
                dve.wait_ge(row_ready, r0 + B)

            def attention(sub):
                dve.wait_ge(weights_in[sub.order], 16)
                if sub.mask or sub.qk_norm:
                    dve.wait_ge(xt_done, xt_at(SUBS[sub.index - 1], B - 1))
                    key_rows(sub)

                prepare(sub, 0, 0)
                if sub.qk_norm:
                    q_squares(sub, 0, 0)
                    q_norm(sub, 0, 0)

                def step(b, g, p, back, more, tail, far):
                    if sub.ctx:
                        if back[0]:
                            heads(sub, b, g, p, (0, 1))
                        if back[1]:
                            norm(sub, *back[1])
                        if back[0]:
                            heads(sub, b, g, p, (2, 3))
                    else:
                        if back[0]:
                            group_scores(sub, b, g, p)
                        if back[1]:
                            norm(sub, *back[1])
                    if (g, 1) == sub.out_at and tail:
                        output_in(sub, b - 1, 1 - p)
                    if g == 3 and tail and sub.diff:
                        normed_output_in(sub, b - 1, 1 - p)
                    if g == 3 and more and sub.qk_norm:
                        q_squares(sub, b + 1, 1 - p)
                    for k, there, q in ((1, tail, 1 - p), (2, far, p)):
                        if (g, k) == sub.y_at and there:
                            ln_first(sub, b - k, q)
                        if (g, k) == sub.ln_at and there:
                            ln_second(sub, b - k, q)
                    if g == sub.prepare_at and more:
                        prepare(sub, b + 1, 1 - p)
                    if g == 3 and more and sub.qk_norm:
                        q_norm(sub, b + 1, 1 - p)
                pipeline(dve, step)

            def split(high, low, src, high_done, count, done):
                dve.tensor_copy(high, src).then_inc(high_done, 1)
                dve.wait_ge(high_done, count)
                dve.tensor_tensor(low, src, high.bitcast(F32), ALU.subtract).then_inc(done, 1)

            def split_weights(j, k):
                half, pair = k % 2, k // 2 % 2
                cols = slice(half * PIECE, (half + 1) * PIECE)
                dve.wait_ge(land_in[half], 8 * (j - half) + 16)
                split(wsplit[:, 2 * pair, cols], wsplit[:, 2 * pair + 1, cols], landing[:, half, :], w_high, j + 1, w_split)

            def split_rows(n, halves=range(2)):
                for u in halves:
                    for k in range(2):
                        half = slice(u * HALF, (u + 1) * HALF)
                        split(xsplit[:, 0, k, half], xsplit[:, 1, k, half], xT[:, k, half], x_high,
                              4 * n + 2 * u + k + 1, x_split)

            def experts(sub, key):
                dve.wait_ge(ffn_small_in, 16)
                n = sub.index // 3
                if n:
                    dve.wait_ge(dn_ready, START + SUBS[2].base["dn"] + 8 + 8 * EXPERTS)
                for k in range(2):
                    split_weights(32 * n + k, k)
                dve.wait_ge(rt_ready, n + 1)
                step = Steps(dve, rt_step[n], 0, 50)

                def bc(a, k=8):
                    return a.unsqueeze(2).to_broadcast([T, B, k])
                ps = bank[0][0:T, 0:8 * B].rearrange("p (t e) -> p t e", e=8)
                if n:
                    step(dve.tensor_tensor(lg[:, :, :], ps, f("gate_b", T).unsqueeze(1).to_broadcast([T, B, 8]), ALU.add))
                else:
                    step(dve.tensor_copy(lg[:, :, :], ps))
                for t in range(B):
                    step(dve.max(top[:, t, :], lg[:, t, :]))
                for t in range(B):
                    step(dve.max_index(topi[:, t, :], top[:, t, :], lg[:, t, :]))
                step(dve.tensor_copy(ti[:, :, :], topi[:, :, 0:2]))
                step(dve.tensor_tensor(ex[:, :, 0:8], lg[:, :, :], bc(top[:, :, 0]), ALU.subtract))
                step(dve.tensor_tensor(ex[:, :, 8], top[:, :, 1], top[:, :, 0], ALU.subtract))
                assert step.n == 20
                iota = c("iota", T).unsqueeze(1).to_broadcast([T, B, 8])
                step(dve.tensor_tensor(oh0[:, :, :], iota, bc(ti[:, :, 0]), ALU.is_equal))
                step(dve.tensor_tensor(oh1[:, :, :], iota, bc(ti[:, :, 1]), ALU.is_equal))
                dve.wait_ge(rt_exp, n + 1)
                if n == 0:
                    step(dve.tensor_scalar(gw[:, 0, :], ex[:, :, 8], 1.0, None, ALU.add))
                    step(dve.reciprocal(gw[:, 1, :], gw[:, 0, :]))
                    step(dve.tensor_tensor(gw[:, 2, :], gw[:, 1, :], ex[:, :, 8], ALU.mult))
                else:
                    step(dve.reduce_sum(gw[:, 0, :], ex[:, :, 0:8], AX_X))
                    step(dve.reciprocal(gw[:, 1, :], gw[:, 0, :]))
                    step(dve.tensor_tensor(gw[:, 2, :], gw[:, 1, :], ex[:, :, 8], ALU.mult))
                    step(dve.tensor_tensor(gw[:, 3, :], ti[:, :, 1], ti[:, :, 0], ALU.is_gt))
                    step(dve.tensor_scalar(gw[:, 4, :], gw[:, 2, :], 0.0, None, ALU.is_gt))
                    step(dve.tensor_tensor(gw[:, 3, :], gw[:, 3, :], gw[:, 4, :], ALU.mult))
                    step(dve.tensor_scalar(gw[:, 4, :], gw[:, 3, :], -1.0, 1.0, ALU.mult, ALU.add))
                    step(dve.tensor_tensor(gw[:, 2, :], gw[:, 2, :], gw[:, 3, :], ALU.mult))
                    step(dve.tensor_tensor(gw[:, 1, :], gw[:, 1, :], gw[:, 4, :], ALU.mult))
                    step(dve.tensor_tensor(gw[:, 5, :], gw[:, 1, :], gw[:, 2, :], ALU.add))
                first, second = (gw[:, 1, :], gw[:, 2, :]) if n == 0 else (gw[:, 4, :], gw[:, 3, :])
                step(dve.tensor_tensor(oh0[:, :, :], oh0[:, :, :], bc(first), ALU.mult))
                step(dve.tensor_tensor(oh1[:, :, :], oh1[:, :, :], bc(second), ALU.mult))
                dve.tensor_tensor(wts[:, :, :], oh0[:, :, :], oh1[:, :, :], ALU.add).then_inc(wt_ready, 1)
                dve.wait_ge(wt_ready, n + 1)
                db = START + sub.base["dn"]
                for t in range(B):
                    dve.wait_ge(dn_ready, db + t + 1)
                    dve.tensor_copy(acc[:, t, :], bank[4 + t % 4][0:T, 0:DM]).then_inc(dn_done, 1)
                if n:
                    wait_xres(dve, sub, B - 1)
                    for t in range(B):
                        if t >= 2:
                            dve.wait_ge(xs_T, t - 1)
                        dve.tensor_scalar(xs[:, t % 2, :], x_res[:, t, :], gw[:, 5, t:t + 1], None, ALU.mult).then_inc(xs_ready, 1)
                    dve.wait_ge(xs_done, B)
                split_rows(n)
                ub = START + sub.base["up"]

                def one(e0, p, last):
                    e = e0 + p
                    for c in range(16):
                        u, m = c // 8, c % 8
                        if m == 0:
                            dve.wait_ge(dn_ready, db + 8 * e + 4 * u + 4)
                        dve.wait_ge(up_done, ub + 16 * e + c + 1)
                        split(hid[:, 0, u, m, :], hid[:, 1, u, m, :], tmp[:, c % 4, :], h_high,
                              sub.base["up"] + 16 * e + c + 1, h_split)
                        if c in (0, 2):
                            if c == 0:
                                dve.wait_ge(dn_ready, db + 8 * e + 8)
                            split_weights(32 * n + 4 * e + 2 + c // 2, 2 + c // 2)
                    if not last:
                        dve.wait_ge(up_ready, ub + 16 * e + 16)
                        for k in range(2):
                            split_weights(32 * n + 4 * e + 4 + k, k)
                    dve.tensor_copy(wcol[:, p, :], wts[:, :, bass.ds(e, 1)].rearrange("p t o -> p (t o)")).then_inc(col_ready, 1)
                    dve.wait_ge(col_ready, 8 * n + e + 1)
                    for t in range(B):
                        dve.wait_ge(dn_ready, db + 8 + 8 * e + t + 1)
                        dve.wait_ge(dn_done, db + 8 * e + t + 1)
                        dve.scalar_tensor_tensor(out=acc[:, t, :], in0=bank[4 + t % 4][0:T, 0:DM], scalar=wcol[:, p, t:t + 1],
                                                 in1=acc[:, t, :], op0=ALU.mult, op1=ALU.add).then_inc(dn_done, 1)
                        if last:
                            dve.wait_ge(dn_done, db + 8 * EXPERTS + t + 1)
                            dve.tensor_tensor(res[:, t % 2, :], acc[:, t, :], x_res[:, t, :], ALU.add).then_inc(ln_dve, 1)
                            stats(sub, t, t % 2, 0)
                            if t:
                                rows_out(sub, t - 1, (t - 1) % 2)
                with dve.Fori(0, EXPERTS // 2 - 1) as pair:
                    e0 = pair * 2
                    one(e0, 0, False)
                    one(e0, 1, False)
                one(EXPERTS - 2, 0, False)
                one(EXPERTS - 2, 1, True)
                rows_out(sub, B - 1, 1)

            def quantised(sub):
                step = Steps(dve, rq_step, 0, 9)
                rT_ = f("rhsT").rearrange("p (m d) -> p m d", m=2)
                step(dve.tensor_reduce(qs[:, :, 0], rT_, AX_X, ALU.max))
                step(dve.tensor_reduce(qs[:, :, 1], rT_, AX_X, ALU.min))
                step(dve.tensor_scalar(qs[:, :, 2], qs[:, :, 1], -1.0, None, ALU.mult))
                step(dve.tensor_tensor(qs[:, :, 3], qs[:, :, 0], qs[:, :, 2], ALU.max))
                step(dve.tensor_scalar(qs[:, :, 4], qs[:, :, 3], 1e-12, 1.0 / 127.0, ALU.max, ALU.mult))
                step(dve.reciprocal(qs[:, :, 5], qs[:, :, 4]))
                for m in range(2):
                    dve.tensor_scalar(diag[:, m, :], c("ident"), qs[:, m, 4:5], None, ALU.mult)
                    ins = dve.tensor_scalar(rqf[:, m, :], rT_[:, m, :], qs[:, m, 5:6], MAGIC, ALU.mult, ALU.add)
                step(ins)
                step(dve.tensor_scalar(rqf[:, :, :], rqf[:, :, :], -MAGIC, None, ALU.add))
                step(dve.tensor_scalar(rqf[:, :, :], rqf[:, :, :], 127.0, -127.0, ALU.min, ALU.max))
                dve.wait_ge(rq_done, 2)

                with dve.Fori(0, B // 2) as pair:
                    b0 = pair * 2
                    row = [x_res[:, bass.ds(b0 + p, 1), :].rearrange("p o n -> p (o n)") for p in range(2)]

                    def quantise(k, p):
                        xr, q = row[p], qs[0:T, p, :]
                        if k in (0, 1):
                            return dve.tensor_reduce(q[:, k:k + 1], xr, AX_X, (ALU.max, ALU.min)[k])
                        if k == 2:
                            return dve.tensor_scalar(q[:, 2:3], q[:, 1:2], -1.0, None, ALU.mult)
                        if k == 3:
                            return dve.tensor_tensor(q[:, 3:4], q[:, 0:1], q[:, 2:3], ALU.max)
                        if k == 4:
                            return dve.tensor_scalar(q[:, 4:5], q[:, 3:4], 1e-12, 1.0 / 127.0, ALU.max, ALU.mult)
                        if k == 5:
                            return dve.reciprocal(q[:, 5:6], q[:, 4:5])
                        if k == 6:
                            return dve.tensor_scalar(qf[:, p, :], xr, q[:, 5:6], MAGIC, ALU.mult, ALU.add)
                        if k == 7:
                            return dve.tensor_scalar(qf[:, p, :], qf[:, p, :], -MAGIC, None, ALU.add)
                        return dve.tensor_scalar(qf[:, p, :], qf[:, p, :], 127.0, -127.0, ALU.min, ALU.max)

                    wait_xres(dve, sub, b0 + 1)
                    dve.wait_ge(q_T, START + b0)
                    apart(dve)
                    for k in range(9):
                        for p in range(2):
                            if k:
                                dve.wait_ge(q_step, START + 9 * b0 + 2 * k - 1 + p)
                            if k == 1:
                                apart(dve)
                            quantise(k, p).then_inc(q_step, 1)
                    for p in range(2):
                        b = b0 + p
                        dve.wait_ge(dn_ready, START + sub.base["dn"] + b + 1)
                        dve.scalar_tensor_tensor(out=junk[:, :], in0=bank[4 + p][0:T, 0:DM], scalar=qs[0:T, p, 4:5],
                                                 in1=rsb[:, :], op0=ALU.mult, op1=ALU.mult).then_inc(dn_done, 1)
                        dve.wait_ge(dn_done, START + sub.base["dn"] + b + 1)
                        dve.tensor_tensor(res[:, p, :], junk[:, :], row[p], ALU.add).then_inc(ln_dve, 1)
                        stats(sub, b, p, 0)
                    for p in range(2):
                        rows_out(sub, b0 + p, p)

            def glu(sub):
                ub, db = START + sub.base["up"], START + sub.base["dn"]

                def item(k):
                    for half in range(2):
                        split_weights(64 + 2 * k + half, 2 * k + half)

                dve.wait_ge(y_ready, at(SUBS[10], "batch", B - 1, 1))
                wait_rows(dve, sub, B // 2 - 1)
                split_rows(2, (0,))
                item(0)
                item(1)
                wait_rows(dve, sub, B - 1)
                split_rows(2, (1,))
                for u in range(2):
                    first = GLU_ITEMS * u
                    for m in range(24):
                        c = 24 * u + m
                        if m == 0 and u:
                            dve.wait_ge(dn_ready, db + 4)
                        if m == 7:
                            dve.wait_ge(up_ready, ub + 32 * u + 16)
                            item(first + 2)
                        dve.wait_ge(up_done, ub + c + 1)
                        if m < 8:
                            dve.wait_ge(up_ready, ub + 32 * u + 2 * m + 2)
                            dve.scalar_tensor_tensor(out=tmp[:, c % 4, :], in0=bank[2 * (m % 2) + 1][:, 0:HALF],
                                                     scalar=f("s2")[:, m:m + 1], in1=tmp[:, c % 4, :],
                                                     op0=ALU.mult, op1=ALU.mult).then_inc(glu_done, 1)
                            dve.wait_ge(glu_done, 8 * u + m + 1)
                        to = m // 8 % 2
                        split(hid[:, 0, to, m % 8, :], hid[:, 1, to, m % 8, :], tmp[:, c % 4, :], h_high,
                              sub.base["up"] + c + 1, h_split)
                        if m == 7:
                            item(first + 3)
                        elif m > 8 and m % 2 == 1 and first + 4 + (m - 9) // 2 < 2 * GLU_ITEMS:
                            item(first + 4 + (m - 9) // 2)
                    for b in range(4 * u, 4 * u + 4):
                        p = b % 2
                        wait_xres(dve, sub, b)
                        dve.wait_ge(dn_ready, db + b + 1)
                        if b == 3:
                            item(GLU_ITEMS + 1)
                        dve.tensor_tensor(junk[:, :], bank[4 + b % 4][0:T, 0:DM], f("s3row", T), ALU.mult).then_inc(dn_done, 1)
                        dve.wait_ge(dn_done, db + b + 1)
                        dve.tensor_tensor(res[:, p, :], junk[:, :], x_res[:, b, :], ALU.add).then_inc(ln_dve, 1)
                        stats(sub, b, p, 0)
                        for done in [b - 1] * (b > 4 * u) + [b] * (b == 4 * u + 3):
                            dve.wait_ge(xres_done, at(sub, "row", done, -1))
                            normed(sub, done, done % 2, 0, xln[:, done % 2, :]).then_inc(xln_ready, 1)

            dve.wait_ge(weights_in[0], 16)
            a0 = w(ATTNS[0], "lam", T)
            for i in range(2):
                dve.tensor_tensor_reduce(junk[:, 32 * i:32 * i + 32], a0[:, 64 * i:64 * i + 32], a0[:, 64 * i + 32:64 * i + 64],
                                         1.0, 0.0, ALU.mult, ALU.add, lamt[:, 32 + i:33 + i]).then_inc(lam_step, 1)
            dve.tensor_scalar(gam[:, :], w(ATTNS[0], "gamma", T), 1.0 - LAMBDA_INIT, None, ALU.mult).then_inc(lam_step, 1)
            dve.wait_ge(lam_exp, 1)
            dve.tensor_tensor(lamt[:, 37:38], lamt[:, 35:36], lamt[:, 34:35], ALU.subtract).then_inc(lam_step, 1)
            dve.wait_ge(lam_step, 4)
            dve.tensor_scalar(lamt[:, 38:39], lamt[:, 37:38], -LAMBDA_INIT, None, ALU.add).then_inc(lam_step, 1)
            dve.wait_ge(lam_step, 5)
            for sub in SUBS:
                if isinstance(sub, Attn):
                    attention(sub)
                elif sub.index in (2, 5):
                    experts(sub, None)
                elif sub.index == 8:
                    quantised(sub)
                else:
                    glu(sub)

        @block.gpsimd
        def _(pool):
            for s in (xtb_ready, qblk_ready, xb_ready, ln_pool, xres_done):
                pool.sem_inc(s, START)
            nc.gpsimd.memset(vbuf, 0.0).then_inc(v_zero, 1)
            pool.wait_ge(consts_in, 16)

            def start_batch(sub, b, p):
                wait_rows(pool, sub, b)
                pool.wait_ge(proj_ready, at(sub, "proj", b - 1, 0))
                apart(pool)
                nc.gpsimd.tensor_copy(xTb[:, p, :, :], xT[:, :, bass.ds(b * T, T)]).then_inc(xtb_ready, 1)

            def squares(sub, b, p):
                for s, src in enumerate((qT, kT)):
                    pool.wait_ge(proj_done, at(sub, "proj", b, s + 1))
                    nc.gpsimd.tensor_tensor(rT[:, p, s, :, :], src[:, p, 0:2, :], src[:, p, 0:2, :], ALU.mult)\
                        .then_inc(sq_ready, 1)

            def spread(sub, b, p):
                if sub.feats:
                    pool.wait_ge(feat_ready, 4 * b + 2)
                    src = fq[:, p, :, :]
                elif sub.rope:
                    pool.wait_ge(rot_step, 6 * b + 3)
                    src = qT[:, p, 0:2, :]
                else:
                    pool.wait_ge(proj_done, at(sub, "proj", b, 1))
                    src = qT[:, p, 0:sub.chunks, :]
                pool.wait_ge(head_ready, START + HEADS * (B * sub.order + b - 1))
                n, k = sub.chunks, sub.hpc
                for m in range(n):
                    ins = nc.gpsimd.tensor_tensor(qblk[:, p, k * m:k * m + k, :],
                                                  src[:, m, :].unsqueeze(1).to_broadcast([128, k, T]),
                                                  w(sub, "headmask").unsqueeze(2).to_broadcast([128, k, T]), ALU.mult)
                ins.then_inc(qblk_ready, 1)

            def q_root(sub, b, p):
                pool.wait_ge(proj_done, at(sub, "proj", b, 2))
                nc.gpsimd.tensor_tensor(qrow[:, p, 1, :], qrow[:, p, 0, :], w(sub, "bqrow", T), ALU.add).then_inc(qrow_ready, 1)
                pool.wait_ge(qn_step, START + 4 * b + 1)
                nc.gpsimd.tensor_tensor(qn[:, p, 1:2], qn[:, p, 0:1], c("plus_half", T)[:, 0:1], ALU.pow).then_inc(qn_root, 1)

            def residual(sub, b, p):
                pool.wait_ge(ln_dve, START + 3 * ln_unit(sub, b - 2) + 1)
                if sub.qk_norm:
                    pool.wait_ge(qrow_ready, b + 1)
                    nc.gpsimd.tensor_tensor(xb[:, p, :], qrow[:, p, 1, :], w(sub, "bo", T), ALU.add).then_inc(xb_ready, 1)
                else:
                    wait_xres(pool, sub, b)
                    nc.gpsimd.tensor_tensor(xb[:, p, :], x_res[:, bass.ds(b, 1), :].rearrange("p o n -> p (o n)"),
                                            w(sub, "bo", T), ALU.add).then_inc(xb_ready, 1)

            def ln_root(sub, b, p, unit):
                u = sub.base["ln"] + int(sub.per["ln"]) * b + unit
                pool.wait_ge(ln_dve, START + 3 * u + 3)
                nc.gpsimd.tensor_tensor(mv[:, p, 2:3], mv[:, p, 1:2], c("eps", T), ALU.add).then_inc(ln_pool, 1)
                pool.wait_ge(ln_pool, START + 2 * u + 1)
                nc.gpsimd.tensor_tensor(mv[:, p, 3:4], mv[:, p, 2:3], c("minus_half", T)[:, 0:1], ALU.pow).then_inc(ln_pool, 1)

            def o_root(sub, b, p):
                pool.wait_ge(o_step, 7 * b + 3)
                apart(pool)
                nc.gpsimd.tensor_scalar(rms[:, p, 1, :], rms[:, p, 0, :], 1.0 / 64, None, ALU.mult).then_inc(o_pool, 1)
                pool.wait_ge(o_pool, 2 * b + 1)
                nc.gpsimd.tensor_tensor(rms[:, p, 2, :], rms[:, p, 1, :], c("plus_half", T), ALU.pow).then_inc(o_pool, 1)

            def keep_rows(sub, b, p):
                pool.wait_ge(xln_ready, at(sub, "row", b, 1))
                apart(pool)
                nc.gpsimd.tensor_copy(x_res[:, bass.ds(b, 1), :].rearrange("p o n -> p (o n)"), xln[:, p, :])\
                    .then_inc(xres_done, 1)

            def attention(sub):
                pool.wait_ge(weights_in[sub.order], 16)
                if sub.order:
                    pool.wait_ge(proj_ready, at(ATTNS[sub.order - 1], "proj", B, 0))
                if sub.index and isinstance(SUBS[sub.index - 1], Ffn):
                    wait_rows(pool, sub, B - 1)

                start_batch(sub, 0, 0)
                if sub.feats:
                    squares(sub, 0, 0)
                spread(sub, 0, 0)
                if sub.qk_norm:
                    q_root(sub, 0, 0)
                    residual(sub, 0, 0)

                def step(b, g, p, back, more, tail, far):
                    if g == 0 and more:
                        start_batch(sub, b + 1, 1 - p)
                    if g == 1 and back[0] and not sub.qk_norm:
                        residual(sub, b, p)
                    if g == 3 and more and sub.qk_norm:
                        q_root(sub, b + 1, 1 - p)
                    if g == 2 and tail and sub.diff:
                        o_root(sub, b - 1, 1 - p)
                    if g == 1 and more and sub.feats:
                        squares(sub, b + 1, 1 - p)
                    if g == sub.spread_at and more:
                        spread(sub, b + 1, 1 - p)
                    for k, there, q in ((1, tail, 1 - p), (2, far, p)):
                        if (g, k) == sub.y_at and there:
                            ln_root(sub, b - k, q, 0)
                        if (g, k) == sub.ln_at and there:
                            if sub.qk_norm:
                                ln_root(sub, b - k, q, 1)
                            keep_rows(sub, b - k, q)
                    if g == 3 and more and sub.qk_norm:
                        residual(sub, b + 1, 1 - p)
                pipeline(pool, step)

            def feed_forward(sub):
                if sub.index in (2, 5):
                    pool.wait_ge(w_split, START + 32 * (sub.index // 3 + 1))
                    nc.gpsimd.memset(vbuf, 0.0).then_inc(v_zero, 1)
                ln_root(sub, 0, 0, 0)
                for b in range(B):
                    ahead = b % 4 != 3 if sub.index == 11 else b % 2 == 0 if sub.index == 8 else True
                    if ahead and b + 1 < B:
                        ln_root(sub, b + 1, (b + 1) % 2, 0)
                    keep_rows(sub, b, b % 2)
                    if not ahead and b + 1 < B:
                        ln_root(sub, b + 1, (b + 1) % 2, 0)

            for sub in SUBS:
                if isinstance(sub, Attn):
                    attention(sub)
                else:
                    feed_forward(sub)


def _columns_of(vector, rows=128):
    return np.ascontiguousarray(vector.reshape(-1, rows).T)


def _chunks(weight, rows=128):
    k, n = weight.shape[0] // rows, weight.shape[1]
    out = np.zeros((128, k * n), np.float32)
    out[:rows] = weight.reshape(k, rows, n).transpose(1, 0, 2).reshape(rows, k * n)
    return out


def _strips(weight):
    n = weight.shape[1]
    out = np.zeros((4, 32, 4, n), np.float32)
    out[:, 0:16] = weight.reshape(4, 4, 16, n).transpose(1, 2, 0, 3)
    return out.reshape(128, 4 * n)


def _pack(sub, parts):
    out = np.zeros((128, sub.cols), np.float32)
    r = np.arange(128)
    own = r[:, None] // (128 // sub.hpc) == np.arange(sub.hpc)[None, :]
    parts["headmask"] = np.where(own, sub.scale if sub.kind == "softmax" and not sub.qk_norm else 1.0, 0.0)
    for key, a in parts.items():
        at, n = sub.at[key]
        if a.ndim == 1:
            a = np.broadcast_to(a, (128, a.shape[0]))
        out[:a.shape[0], at:at + a.shape[1]] = a
    return out


def _rope_tables():
    i = np.arange(T)
    inv = (1.0 / 10000.0 ** (np.arange(2, dtype=np.float32) / np.float32(2.0))).astype(np.float32)
    cos, sin = np.ones((16, T), np.float32), np.zeros((16, T), np.float32)
    frame = i // 256
    rest = i - 256 * frame
    for s, pos in enumerate((frame, rest // 16, rest - 16 * (rest // 16))):
        for d in range(4):
            freq = (pos.astype(np.float32) * inv[d % 2]).astype(np.float32)
            cos[4 * s + d], sin[4 * s + d] = np.cos(freq), np.sin(freq)
    rot = np.zeros((128, 128), np.float32)
    for k in range(0, 128, 2):
        rot[k + 1, k], rot[k, k + 1] = -1.0, 1.0
    return np.tile(cos, (8, 1)), np.tile(sin, (8, 1)), rot


def kernel(**inputs):
    import concourse.bacc as bacc
    from concourse.bass_utils import run_bass_kernel_spmd

    a = {k: np.asarray(v) for k, v in inputs.items()}

    consts = np.zeros((128, CONST_COLS), np.float32)
    for key, value in (("ident", np.eye(128)), ("iota", np.broadcast_to(np.arange(8), (128, 8))),
                       ("causal", np.tril(np.ones((128, 128)))[:, 0:T]), ("ones", np.ones((128, T))),
                       ("eps", np.full((128, 1), LN_EPS)),
                       ("minus_half", np.full((128, 8), -0.5)), ("plus_half", np.full((128, 8), 0.5))):
        at, n = CONST_AT[key]
        consts[:, at:at + n] = value

    ffn_small = np.zeros((128, FFN_COLS), np.float32)

    def put(key, value):
        at, n = FFN_AT[key]
        ffn_small[:value.shape[0], at:at + n] = value

    put("L0_router", _chunks(a["L0_ffn_w_router"].T))
    put("L0_bup", _columns_of(a["L0_ffn_b_up"].reshape(-1)))
    put("L0_bdown", a["L0_ffn_b_down"])
    put("L1_router", _chunks(a["L1_ffn_gate_w"]))
    put("gate_b", np.broadcast_to(a["L1_ffn_gate_b"], (128, 8)))
    put("L1_b1", _columns_of(a["L1_ffn_b1"].reshape(-1)))
    put("L1_b2", a["L1_ffn_b2"])
    put("rhsT", _chunks(a["L2_ffn_rhs"].T))
    for key, name in (("s1", "w1_s"), ("s2", "w2_s"), ("sh1", "h1_s"), ("sh2", "h2_s")):
        put(key, _columns_of(a["L3_ffn_" + name]))
    put("s3row", np.broadcast_to(a["L3_ffn_w3_s"], (128, DM)))

    def qkv(sub, wq, wk, wv):
        rows = KC if sub.ctx else 128
        return {"wq": _chunks(wq), "wk": _chunks(wk, rows), "wv": _chunks(wv, rows)}

    def biases(name):
        return {"bq": _columns_of(a[name + "_bq"]), "bk": _columns_of(a[name + "_bk"]),
                "bvT": _strips(a[name + "_bv"].reshape(-1, 1))}

    cos, sin, rot = _rope_tables()
    rf, ones2 = np.zeros((4, 128, 128), np.float32), np.zeros((4, 128, 128), np.float32)
    for u in range(4):
        for i in range(2):
            h = 2 * u + i
            rf[u, 16 * h:16 * h + 16, 64 * i:64 * i + 64] = a["L3_attn_random_features"].T
            ones2[u, 16 * h:16 * h + 16, 64 * i:64 * i + 64] = 1.0
    side_by_side = lambda t: t.transpose(1, 0, 2).reshape(128, -1)
    s = {x.name: x for x in ATTNS}
    w_kv, w_qkv = a["L0_attn_Wkv"], a["L3_attn_w_qkv"].T
    parts = {
        "L0_attn": {**qkv(s["L0_attn"], a["L0_attn_Wq"], w_kv[:, :512], w_kv[:, 512:]), "wo": _chunks(a["L0_attn_Wout"]),
                    "lam": np.concatenate([a["L0_attn_lambda_" + k] for k in ("q1", "k1", "q2", "k2")]),
                    "gamma": a["L0_attn_gamma"]},
        "L0_xattn": {**qkv(s["L0_xattn"], a["L0_xattn_Wq"], a["L0_xattn_Wk"], a["L0_xattn_Wv"]), **biases("L0_xattn"),
                     "wo": _strips(a["L0_xattn_Wo"]), "bo": a["L0_xattn_bo"]},
        "L1_attn": {**qkv(s["L1_attn"], a["L1_attn_Wq"], a["L1_attn_Wk"], a["L1_attn_Wv"]), **biases("L1_attn"),
                    "wo": _strips(a["L1_attn_Wo"]), "bo": a["L1_attn_bo"], "cos": cos, "sin": sin, "rot": rot},
        "L1_xattn": {**qkv(s["L1_xattn"], a["L1_xattn_Wq"], a["L1_xattn_Wk"], a["L1_xattn_Wv"]),
                     "wo": _strips(a["L1_xattn_Wo"])},
        "L2_attn": {**qkv(s["L2_attn"], a["L2_attn_Wq"].T, a["L2_attn_Wk"].T, a["L2_attn_Wv"].T), **biases("L2_attn"),
                    "wo": _strips(a["L2_attn_Wo"].T), "bo": a["L2_attn_bo"]},
        "L2_xattn": {**qkv(s["L2_xattn"], a["L2_xattn_Wq"], a["L2_xattn_Wk"], a["L2_xattn_Wv"]), **biases("L2_xattn"),
                     "wo": _strips(a["L2_xattn_Wo"]), "bo": a["L2_xattn_bo"], "bqrow": a["L2_xattn_bq"],
                     "ln_g": a["L2_xattn_ln_gamma"], "ln_b": a["L2_xattn_ln_beta"]},
        "L3_attn": {**qkv(s["L3_attn"], w_qkv[:, :256], w_qkv[:, 256:512], w_qkv[:, 512:]),
                    "wo": _strips(a["L3_attn_w_out"].T), "bo": a["L3_attn_b_out"],
                    "rf": side_by_side(rf), "ones2": side_by_side(ones2)},
        "L3_xattn": {**qkv(s["L3_xattn"], a["L3_xattn_Wq"], a["L3_xattn_Wk"], a["L3_xattn_Wv"]), **biases("L3_xattn"),
                     "b1": _columns_of(a["L3_xattn_b1"]), "bo": a["L3_xattn_b2"]},
    }
    packs = [_pack(x, parts[x.name]) for x in ATTNS]

    ring = np.zeros((RING_ALL, 128, RCOLS), np.float32)
    for e in range(EXPERTS):
        ring[RING_L0 + 2 * e] = _chunks(a["L0_ffn_w_up"][e].T)
        ring[RING_L0 + 2 * e + 1] = _chunks(a["L0_ffn_w_down"][e].T)
        ring[RING_L1 + 2 * e] = _chunks(a["L1_ffn_w1"][e])
        ring[RING_L1 + 2 * e + 1] = _chunks(a["L1_ffn_w2"][e])
    ring[RING_X] = _strips(a["L3_xattn_W1"])
    ring[RING_X + 1, :, 0:4 * DM] = _chunks(a["L3_xattn_W2"])
    ring[RING_GLU], ring[RING_GLU + 1] = _chunks(a["L3_ffn_w1_w"].T), _chunks(a["L3_ffn_w2_w"].T)
    for j in range(4):
        ring[RING_H1 + j] = _chunks(a["L3_ffn_h1_w"].T[:, 256 * j:256 * j + 256])
        ring[RING_H2 + j] = _chunks(a["L3_ffn_h2_w"].T[:, 256 * j:256 * j + 256])
    ring[RING_W3] = _chunks(a["L3_ffn_w3_w"].T)

    arrays = {"ctxT": np.ascontiguousarray(a["ctx_768"].reshape(B, S2, 2, KC).transpose(0, 3, 2, 1)),
              "mask": a["mask_BxS2_bf1"], "x": a["x"], "consts": consts, "ffn_small": ffn_small, "ring": ring}
    arrays.update({f"pack{i}": p for i, p in enumerate(packs)})

    nc = bacc.Bacc("TRN2", target_bir_lowering=False, num_devices=1)
    dram = {k: nc.dram_tensor("in_" + k, v.shape, mybir.dt.from_np(v.dtype), kind="ExternalInput").ap()
            for k, v in arrays.items()}
    out = nc.dram_tensor("out", (B, T, DM), F32, kind="ExternalOutput").ap()
    decoder(nc, dram["ctxT"], dram["mask"], dram["x"], dram["consts"], dram["ffn_small"],
            [dram[f"pack{i}"] for i in range(len(packs))], dram["ring"], out)
    r = run_bass_kernel_spmd(nc, [{"in_" + k: v for k, v in arrays.items()}], core_ids=[0])
    return r.results[0]["out"]
```
